# Optimizing a Trainium2 kernel written in Bass

```python
import numpy as np
import jax
import jax.numpy as jnp

def _softmax(x, axis=-1):
    return jax.nn.softmax(x, axis=axis)
def _gelu(x):
    return jax.nn.gelu(x, approximate=True)
def _silu(x):
    return jax.nn.silu(x)
def _sigmoid(x):
    return jax.nn.sigmoid(x)
def _layernorm(x, axis=-1, eps=1e-5):
    m = jnp.mean(x, axis=axis, keepdims=True)
    v = jnp.var(x, axis=axis, keepdims=True)
    return (x - m) / jnp.sqrt(v + eps)
def _scatter_add(tgt, idx, src, axis=0):
    return tgt.at[idx].add(src)
def _segment_sum(src, seg, n):
    return jax.ops.segment_sum(src, seg, n)

kernel_name = 'mk_conv_preact_d2_conv_nhwc128_762caa'

def setup_inputs(seed: int = 0):
    np.random.seed(seed)
    _w = jnp.asarray
    def _rec_inputs():
        import jax
        import jax.numpy as jnp
        _gk = jax.random.key(seed)
        x = 7.22e-05 + 1 * jax.random.normal(jax.random.fold_in(_gk, 1), (1, 256, 256, 128), jnp.float32)
        return x
    x = _rec_inputs()
    def _L0_conv_setup():
        import jax, jax.numpy as jnp
        import numpy as np
        C_Z, C, N_HEAD, N = (128, 32, 4, 256)
        EPS = 1e-05
        NEG = -1000000000.0

        def _layer_norm(x, gamma, beta):
            mu = jnp.mean(x, axis=-1, keepdims=True)
            var = jnp.var(x, axis=-1, keepdims=True)
            return (x - mu) * jax.lax.rsqrt(var + EPS) * gamma + beta
        key = jax.random.key(seed)
        ks = jax.random.split(key, 9)
        s = lambda d: 1.0 / np.sqrt(d)
        return {'z': jax.random.normal(ks[0], (1, N, N, C_Z), jnp.float32), 'single_mask': jax.random.bernoulli(ks[1], 0.9, (1, N)), 'ln_gamma': jnp.ones((C_Z,), jnp.float32), 'ln_beta': jnp.zeros((C_Z,), jnp.float32), 'Wq': jax.random.normal(ks[2], (C_Z, N_HEAD * C), jnp.float32) * s(C_Z), 'Wk': jax.random.normal(ks[3], (C_Z, N_HEAD * C), jnp.float32) * s(C_Z), 'Wv': jax.random.normal(ks[4], (C_Z, N_HEAD * C), jnp.float32) * s(C_Z), 'Wb': jax.random.normal(ks[5], (C_Z, N_HEAD), jnp.float32) * s(C_Z), 'Wg': jax.random.normal(ks[6], (C_Z, N_HEAD * C), jnp.float32) * s(C_Z), 'Wout': jax.random.normal(ks[7], (N_HEAD * C, C_Z), jnp.float32) * s(N_HEAD * C)}
    _L0_conv_all = _L0_conv_setup()
    _L0_conv_in = {k: v for k, v in _L0_conv_all.items() if k in ('single_mask', 'ln_gamma', 'ln_beta', 'Wq', 'Wk', 'Wv', 'Wb', 'Wg', 'Wout', )}
    del _L0_conv_all

    def _L1_conv_setup():
        import jax, jax.numpy as jnp
        import numpy as np
        EPS = 1e-06

        def kernel_to_freq_2d(kernel, H, W):
            C, kh, kw = kernel.shape
            th = (jnp.arange(kh) - kh // 2) % H
            tw = (jnp.arange(kw) - kw // 2) % W
            TH, TW = jnp.meshgrid(th, tw, indexing='ij')
            padded = jnp.zeros((C, H, W), dtype=kernel.dtype).at[:, TH, TW].set(kernel)
            return jnp.fft.fft2(padded, axes=(1, 2))

        def heinsen_scan_log(log_coeffs, log_values):

            def op(left, right):
                la, lb = left
                ra, rb = right
                return (la + ra, jnp.logaddexp(ra + lb, rb))
            _, log_h = jax.lax.associative_scan(op, (log_coeffs, log_values), axis=0)
            return log_h
        key = jax.random.key(seed)
        ks = jax.random.split(key, 7)
        B, H, W, C, k = (4, 128, 128, 128, 7)
        fan_in = k * k
        x = jax.random.normal(ks[0], (B, H, W, C), dtype=jnp.float32)
        A_kernel = jax.random.normal(ks[1], (C, k, k), dtype=jnp.float32) / np.sqrt(fan_in)
        B_kernel = jax.random.normal(ks[2], (C, k, k), dtype=jnp.float32) / np.sqrt(fan_in)
        gate_A_kernel = jax.random.normal(ks[3], (C, k, k), dtype=jnp.float32) * 0.02
        gate_B_kernel = jax.random.normal(ks[4], (C, k, k), dtype=jnp.float32) * 0.02
        W_out = jax.random.normal(ks[5], (C, C), dtype=jnp.float32) / np.sqrt(C)
        b_out = jnp.zeros((C,), dtype=jnp.float32)
        return dict(x=x, A_kernel=A_kernel, B_kernel=B_kernel, gate_A_kernel=gate_A_kernel, gate_B_kernel=gate_B_kernel, W_out=W_out, b_out=b_out, T=8)
    _L1_conv_all = _L1_conv_setup()
    _L1_conv_in = {k: v for k, v in _L1_conv_all.items() if k in ('A_kernel', 'B_kernel', 'gate_A_kernel', 'gate_B_kernel', 'W_out', 'b_out', )}
    del _L1_conv_all

    return {
        "x": x,
        "L0_conv_single_mask": _L0_conv_in["single_mask"],
        "L0_conv_ln_gamma": _L0_conv_in["ln_gamma"],
        "L0_conv_ln_beta": _L0_conv_in["ln_beta"],
        "L0_conv_Wq": _L0_conv_in["Wq"],
        "L0_conv_Wk": _L0_conv_in["Wk"],
        "L0_conv_Wv": _L0_conv_in["Wv"],
        "L0_conv_Wb": _L0_conv_in["Wb"],
        "L0_conv_Wg": _L0_conv_in["Wg"],
        "L0_conv_Wout": _L0_conv_in["Wout"],
        "L1_conv_A_kernel": _L1_conv_in["A_kernel"],
        "L1_conv_B_kernel": _L1_conv_in["B_kernel"],
        "L1_conv_gate_A_kernel": _L1_conv_in["gate_A_kernel"],
        "L1_conv_gate_B_kernel": _L1_conv_in["gate_B_kernel"],
        "L1_conv_W_out": _L1_conv_in["W_out"],
        "L1_conv_b_out": _L1_conv_in["b_out"],
    }

def reference(x, L0_conv_single_mask, L0_conv_ln_gamma, L0_conv_ln_beta, L0_conv_Wq, L0_conv_Wk, L0_conv_Wv, L0_conv_Wb, L0_conv_Wg, L0_conv_Wout, L1_conv_A_kernel, L1_conv_B_kernel, L1_conv_gate_A_kernel, L1_conv_gate_B_kernel, L1_conv_W_out, L1_conv_b_out):
    import jax
    import jax.numpy as jnp
    def _L0_conv_ref(z, single_mask, ln_gamma, ln_beta, Wq, Wk, Wv, Wb, Wg, Wout):
        import jax, jax.numpy as jnp
        import numpy as np
        C_Z, C, N_HEAD, N = (128, 32, 4, 256)
        EPS = 1e-05
        NEG = -1000000000.0

        def _layer_norm(x, gamma, beta):
            mu = jnp.mean(x, axis=-1, keepdims=True)
            var = jnp.var(x, axis=-1, keepdims=True)
            return (x - mu) * jax.lax.rsqrt(var + EPS) * gamma + beta
        B = z.shape[0]
        zn = _layer_norm(z, ln_gamma, ln_beta)
        proj = lambda W: (zn @ W).reshape(B, N, N, N_HEAD, C)
        q, k, v, g = (proj(Wq), proj(Wk), proj(Wv), proj(Wg))
        bias = zn @ Wb
        bias = jnp.transpose(bias, (0, 3, 1, 2))
        bias = bias + NEG * (~single_mask)[:, None, None, :].astype(bias.dtype)
        scores = jnp.einsum('bijhc,bikhc->bihjk', q, k) / np.sqrt(C)
        scores = scores + bias[:, None]
        attn = jax.nn.softmax(scores, axis=-1)
        o = jnp.einsum('bihjk,bikhc->bijhc', attn, v)
        o = jax.nn.sigmoid(g) * o
        o = o.reshape(B, N, N, N_HEAD * C)
        return o @ Wout

    def _L1_conv_ref(x, A_kernel, B_kernel, gate_A_kernel, gate_B_kernel, W_out, b_out, T):
        import jax, jax.numpy as jnp
        import numpy as np
        EPS = 1e-06

        def kernel_to_freq_2d(kernel, H, W):
            C, kh, kw = kernel.shape
            th = (jnp.arange(kh) - kh // 2) % H
            tw = (jnp.arange(kw) - kw // 2) % W
            TH, TW = jnp.meshgrid(th, tw, indexing='ij')
            padded = jnp.zeros((C, H, W), dtype=kernel.dtype).at[:, TH, TW].set(kernel)
            return jnp.fft.fft2(padded, axes=(1, 2))

        def heinsen_scan_log(log_coeffs, log_values):

            def op(left, right):
                la, lb = left
                ra, rb = right
                return (la + ra, jnp.logaddexp(ra + lb, rb))
            _, log_h = jax.lax.associative_scan(op, (log_coeffs, log_values), axis=0)
            return log_h
        B, H, W, C = x.shape

        def ifft_real(z_bhwc):
            return jnp.fft.ifft2(z_bhwc.transpose(0, 3, 1, 2), axes=(2, 3)).real.transpose(0, 2, 3, 1)
        A_f = kernel_to_freq_2d(A_kernel, H, W).transpose(1, 2, 0)
        B_f = kernel_to_freq_2d(B_kernel, H, W).transpose(1, 2, 0)
        gA_f = kernel_to_freq_2d(gate_A_kernel, H, W).transpose(1, 2, 0)
        gB_f = kernel_to_freq_2d(gate_B_kernel, H, W).transpose(1, 2, 0)
        x_f = jnp.fft.fft2(x.transpose(0, 3, 1, 2), axes=(2, 3)).transpose(0, 2, 3, 1)
        gate_A = jax.nn.sigmoid(ifft_real(gA_f[None] * x_f))
        gate_B = jax.nn.sigmoid(ifft_real(gB_f[None] * x_f))
        a_spatial = ifft_real(jnp.broadcast_to(A_f[None], (B, H, W, C)))
        b_spatial = ifft_real(B_f[None] * x_f)
        a_t = a_spatial * gate_A
        b_t = b_spatial * gate_B
        gate_seq = jnp.tile(a_t[None], (T, 1, 1, 1, 1))
        h_tilde_seq = jnp.tile(b_t[None], (T, 1, 1, 1, 1))
        log_z = -jax.nn.softplus(-gate_seq)
        log_coeffs = -jax.nn.softplus(gate_seq)
        log_values = log_z + jnp.log(jax.nn.softplus(h_tilde_seq) + EPS)
        log_h = heinsen_scan_log(log_coeffs, log_values)
        h_final = jnp.exp(log_h[-1])
        return h_final @ W_out + b_out

    def _gn(v, G=32, eps=1e-5):
        B_, H_, W_, C_ = v.shape
        g = v.reshape(B_, H_, W_, G, C_ // G)
        m = jnp.mean(g, axis=(1, 2, 4), keepdims=True)
        s = jnp.var(g, axis=(1, 2, 4), keepdims=True)
        return ((g - m) / jnp.sqrt(s + eps)).reshape(v.shape)

    def _ln_c(v, eps=1e-6):
        m = jnp.mean(v, axis=-1, keepdims=True)
        s = jnp.var(v, axis=-1, keepdims=True)
        return (v - m) / jnp.sqrt(s + eps)

    def _ln_t(v, eps=1e-5):
        m = jnp.mean(v, axis=-1, keepdims=True)
        s = jnp.var(v, axis=-1, keepdims=True)
        return (v - m) / jnp.sqrt(s + eps)

    def _to_tokens(v):
        B_, H_, W_, C_ = v.shape
        return v.reshape(B_, H_ * W_, C_)
    def _from_tokens(t, like):
        return t.reshape(like.shape)

    x = x + _L0_conv_ref(_gn(x), L0_conv_single_mask, L0_conv_ln_gamma, L0_conv_ln_beta, L0_conv_Wq, L0_conv_Wk, L0_conv_Wv, L0_conv_Wb, L0_conv_Wg, L0_conv_Wout)
    x = x + _L1_conv_ref(_gn(x), L1_conv_A_kernel, L1_conv_B_kernel, L1_conv_gate_A_kernel, L1_conv_gate_B_kernel, L1_conv_W_out, L1_conv_b_out, 8)
    return x


_drawn_inputs = setup_inputs


def setup_inputs(seed=0):
    import zlib

    import numpy as np

    out = dict(_drawn_inputs(seed))
    spreads = {'L0_conv_ln_gamma': (1.0, 0.542),
     'L0_conv_ln_beta': (0.0, 0.1),
     'L1_conv_b_out': (0.0, 0.1)}
    factors = {'L1_conv_A_kernel': 8.0, 'L1_conv_gate_A_kernel': 8.0, 'L1_conv_gate_B_kernel': 3.76}
    for name, (base, spread) in spreads.items():
        noise = np.random.default_rng([zlib.crc32(name.encode()), seed]).standard_normal(out[name].shape)
        drawn = base * np.exp(spread * noise) if base else spread * noise
        out[name] = jnp.asarray(drawn.astype(out[name].dtype))
    for name, factor in factors.items():
        out[name] = (out[name] * factor).astype(out[name].dtype)
    return out
```

```python
from contextlib import ExitStack

import concourse.bass as bass
from concourse import mybir

F32 = mybir.dt.float32
U8 = mybir.dt.uint8
ALU = mybir.AluOpType
ACT = mybir.ActivationFunctionType
AX = mybir.AxisListType
ds = bass.ds

P = 128
C = 128
N = 256
HEADS, DH = 4, 32
G, GC = 32, 4
TAPS = 7
R = TAPS // 2
GN_EPS, LN_EPS, SP_EPS = 1e-5, 1e-5, 1e-6
NEG = -1e9
WT = N // P

BH, BW = 8, 16
assert BH * BW == P
HB, WB = N // BH, N // BW
PITCH = BW + 2 * R
WROWS = BH + 2 * R
WIN = WROWS * PITCH
ORIGIN = (WROWS - 1 - R) * PITCH + (PITCH - 1 - R)
FLAT = 2 * ORIGIN + 4
CCH = 32
NCC = C // CCH
SROWS = 8
STRIPS = HB // SROWS
HPAD = N + 2 * BH


class Chain:

    def __init__(self, eng, sem, base=0):
        self.eng, self.sem, self.base, self.n = eng, sem, base, 0

    def link(self, ins):
        self.n += 1
        ins.then_inc(self.sem, 1)

    def wait(self):
        self.eng.wait_ge(self.sem, self.base + self.n)

    def step(self, ins):
        self.link(ins)
        self.wait()


def hold(eng, sem, value, passed):
    eng.wait_ge(sem, value)
    eng.sem_inc(passed, 1)


def bcast_rows(t, n):
    return t.unsqueeze(1).to_broadcast([t.shape[0], n, t.shape[1]])


def setup_stage(nc, d, b):
    with ExitStack() as ctx:
        def sem(name):
            return ctx.enter_context(nc.semaphore(name))

        w_in, pool_chain = sem("w_in"), sem("su_pool")
        block = ctx.enter_context(nc.Block())

        @block.sync
        def _(sp):
            for name in ("wq", "wk", "wv", "wg", "wo", "w2", "wb"):
                sp.dma_start(b[name][:, :], d[name]).then_inc(w_in, 16)
            sp.dma_start(b["gamma"][:, :], d["gamma"]).then_inc(w_in, 16)
            sp.dma_start(b["beta"][:, :], d["beta"]).then_inc(w_in, 16)
            sp.dma_start(b["bout"][:, :], d["bout"].partition_broadcast(P)).then_inc(w_in, 16)
            sp.dma_start(b["mask8"][:, :], d["mask"].partition_broadcast(P)).then_inc(w_in, 16)
            sp.wait_ge(w_in, 16 * 11)

        @block.gpsimd
        def _(pool):
            ch = Chain(pool, pool_chain)
            ch.link(pool.memset(b["ident"][:, :], 0.0))
            ch.link(pool.memset(b["mean_w"][:, :], 1.0 / P))
            ch.link(pool.memset(b["half"][:, :], 0.5))
            ch.link(pool.memset(b["pow"][:, :], -0.5))
            ch.step(pool.memset(b["acc"][:, :, :], 0.0))
            ch.step(pool.affine_select(out=b["ident"][:, :], in_=b["ident"][:, :], compare_op=ALU.not_equal,
                                       fill=1.0, base=0, pattern=[[-1, P]], channel_multiplier=1))


def stats_stage(nc, d, b):
    TOK = N * N // P
    TT = 64
    NT = TOK // TT
    xs = d["x"].rearrange("o h w c -> (o h w c)").rearrange("(p t c) -> p t c", p=P, c=C)
    with ExitStack() as ctx:
        def sem(name):
            return ctx.enter_context(nc.semaphore(name))

        def sb(name, shape):
            return ctx.enter_context(nc.sbuf_tensor(name, shape, F32))

        xt = [sb(f"st_x{s}", [P, TT, C]) for s in range(2)]
        st = sb("st_st", [P, G, NT, 6])
        mv = sb("st_mv", [P, G, 2])
        me = sb("st_me", [P, 2, G])
        tot = sb("st_tot", [P, 2, G])
        rs = sb("st_rs", [P, 4, G])
        ps = ctx.enter_context(nc.psum_tensor("st_ps", [P, 2, G], F32))
        loaded = [sem(f"st_loaded{s}") for s in range(2)]
        used, chain, sp_passed = sem("st_used"), sem("st_chain"), sem("st_spp")
        me_ready, sum_ready, var_ready, std_ready = sem("st_me"), sem("st_sum"), sem("st_var"), sem("st_std")
        block = ctx.enter_context(nc.Block())

        @block.sync
        def _(sp):
            for s in range(2):
                sp.dma_start(xt[s][:, :, :], xs[:, s * TT:(s + 1) * TT, :]).then_inc(loaded[s], 16)
            with sp.Fori(0, NT // 2 - 1) as n:
                for s in range(2):
                    hold(sp, used, n * 2 + s + 1, sp_passed)
                    sp.dma_start(xt[s][:, :, :], xs[:, ds(n * (2 * TT) + (2 + s) * TT, TT), :])\
                        .then_inc(loaded[s], 16)

        @block.vector
        def _(dve):
            with dve.Fori(0, NT // 2) as n:
                for s in range(2):
                    dve.wait_ge(loaded[s], n * 16 + 16)
                    for g in range(G):
                        last = dve.bn_stats(st[:, g, ds(n * 2 + s, 1), :].rearrange("p a b -> p (a b)"),
                                            xt[s][:, :, g * GC:(g + 1) * GC])
                    last.then_inc(used, 1)
            dve.wait_ge(used, NT)
            ch = Chain(dve, chain)
            for g in range(G):
                last = dve.bn_aggr(mv[:, g, :], st[:, g, :, :].rearrange("p a b -> p (a b)"))
            ch.step(last)
            ch.link(dve.tensor_copy(me[:, 0, :], mv[:, :, 0]))
            ch.step(dve.tensor_tensor(me[:, 1, :], mv[:, :, 0], mv[:, :, 0], ALU.mult))
            dve.tensor_tensor(me[:, 1, :], me[:, 1, :], mv[:, :, 1], ALU.add).then_inc(me_ready, 1)
            dve.wait_ge(sum_ready, 1)
            ch.step(dve.tensor_copy(tot[:, :, :], ps[:, :, :]))
            ch.step(dve.tensor_tensor(rs[:, 0, :], tot[:, 0, :], tot[:, 0, :], ALU.mult))
            ch.step(dve.tensor_tensor(rs[:, 1, :], tot[:, 1, :], rs[:, 0, :], ALU.subtract))
            dve.tensor_scalar(rs[:, 2, :], rs[:, 1, :], GN_EPS, None, ALU.add).then_inc(var_ready, 1)
            dve.wait_ge(std_ready, 1)
            ch.step(dve.reciprocal(rs[:, 0, :], rs[:, 3, :]))
            ch.step(dve.tensor_tensor(rs[:, 1, :], tot[:, 0, :], rs[:, 0, :], ALU.mult))
            for t, src, by in ((b["gn_a"], rs[:, 0, :], 1.0), (b["gn_b"], rs[:, 1, :], -1.0), (b["mean0"], tot[:, 0, :], 1.0)):
                ch.link(dve.tensor_scalar(t[:, :].rearrange("p (g c) -> p g c", c=GC),
                                          src.unsqueeze(2).to_broadcast([P, G, GC]), by, None, ALU.mult))

        @block.tensor
        def _(pe):
            pe.wait_ge(me_ready, 1)
            nc.tensor.matmul(ps[:, :, :].rearrange("p a g -> p (a g)"), b["mean_w"][:, :],
                             me[:, :, :].rearrange("p a g -> p (a g)"), start=True, stop=True).then_inc(sum_ready, 1)

        @block.scalar
        def _(act):
            act.wait_ge(var_ready, 1)
            act.activation(rs[:, 3, :], rs[:, 2, :], ACT.Sqrt).then_inc(std_ready, 1)


def norm_stage(nc, d, b):
    RQ = 4
    T = RQ * WT
    NQ = N // RQ
    xv = d["x"].rearrange("o r (t w) c -> w (o r t) c", t=WT)
    with ExitStack() as ctx:
        def sem(name):
            return ctx.enter_context(nc.semaphore(name))

        def sb(name, shape):
            return ctx.enter_context(nc.sbuf_tensor(name, shape, F32))

        xt = [sb(f"no_x{s}", [P, T, C]) for s in range(3)]
        xn = [sb(f"no_n{s}", [P, T, C]) for s in range(2)]
        st = sb("no_st", [P, 2, T, 6])
        mv = sb("no_mv", [P, 2, T, 2])
        ve = sb("no_ve", [P, 2, T])
        rstd = sb("no_rstd", [P, 2, T])
        zt = [sb(f"no_z{s}", [P, T * P]) for s in range(2)]
        bias_t = sb("no_bt", [P, WT, HEADS, N])
        bias_q = sb("no_bq", [P, WT, HEADS, N])
        negm = sb("no_negm", [P, N])
        zp = [ctx.enter_context(nc.psum_tensor(f"no_zp{k}", [P, 512], F32)) for k in range(4)]
        bp = [ctx.enter_context(nc.psum_tensor(f"no_bp{k}", [P, RQ, WT, HEADS], F32)) for k in range(2)]
        loaded = [sem(f"no_loaded{s}") for s in range(2)]
        stored = [sem(f"no_stored{s}") for s in range(2)]
        scaled, centred, mv_ready, rstd_ready, normed = (sem(f"no_{x}") for x in
                                                         ("scaled", "centred", "mv", "rstd", "normed"))
        z_psum, z_ready, b_psum, b_read = (sem(f"no_{x}") for x in ("zpsum", "zready", "bpsum", "bread"))
        pool_own, dve_own = sem("no_pool"), sem("no_dve")
        tr_ready, neg_ready = sem("no_tr"), sem("no_neg")
        tr_read = sem("no_trread")
        sp_passed, dve_passed, pool_passed = sem("no_spp"), sem("no_dvep"), sem("no_poolp")

        def pool_rstd(pool, n, s):
            hold(pool, mv_ready, n + 1, pool_passed)
            pool.tensor_scalar(ve[:, s, :], mv[:, s, :, 1], LN_EPS, None, ALU.add).then_inc(pool_own, 1)
            pool.wait_ge(pool_own, n + 1)
            pool.tensor_tensor(rstd[:, s, :], ve[:, s, :], b["pow"][:, 0:T], ALU.pow).then_inc(rstd_ready, 1)

        def dve_stats(dve, n, s):
            dve.wait_ge(scaled, n + 1)
            dve.tensor_tensor(xn[s][:, :, :], xn[s][:, :, :], bcast_rows(b["gn_b"][:, :], T), ALU.add)\
                .then_inc(centred, 1)
            dve.wait_ge(centred, n + 1)
            for t in range(T):
                last = dve.bn_stats(st[:, s, t, :], xn[s][:, t, :])
            last.then_inc(dve_own, 1)
            hold(dve, dve_own, n + 1, dve_passed)
            for t in range(T):
                last = dve.bn_aggr(mv[:, s, t, :], st[:, s, t, :])
            last.then_inc(mv_ready, 1)

        def dve_normalise(dve, n, s):
            dve.wait_ge(rstd_ready, n + 1)
            for t in range(T):
                last = dve.tensor_scalar(xn[s][:, t, :], xn[s][:, t, :], mv[:, s, t, 0:1], rstd[:, s, t:t + 1],
                                         ALU.subtract, ALU.mult)
            last.then_inc(normed, 1)

        def dve_bias(dve, n, s):
            dve.wait_ge(b_psum, n + 1)
            for t in range(WT):
                last = dve.tensor_scalar(bias_t[:, t, :, ds(n * RQ, RQ)].rearrange("p h r -> p r h"),
                                         bp[s][:, :, t, :], -1.0, None, ALU.mult)
            last.then_inc(b_read, 1)

        def pe_transpose(pe, n, s):
            pe.wait_ge(normed, n + 1)
            for k in range(2):
                for t in range(4):
                    last = nc.tensor.transpose(zp[2 * s + k][:, t * P:(t + 1) * P], xn[s][:, 4 * k + t, :], b["ident"][:, :])
                last.then_inc(z_psum, 1)

        def pe_bias(pe, n, s):
            pe.wait_ge(z_ready, n * 2 + 2)
            for t in range(T):
                last = nc.tensor.matmul(bp[s][:, t // WT, t % WT, :], zt[s][:, t * P:(t + 1) * P], b["wb"][:, :],
                                        start=True, stop=True)
            last.then_inc(b_psum, 1)

        block = ctx.enter_context(nc.Block())

        @block.sync
        def _(sp):
            for s in range(2):
                sp.dma_start(xt[s][:, :, :], xv[:, s * T:(s + 1) * T, :]).then_inc(loaded[s], 16)
            with sp.Fori(0, NQ // 2 - 1) as n:
                for s in range(2):
                    hold(sp, scaled, n * 2 + s + 1, sp_passed)
                    sp.dma_start(xt[s][:, :, :], xv[:, ds(n * (2 * T) + (2 + s) * T, T), :]).then_inc(loaded[s], 16)

        @block.gpsimd
        def _(pool):
            def scale(n, s, half, first):
                pool.wait_ge(loaded[s], half * 16 + 16)
                if not first:
                    pool.wait_ge(z_psum, n * 2 - 2)
                pool.tensor_tensor(xn[s][:, :, :], xt[s][:, :, :], bcast_rows(b["gn_a"][:, :], T), ALU.mult)\
                    .then_inc(scaled, 1)

            scale(0, 0, 0, True)
            scale(1, 1, 0, True)
            with pool.Fori(0, NQ // 2 - 1) as m:
                for s in range(2):
                    pool_rstd(pool, m * 2 + s, s)
                    scale(m * 2 + (s + 2), s, m + 1, False)
            for s in range(2):
                pool_rstd(pool, NQ - 2 + s, s)

        @block.vector
        def _(dve):
            dve_stats(dve, 0, 0)
            dve_stats(dve, 1, 1)
            dve_normalise(dve, 0, 0)
            with dve.Fori(0, NQ // 2 - 1) as m:
                for s in range(2):
                    dve_stats(dve, m * 2 + (s + 2), s)
                    dve_normalise(dve, m * 2 + (s + 1), 1 - s)
                    dve_bias(dve, m * 2 + s, s)
            dve_normalise(dve, NQ - 1, 1)
            dve_bias(dve, NQ - 2, 0)
            dve_bias(dve, NQ - 1, 1)
            dve.tensor_scalar(negm[:, :], b["mask8"][:, :], NEG, -NEG, ALU.mult, ALU.add).then_inc(neg_ready, 1)
            dve.wait_ge(b_read, NQ)
            for k in range(WT):
                for h in range(HEADS):
                    dve.tensor_copy(bias_q[:, k, h, :].rearrange("p (t m b) -> p t m b", t=WT, b=WB),
                                    bias_t[:, k, h, :].rearrange("p (b t m) -> p t m b", t=WT, b=WB)).then_inc(neg_ready, 1)
            dve.wait_ge(neg_ready, 1)
            for h in range(HEADS):
                dve.wait_ge(tr_ready, h + 1)
                for j in range(WT):
                    last = dve.tensor_tensor(b["nbias"][:, j, h, :], zp[h % 2][:, j * N:(j + 1) * N], negm[:, :], ALU.add)
                last.then_inc(tr_read, 1)

        @block.tensor
        def _(pe):
            pe_transpose(pe, 0, 0)
            pe_transpose(pe, 1, 1)
            pe_bias(pe, 0, 0)
            pe_bias(pe, 1, 1)
            with pe.Fori(1, NQ // 2) as m:
                for s in range(2):
                    pe.wait_ge(z_ready, m * 4 + (2 * s - 2))
                    pe_transpose(pe, m * 2 + s, s)
                    pe.wait_ge(b_read, m * 2 + (s - 1))
                    pe_bias(pe, m * 2 + s, s)
            pe.wait_ge(neg_ready, 1 + WT * HEADS)
            for h in range(HEADS):
                if h >= 2:
                    pe.wait_ge(tr_read, h - 1)
                for j in range(WT):
                    for k in range(WT):
                        last = nc.tensor.transpose(zp[h % 2][:, j * N + k * P:j * N + (k + 1) * P],
                                                   bias_q[:, k, h, j * P:(j + 1) * P], b["ident"][:, :])
                last.then_inc(tr_ready, 1)

        @block.scalar
        def _(act):
            def copy_out(n, s, m):
                for k in range(2):
                    act.wait_ge(z_psum, n * 2 + k + 1)
                    act.activation(zt[s][:, k * 512:(k + 1) * 512], zp[2 * s + k][:, :], ACT.Identity,
                                   bias=b["beta"][:, :], scale=b["gamma"][:, :]).then_inc(z_ready, 1)
                act.wait_ge(z_ready, n * 2 + 2)
                act.dma_start(d["znt"][:, ds(n * (T * P), T * P)], zt[s][:, :]).then_inc(stored[s], 16)

            copy_out(0, 0, 0)
            copy_out(1, 1, 0)
            with act.Fori(1, NQ // 2) as m:
                for s in range(2):
                    act.wait_ge(stored[s], m * 16)
                    act.wait_ge(b_psum, m * 2 + (s - 1))
                    copy_out(m * 2 + s, s, m)
            for s in range(2):
                act.wait_ge(stored[s], NQ // 2 * 16)


def attention_stage(nc, d, b):
    xv = [d["x"][0].rearrange("r (b t m) c -> t r m b c", t=WT, m=BW // WT)[t] for t in range(WT)]
    nat = [d["x1"].rearrange("r (b t m) c -> t r m b c", t=WT, m=BW // WT)[t] for t in range(WT)]

    def row_of(v, r):
        return v[r] if isinstance(r, int) else v[ds(r, 1)].squeeze(0)

    halo = [d["x1h"].rearrange("q r m b c -> r (m b) q c")[:, t * P:(t + 1) * P, :, :] for t in range(WT)]
    QSCALE = -1.0 / float(DH) ** 0.5
    with ExitStack() as ctx:
        def sem(name):
            return ctx.enter_context(nc.semaphore(name))

        def sb(name, shape):
            return ctx.enter_context(nc.sbuf_tensor(name, shape, F32))

        def pb(name, shape):
            return ctx.enter_context(nc.psum_tensor(name, shape, F32))

        znt = [sb(f"at_znt{s}", [P, N]) for s in range(2)]
        xin = [sb(f"at_x{s}", [P, WT, C]) for s in range(2)]
        qt = [sb(f"at_q{s}", [P, N]) for s in range(2)]
        kt = [sb(f"at_k{s}", [P, N]) for s in range(2)]
        gt = [sb(f"at_gate{s}", [P, N]) for s in range(3)]
        v = [sb(f"at_v{s}", [P, WT, C]) for s in range(3)]
        probs = [sb(f"at_p{s}", [P, HEADS, WT, N]) for s in range(2)]
        top = [sb(f"at_top{s}", [P, WT, HEADS]) for s in range(2)]
        tot = [sb(f"at_tot{s}", [P, WT, HEADS]) for s in range(2)]
        rec = [sb(f"at_rec{s}", [P, WT * HEADS]) for s in range(2)]
        rb = [sb(f"at_rb{s}", [P, WT * HEADS, DH]) for s in range(2)]
        pt = [sb(f"at_pt{k}", [P, WT, N]) for k in range(2)]
        g1 = sb("at_g1", [P, N])
        og = [sb(f"at_og{s}", [P, N]) for s in range(2)]
        x1 = [sb(f"at_x1{s}", [P, WT, C]) for s in range(2)]
        dev = sb("at_dev", [P, WT, C])
        sq = sb("at_sq", [P, WT, C])

        s_ps = [pb(f"at_s{k}", [P, WT, N]) for k in range(2)]
        pt_ps = [pb(f"at_ptp{k}", [P, WT, N]) for k in range(2)]
        qg_ps, kv_ps, or_ps = pb("at_qg", [P, 2, N]), pb("at_kv", [P, 2, N]), pb("at_or", [P, 2, N])
        w_ps = pb("at_w", [P, 2, N])

        znt_in = [sem(f"at_znt_in{s}") for s in range(2)]
        x_in = [sem(f"at_x_in{s}") for s in range(2)]
        stored = [sem(f"at_stored{s}") for s in range(2)]
        qg_done, kv_done = sem("at_qg_done"), sem("at_kv_done")
        q_ready, k_ready, g_ready, v_ready = (sem(f"at_{x}_ready") for x in "qkgv")
        s_done, s_read, p_ready = sem("at_s_done"), sem("at_s_read"), sem("at_p_ready")
        pt_done, pt_even, pt_odd, o_done = sem("at_pt_done"), sem("at_pt_even"), sem("at_pt_odd"), sem("at_o_done")
        rec_ready, rb_ready, r_done, og_ready = sem("at_rec"), sem("at_rb"), sem("at_r_done"), sem("at_og")
        g1_ready = sem("at_g1_ready")
        w_done, x1_ready, acc_done, pool_own = sem("at_w_done"), sem("at_x1_ready"), sem("at_acc"), sem("at_pool")
        sp_passed, dve_passed = sem("at_spp"), sem("at_dvep")
        STORES = 4

        block = ctx.enter_context(nc.Block())

        def rows(eng, step):
            lead = 4
            body = 6
            turns = (N - 1 - lead) // body
            for i in range(lead):
                step(i, i)
            with eng.Fori(0, turns) as m:
                for u in range(body):
                    step(m * body + (lead + u), lead + u)
            for i in range(lead + turns * body, N + 2):
                step(i, i)

        def full(i):
            return isinstance(i, int)

        @block.sync
        def _(sp):
            sp.dma_start(znt[0][:, :], d["znt"][:, 0:N]).then_inc(znt_in[0], 16)
            sp.dma_start(znt[1][:, :], d["znt"][:, N:2 * N]).then_inc(znt_in[1], 16)
            for t in range(2):
                for j in range(WT):
                    sp.dma_start(xin[t][:, j, :], row_of(xv[j], t)).then_inc(x_in[t], 16)

            def store(r, u):
                s = u % 2
                hold(sp, x1_ready, r + 1, sp_passed)
                for t in range(WT):
                    sp.dma_start(row_of(nat[t], r), x1[s][:, t, :]).then_inc(stored[s], 16)
                    sp.dma_start(row_of(halo[t], r + BH), x1[s][:, t, :].rearrange("p (q c) -> p q c", c=CCH))\
                        .then_inc(stored[s], 16)

            def step(i, u):
                if not full(i) or i + 2 < N:
                    hold(sp, kv_done, i + 1, sp_passed)
                    sp.dma_start(znt[u % 2][:, :], d["znt"][:, ds(i * N + 2 * N, N)]).then_inc(znt_in[u % 2], 16)
                if u >= 2:
                    store(i - 2, u)
                    if not full(i) or i < N:
                        for j in range(WT):
                            sp.dma_start(xin[u % 2][:, j, :], row_of(xv[j], i)).then_inc(x_in[u % 2], 16)

            rows(sp, step)
            for s in range(2):
                sp.wait_ge(stored[s], N // 2 * STORES * 16)

        @block.tensor
        def _(pe):
            def project(r, u):
                s = u % 2
                pe.wait_ge(znt_in[s], (r + (2 - s)) * 8)
                queries = znt[s][:, :].rearrange("p (b t m) -> p t m b", t=WT, m=BW // WT)
                if u >= 1:
                    pe.wait_ge(g_ready, r)
                nc.tensor.matmul(qg_ps[:, 0, :], b["wq"][:, :], queries, start=True, stop=True)
                nc.tensor.matmul(qg_ps[:, 1, :], b["wg"][:, :], queries, start=True, stop=True).then_inc(qg_done, 1)
                if u >= 1:
                    pe.wait_ge(v_ready, r)
                nc.tensor.matmul(kv_ps[:, 0, :], b["wk"][:, :], znt[s][:, :], start=True, stop=True)
                for t in range(WT):
                    last = nc.tensor.matmul(kv_ps[:, 1, t * P:(t + 1) * P], znt[s][:, t * P:(t + 1) * P], b["wv"][:, :],
                                            start=True, stop=True)
                last.then_inc(kv_done, 1)

            def scores(r, u, h):
                s = u % 2
                if h == 0:
                    pe.wait_ge(q_ready, r + 1)
                    pe.wait_ge(k_ready, r + 1)
                if u >= 1 or h >= 2:
                    pe.wait_ge(s_read, r * HEADS + (h - 1))
                lo = h * DH
                for j in range(WT):
                    last = nc.tensor.matmul(s_ps[h % 2][:, j, :], qt[s][lo:lo + DH, j * P:(j + 1) * P], kt[s][lo:lo + DH, :],
                                            start=True, stop=True)
                last.then_inc(s_done, 1)

            def transposes(r, u, h):
                s = u % 2
                pe.wait_ge(p_ready, r * HEADS + (h + 1))
                if u >= 1 or h >= 2:
                    if h % 2 == 0:
                        pe.wait_ge(pt_even, r * 2 + h // 2)
                    else:
                        pe.wait_ge(pt_odd, r * 2 + h // 2)
                for k in range(WT):
                    for j in range(WT):
                        last = nc.tensor.transpose(pt_ps[h % 2][:, k, j * P:(j + 1) * P],
                                                   probs[s][:, h, j, k * P:(k + 1) * P], b["ident"][:, :])
                last.then_inc(pt_done, 1)

            def values(r, u, h):
                if h == 0:
                    pe.wait_ge(v_ready, r + 1)
                    if u >= 1:
                        pe.wait_ge(og_ready, r)
                if h % 2 == 0:
                    pe.wait_ge(pt_even, r * 2 + (h // 2 + 1))
                else:
                    pe.wait_ge(pt_odd, r * 2 + (h // 2 + 1))
                lo = h * DH
                for k in range(WT):
                    last = nc.tensor.matmul(or_ps[lo:lo + DH, 0, :], v[u % 3][:, k, lo:lo + DH], pt[h % 2][:, k, :],
                                            start=(k == 0), stop=(k == WT - 1), tile_position=(0, lo))
                last.then_inc(o_done, 1)

            def sums(r, u):
                pe.wait_ge(rb_ready, r + 1)
                for j in range(WT):
                    last = nc.tensor.transpose(or_ps[:, 1, j * P:(j + 1) * P],
                                               rb[u % 2][:, j * HEADS:(j + 1) * HEADS, :].rearrange("p h c -> p (h c)"),
                                               b["ident"][:, :])
                last.then_inc(r_done, 1)

            def output(r, u):
                pe.wait_ge(og_ready, r + 1)
                if u >= 1:
                    pe.wait_ge(x1_ready, r)
                for j in range(WT):
                    last = nc.tensor.matmul(w_ps[:, 0, j * P:(j + 1) * P], og[u % 2][:, j * P:(j + 1) * P], b["wo"][:, :],
                                            start=True, stop=True)
                last.then_inc(w_done, 1)

            project(0, 0)

            def step(i, u):
                now = not full(i) or i < N
                back = u >= 1 and (not full(i) or i - 1 < N)
                for h in range(HEADS):
                    if now:
                        scores(i, u, h)
                    if back:
                        transposes(i - 1, u - 1, h)
                        if h >= 1:
                            values(i - 1, u - 1, h - 1)
                    if h == 2:
                        if not full(i) or i + 1 < N:
                            project(i + 1, u + 1)
                        if u >= 2:
                            output(i - 2, u - 2)
                if back:
                    values(i - 1, u - 1, HEADS - 1)
                    sums(i - 1, u - 1)

            rows(pe, step)

        @block.vector
        def _(dve):
            def key_value(r, u):
                dve.wait_ge(kv_done, r + 1)
                if u >= 2:
                    dve.wait_ge(s_done, (r - 1) * HEADS)
                dve.tensor_copy(kt[u % 2][:, :], kv_ps[:, 0, :]).then_inc(k_ready, 1)
                if u >= 3:
                    dve.wait_ge(o_done, (r - 2) * HEADS)
                dve.tensor_copy(v[u % 3][:, :, :].rearrange("p t c -> p (t c)"), kv_ps[:, 1, :]).then_inc(v_ready, 1)

            def bias_max(r, u, h):
                if u >= 2:
                    dve.wait_ge(pt_done, r * HEADS + (h + 1 - 2 * HEADS))
                hold(dve, s_done, r * HEADS + (h + 1), dve_passed)
                for j in range(WT):
                    last = dve.tensor_tensor_reduce(out=probs[u % 2][:, h, j, :], in0=s_ps[h % 2][:, j, :],
                                                    in1=b["nbias"][:, j, h, :], scale=1.0, scalar=3.0e38,
                                                    op0=ALU.add, op1=ALU.min, accum_out=top[u % 2][:, j, h:h + 1])
                last.then_inc(s_read, 1)

            def copy_pt(r, u, h):
                dve.wait_ge(pt_done, r * HEADS + (h + 1))
                if u >= 1 or h >= 2:
                    dve.wait_ge(o_done, r * HEADS + (h - 1))
                dve.tensor_copy(pt[h % 2][:, :, :], pt_ps[h % 2][:, :, :]).then_inc(pt_odd, 1)

            def reciprocals(r, u):
                dve.wait_ge(p_ready, r * HEADS + HEADS)
                if u >= 2:
                    dve.wait_ge(rb_ready, r - 1)
                dve.reciprocal(rec[u % 2][:, :], tot[u % 2][:, :, :].rearrange("p t h -> p (t h)")).then_inc(rec_ready, 1)

            def gate(r, u):
                dve.wait_ge(r_done, r + 1)
                dve.wait_ge(g_ready, r + 1)
                dve.scalar_tensor_tensor(g1[:, :], gt[u % 3][:, :], 1.0, or_ps[:, 1, :], ALU.add, ALU.mult)\
                    .then_inc(g1_ready, 1)
                dve.wait_ge(g1_ready, r + 1)
                dve.wait_ge(o_done, r * HEADS + HEADS)
                if u >= 2:
                    dve.wait_ge(w_done, r - 1)
                dve.tensor_tensor(og[u % 2][:, :], g1[:, :], or_ps[:, 0, :], ALU.mult).then_inc(og_ready, 1)

            def residual(r, u):
                s = u % 2
                dve.wait_ge(w_done, r + 1)
                dve.wait_ge(x_in[s], (r + (2 - s)) * 16)
                if u >= 2:
                    dve.wait_ge(stored[s], (r - s) * (8 * STORES))
                    dve.wait_ge(acc_done, r - 1)
                dve.tensor_tensor(x1[s][:, :, :].rearrange("p t c -> p (t c)"), w_ps[:, 0, :],
                                  xin[s][:, :, :].rearrange("p t c -> p (t c)"), ALU.add).then_inc(x1_ready, 1)

            key_value(0, 0)

            def step(i, u):
                now = not full(i) or i < N
                back = u >= 1 and (not full(i) or i - 1 < N)
                if back:
                    reciprocals(i - 1, u - 1)
                for h in range(HEADS):
                    if now:
                        bias_max(i, u, h)
                    if back and h % 2:
                        copy_pt(i - 1, u - 1, h)
                    if h == 2:
                        if not full(i) or i + 1 < N:
                            key_value(i + 1, u + 1)
                        if u >= 2:
                            residual(i - 2, u - 2)
                if back:
                    gate(i - 1, u - 1)

            rows(dve, step)

        @block.scalar
        def _(act):
            def query_gate(r, u):
                act.wait_ge(qg_done, r + 1)
                if u >= 2:
                    act.wait_ge(s_done, (r - 1) * HEADS)
                act.activation(qt[u % 2][:, :], qg_ps[:, 0, :], ACT.Copy, scale=QSCALE).then_inc(q_ready, 1)
                if u >= 3:
                    act.wait_ge(g1_ready, r - 2)
                act.activation(gt[u % 3][:, :], qg_ps[:, 1, :], ACT.Tanh, scale=0.5).then_inc(g_ready, 1)

            def exponentials(r, u, h):
                act.wait_ge(s_read, r * HEADS + (h + 1))
                if u >= 2 and h == 0:
                    act.wait_ge(rec_ready, r - 1)
                for j in range(WT):
                    row = probs[u % 2][:, h, j, :]
                    last = act.activation(row, row, ACT.Exp, scale=-1.0, bias=top[u % 2][:, j, h:h + 1],
                                          accum_out=tot[u % 2][:, j, h:h + 1])
                last.then_inc(p_ready, 1)

            def copy_pt(r, u, h):
                act.wait_ge(pt_done, r * HEADS + (h + 1))
                if u >= 1 or h >= 2:
                    act.wait_ge(o_done, r * HEADS + (h - 1))
                act.activation(pt[h % 2][:, :, :], pt_ps[h % 2][:, :, :], ACT.Copy).then_inc(pt_even, 1)

            query_gate(0, 0)

            def step(i, u):
                now = not full(i) or i < N
                back = u >= 1 and (not full(i) or i - 1 < N)
                for h in range(HEADS):
                    if back and h % 2 == 0:
                        copy_pt(i - 1, u - 1, h)
                    if now:
                        exponentials(i, u, h)
                    if h == 2 and (not full(i) or i + 1 < N):
                        query_gate(i + 1, u + 1)

            rows(act, step)

        @block.gpsimd
        def _(pool):
            def spread(r, u):
                pool.wait_ge(rec_ready, r + 1)
                if u >= 2:
                    pool.wait_ge(r_done, r - 1)
                pool.tensor_tensor(rb[u % 2][:, :, :], rec[u % 2][:, :].unsqueeze(2).to_broadcast([P, WT * HEADS, DH]),
                                   b["half"][:, :].rearrange("p (a c) -> p a c", c=DH), ALU.mult).then_inc(rb_ready, 1)

            def accumulate(r, u):
                s = u % 2
                pool.wait_ge(x1_ready, r + 1)
                pool.tensor_tensor(dev[:, :, :], x1[s][:, :, :], bcast_rows(b["mean0"][:, :], WT), ALU.subtract)\
                    .then_inc(acc_done, 1)
                pool.wait_ge(acc_done, r + 1)
                pool.tensor_tensor(sq[:, :, :], dev[:, :, :], dev[:, :, :], ALU.mult).then_inc(pool_own, 1)
                pool.tensor_tensor(b["acc"][:, 0, :], b["acc"][:, 0, :], dev[:, :, :].rearrange("p t c -> p (t c)"), ALU.add)\
                    .then_inc(pool_own, 1)
                pool.wait_ge(pool_own, r * 3 + 2)
                pool.tensor_tensor(b["acc"][:, 1, :], b["acc"][:, 1, :], sq[:, :, :].rearrange("p t c -> p (t c)"), ALU.add)\
                    .then_inc(pool_own, 1)
                pool.wait_ge(pool_own, r * 3 + 3)

            def step(i, u):
                if u >= 1 and (not full(i) or i - 1 < N):
                    spread(i - 1, u - 1)
                if u >= 2:
                    accumulate(i - 2, u - 2)

            rows(pool, step)


def corner_stage(nc, d, b):
    K2 = TAPS * TAPS
    S = 2 * TAPS - 1
    SC = 1.0 / (N * N // P * GC)
    with ExitStack() as ctx:
        def sem(name):
            return ctx.enter_context(nc.semaphore(name))

        def sb(name, shape):
            return ctx.enter_context(nc.sbuf_tensor(name, shape, F32))

        sums = sb("co_sums", [P, 2, C])
        gsum = sb("co_gsum", [P, 2, G])
        tot = sb("co_tot", [P, 2, G])
        rs = sb("co_rs", [P, 4, G])
        m0 = sb("co_m0", [P, G])
        patch = sb("co_patch", [K2, K2, C])
        kern = [sb(f"co_kern{i}", [K2, K2, C]) for i in range(3)]
        conv = sb("co_conv", [K2, 3, C])
        at = sb("co_at", [K2, C])
        x1c = sb("co_x1", [K2, C])
        w = [sb(f"co_w{i}", [K2, C]) for i in range(8)]
        ht = sb("co_ht", [C, K2])
        raw = sb("co_raw", [C, 2, K2])
        flat = sb("co_flat", [C, 2, FLAT])
        acol = sb("co_acol", [C, 1])
        cps = ctx.enter_context(nc.psum_tensor("co_cps", [C, P], F32))
        scale_ready, scale_col, raw_in, flat_ready, flat_out = (sem(f"co_{x}") for x in
                                                                ("scale", "scol", "raw", "flatr", "flato"))
        ps = ctx.enter_context(nc.psum_tensor("co_ps", [P, 2, G], F32))
        tp = ctx.enter_context(nc.psum_tensor("co_tp", [C, K2], F32))
        op = ctx.enter_context(nc.psum_tensor("co_op", [K2, C], F32))
        halo_done, square_done, patch_in, kern_in, small_in = (sem(f"co_{x}") for x in
                                                               ("halo", "square", "patch", "kern", "small"))
        chain, gsum_ready, mean_ready, var_ready, std_ready = (sem(f"co_{x}") for x in
                                                               ("chain", "gsumr", "meanr", "varr", "stdr"))
        conv_ready, gates, b_ready, act_own, sp_ready, h_ready, t_done, ht_ready, o_done = (
            sem(f"co_{x}") for x in ("convr", "gates", "br", "acto", "spr", "hr", "td", "htr", "od"))
        block = ctx.enter_context(nc.Block())

        @block.sync
        def _(sp):
            sq = d["square"]
            for dst, src, n in ((0, N - R - R, R + R), (R + R, 0, R + R + 1)):
                for dst2, src2, n2 in ((0, N - R - R, R + R), (R + R, 0, R + R + 1)):
                    sp.dma_start(sq[dst:dst + n, dst2:dst2 + n2, :], d["x1"][src:src + n, src2:src2 + n2, :])\
                        .then_inc(square_done, 16)
            sp.dma_start(raw[:, 0, :], d["gB"]).then_inc(raw_in, 16)
            sp.dma_start(raw[:, 1, :], d["kB"]).then_inc(raw_in, 16)
            for i in range(3):
                sp.dma_start(kern[i][:, :, :].rearrange("p t c -> p (t c)"), d["taps"][i].rearrange("t c -> (t c)")
                             .partition_broadcast(K2)).then_inc(kern_in, 16)
            sp.dma_start(at[:, :], d["kA"]).then_inc(small_in, 16)
            sp.wait_ge(square_done, 64)
            sp.dma_start(x1c[:, :], sq[R:R + TAPS, R:R + TAPS, :]).then_inc(small_in, 16)
            for a in range(TAPS):
                rows = sq[a:a + TAPS].rearrange("t u c -> t (u c)")
                window = bass.AP(rows.tensor, rows.offset, [[C, TAPS], [S * C, TAPS], [1, TAPS * C]])
                sp.dma_start(patch[a * TAPS:(a + 1) * TAPS, :, :], window).then_inc(patch_in, 16)
            sp.dma_start(d["x1h"][:, 0:BH], d["x1h"][:, N:N + BH]).then_inc(halo_done, 16)
            sp.dma_start(d["x1h"][:, N + BH:HPAD], d["x1h"][:, BH:2 * BH]).then_inc(halo_done, 16)
            sp.wait_ge(halo_done, 32)
            sp.wait_ge(flat_ready, 2)
            sp.dma_start(d["flat"].rearrange("c k f -> c (k f)"),
                         flat[:, :, :].rearrange("p k f -> p (k f)")).then_inc(flat_out, 16)
            sp.wait_ge(flat_out, 16)

        @block.vector
        def _(dve):
            ch = Chain(dve, chain)
            ch.step(dve.tensor_tensor(sums[:, :, :], b["acc"][:, :, 0:C], b["acc"][:, :, C:2 * C], ALU.add))
            dve.tensor_reduce(gsum[:, :, :], sums[:, :, :].rearrange("p a (g c) -> p a g c", c=GC), AX.X, ALU.add)\
                .then_inc(gsum_ready, 1)
            dve.wait_ge(mean_ready, 1)
            ch.step(dve.tensor_scalar(tot[:, :, :], ps[:, :, :], SC, None, ALU.mult))
            ch.step(dve.tensor_tensor(rs[:, 0, :], tot[:, 0, :], tot[:, 0, :], ALU.mult))
            ch.step(dve.tensor_tensor(rs[:, 1, :], tot[:, 1, :], rs[:, 0, :], ALU.subtract))
            dve.tensor_scalar(rs[:, 2, :], rs[:, 1, :], GN_EPS, None, ALU.add).then_inc(var_ready, 1)
            ch.step(dve.tensor_tensor(m0[:, :], tot[:, 0, :], b["mean0"][:, :].rearrange("p (g c) -> p g c", c=GC)[:, :, 0],
                                      ALU.add))
            dve.wait_ge(std_ready, 1)
            ch.step(dve.reciprocal(rs[:, 0, :], rs[:, 3, :]))
            for t, src in ((b["gn_a"], rs[:, 0, :]), (b["mean0"], m0[:, :])):
                ch.step(dve.tensor_scalar(t[:, :].rearrange("p (g c) -> p g c", c=GC),
                                          src.unsqueeze(2).to_broadcast([P, G, GC]), 1.0, None, ALU.mult))
            dve.sem_inc(scale_ready, 1)
            taps = flat[:, :, ORIGIN - R * PITCH - R:ORIGIN - R * PITCH - R + TAPS * PITCH]\
                .rearrange("p k (t q) -> p k t q", q=PITCH)
            ch.step(dve.memset(flat[:, :, :], 0.0))
            dve.wait_ge(raw_in, 32)
            dve.wait_ge(scale_col, 1)
            ch.step(dve.tensor_copy(acol[:, :], cps[:, 0:1]))
            for k, by in ((0, 1.0), (1, 0.5)):
                dve.tensor_scalar(taps[:, k, :, 0:TAPS], raw[:, k, :].rearrange("p (t u) -> p t u", u=TAPS),
                                  acol[:, 0:1], by, ALU.mult, ALU.mult).then_inc(flat_ready, 1)
            dve.wait_ge(patch_in, 16 * TAPS)
            ch.step(dve.tensor_tensor(patch[:, :, :], patch[:, :, :], bcast_rows(b["mean0"][0:K2, :], K2), ALU.subtract))
            ch.step(dve.tensor_tensor(patch[:, :, :], patch[:, :, :], bcast_rows(b["gn_a"][0:K2, :], K2), ALU.mult))
            dve.wait_ge(kern_in, 48)
            for i in range(3):
                ch.step(dve.tensor_tensor(kern[i][:, :, :], kern[i][:, :, :], patch[:, :, :], ALU.mult))
                dve.tensor_reduce(conv[:, i, :], kern[i][:, :, :].rearrange("p t c -> p c t"), AX.X, ALU.add)\
                    .then_inc(conv_ready, 1)
            dve.wait_ge(gates, 2)
            dve.wait_ge(small_in, 32)
            ch.step(dve.tensor_tensor(w[2][:, :], at[:, :], w[0][:, :], ALU.mult))
            dve.tensor_tensor(w[3][:, :], conv[:, 2, :], w[1][:, :], ALU.mult).then_inc(b_ready, 1)
            dve.wait_ge(sp_ready, 3)
            ch.step(dve.scalar_tensor_tensor(w[6][:, :], w[3][:, :], 0.0, w[6][:, :], ALU.max, ALU.add))
            ch.step(dve.tensor_scalar(w[6][:, :], w[6][:, :], SP_EPS, None, ALU.add))
            ch.step(dve.tensor_tensor(w[6][:, :], w[6][:, :], w[4][:, :], ALU.mult))
            for i in range(3):
                ch.step(dve.scalar_tensor_tensor(w[6][:, :], w[5][:, :], 1.0, w[6][:, :], ALU.add, ALU.mult))
                if i < 2:
                    ch.step(dve.tensor_tensor(w[5][:, :], w[5][:, :], w[5][:, :], ALU.mult))
            ch.step(dve.tensor_copy(w[7][:, :], w[6][:, :]))
            dve.tensor_tensor(x1c[:, :], x1c[:, :], b["bout"][0:K2, :], ALU.add).then_inc(h_ready, 1)
            dve.wait_ge(t_done, 1)
            dve.tensor_copy(ht[:, :], tp[:, :]).then_inc(ht_ready, 1)
            dve.wait_ge(o_done, 1)
            ch.step(dve.tensor_tensor(b["corner"][:, :], op[:, :], x1c[:, :], ALU.add))

        @block.scalar
        def _(act):
            act.wait_ge(var_ready, 1)
            act.activation(rs[:, 3, :], rs[:, 2, :], ACT.Sqrt).then_inc(std_ready, 1)
            for i in range(2):
                act.wait_ge(conv_ready, i + 1)
                act.activation(w[i][:, :], conv[:, i, :], ACT.Sigmoid).then_inc(gates, 1)
            act.wait_ge(b_ready, 1)
            act.activation(w[4][:, :], w[2][:, :], ACT.Sigmoid).then_inc(sp_ready, 1)
            act.activation(w[5][:, :], w[2][:, :], ACT.Sigmoid, scale=-1.0).then_inc(sp_ready, 1)
            act.activation(w[6][:, :], w[3][:, :], ACT.Abs).then_inc(act_own, 1)
            act.wait_ge(act_own, 1)
            act.activation(w[6][:, :], w[6][:, :], ACT.Exp, scale=-1.0).then_inc(act_own, 1)
            act.wait_ge(act_own, 2)
            act.activation(w[6][:, :], w[6][:, :], ACT.Ln, bias=1.0).then_inc(sp_ready, 1)

        @block.tensor
        def _(pe):
            pe.wait_ge(gsum_ready, 1)
            nc.tensor.matmul(ps[:, :, :].rearrange("p a g -> p (a g)"), b["mean_w"][:, :],
                             gsum[:, :, :].rearrange("p a g -> p (a g)"), start=True, stop=True).then_inc(mean_ready, 1)
            pe.wait_ge(scale_ready, 1)
            nc.tensor.transpose(cps[:, :], b["gn_a"][:, :], b["ident"][:, :]).then_inc(scale_col, 1)
            pe.wait_ge(h_ready, 1)
            nc.tensor.transpose(tp[:, :], w[7][:, :], b["ident"][0:K2, 0:K2]).then_inc(t_done, 1)
            pe.wait_ge(ht_ready, 1)
            nc.tensor.matmul(op[:, :], ht[:, :], b["w2"][:, :], start=True, stop=True).then_inc(o_done, 1)


def conv_stage(nc, d, b):
    TG = 4
    GROUPS = C // TG
    SUB = 16
    XR = SROWS + 2
    QW = 4
    STEPS = P // QW
    RES = 4
    rows3 = ((R, BH, 0, 1), (0, R, BH - R, 0), (R + BH, R, 0, 2))
    cols3 = ((R, BW, 0, False), (0, R, BW - R, True), (R + BW, R, 0, True))
    scan = 1.0 - 0.5 ** 8
    with ExitStack() as ctx:
        def sem(name):
            return ctx.enter_context(nc.semaphore(name))

        def sb(name, shape):
            return ctx.enter_context(nc.sbuf_tensor(name, shape, F32))

        xc = [sb(f"cv_xc{s}", [P, XR, WB, CCH]) for s in range(2)]
        xl = [sb(f"cv_xl{s}", [P, XR, WB, CCH]) for s in range(2)]
        tk = [sb(f"cv_tk{s}", [P, TG, 2, WROWS, PITCH]) for s in range(2)]
        u = [sb(f"cv_u{s}", [P, SUB, P]) for s in range(2)]
        soft = sb("cv_soft", [P, SUB, P])
        h = sb("cv_h", [P, C, P])
        ht = [sb(f"cv_ht{s}", [P, QW * P]) for s in range(2)]
        res = [sb(f"cv_res{s}", [P, QW, C]) for s in range(RES)]
        eps = sb("cv_eps", [P, 1])
        cp = [ctx.enter_context(nc.psum_tensor(f"cv_cp{s}", [P, TG, 2, BH, BW], F32)) for s in range(2)]
        tp = [ctx.enter_context(nc.psum_tensor(f"cv_tp{s}", [P, QW * P], F32)) for s in range(2)]
        op = [ctx.enter_context(nc.psum_tensor(f"cv_op{s}", [P, QW * C], F32)) for s in range(2)]

        x_in = [sem(f"cv_x_in{s}") for s in range(2)]
        tk_in = [sem(f"cv_tk_in{s}") for s in range(2)]
        res_in = [sem(f"cv_res_in{s}") for s in range(RES)]
        res_free = [sem(f"cv_res_free{s}") for s in range(RES)]
        x_free, x_ready, group_done = sem("cv_x_free"), sem("cv_x_ready"), sem("cv_group")
        tanh_done, u_ready, soft_own, soft_ready, h_ready = (sem(f"cv_{x}") for x in
                                                             ("tanh", "ur", "softo", "softr", "hr"))
        t_done, ht_ready, o_done, o_ready, res_own = (sem(f"cv_{x}") for x in ("t", "htr", "o", "or", "reso"))
        eps_ready, corner_out, sp_passed = sem("cv_epsr"), sem("cv_corner"), sem("cv_spp")
        XDMA = 1 + 4 * R
        block = ctx.enter_context(nc.Block())

        def res_view(t, s, k):
            hm, wm = BH - 1 - k // (BW // QW), BW - QW - (k % (BW // QW)) * QW
            v = t.rearrange("(i h) (j w) c -> h i j w c", h=BH, w=BW)[hm]
            return v[ds(s * SROWS, SROWS), :, wm:wm + QW, :].rearrange("i j w c -> i j (w c)")

        @block.gpsimd
        def _(pool):
            pool.memset(eps[:, :], scan * SP_EPS).then_inc(eps_ready, 1)
            for s in range(2):
                pool.memset(xl[s][:, :, :, :], 0.0).then_inc(x_free, 1)
            with pool.Fori(0, STRIPS) as s:
                for q in range(NCC):
                    slot = q % 2

                    def part(lo, hi, m0, m1):
                        v = d["x1h"][q, ds(s * (SROWS * BH), XR * BH)].rearrange("(a h) m b c -> h m a b c", h=BH)
                        return v[:, m0:m1, :, lo:hi, :].rearrange("h m a b c -> (h m) a (b c)")

                    pool.wait_ge(x_free, s * NCC + (q + 1))
                    pool.dma_start(xc[slot][:, :, :, :].rearrange("p a b c -> p a (b c)"), part(0, WB, 0, BW))\
                        .then_inc(x_in[slot], 16)
                    for r in range(R):
                        for m, far, near in ((r, (0, WB - 1, 1, WB), (WB - 1, WB, 0, 1)),
                                             (BW - R + r, (1, WB, 0, WB - 1), (0, 1, WB - 1, WB))):
                            to = xl[slot][m:m + (BH - 1) * BW + 1:BW]
                            for t0, t1, f0, f1 in (far, near):
                                pool.dma_start(to[:, :, t0:t1, :].rearrange("p a b c -> p a (b c)"), part(f0, f1, m, m + 1))\
                                    .then_inc(x_in[slot], 16)
                    pool.wait_ge(x_in[slot], s * (NCC // 2 * XDMA * 16) + (q // 2 + 1) * XDMA * 16)
                    mean = b["mean0"][:, q * CCH:(q + 1) * CCH].unsqueeze(1).to_broadcast([P, XR * WB, CCH])
                    for t in (xc[slot], xl[slot]):
                        flat_t = t[:, :, :, :].rearrange("p a b c -> p (a b) c")
                        last = pool.tensor_tensor(flat_t, flat_t, mean, ALU.subtract)
                    last.then_inc(x_ready, 1)

        @block.sync
        def _(sp):
            for r in range(RES):
                sp.sem_inc(res_free[r], 16)
            flat = d["flat"]
            with sp.Fori(0, STRIPS) as s:
                with sp.Fori(0, GROUPS // 2) as g:
                    for slot in range(2):
                        hold(sp, group_done, s * GROUPS + g * 2 + (slot + 1), sp_passed)
                        for hm in range(BH):
                            windows = bass.AP(flat.tensor, g * (2 * TG * 2 * FLAT) + (slot * TG * 2 * FLAT + hm * PITCH),
                                              [[1, BW], [FLAT, TG * 2], [1, WIN]])
                            sp.dma_start(tk[slot][hm * BW:(hm + 1) * BW].rearrange("p c k a b -> p (c k) (a b)"), windows)\
                                .then_inc(tk_in[slot], 16)

                def load(k):
                    hold(sp, res_free[k % RES], s * (STEPS // RES * 16) + (k // RES + 1) * 16, sp_passed)
                    sp.dma_start(res[k % RES][:, :, :].rearrange("p w c -> p (w c)"), res_view(d["x1"], s, k))\
                        .then_inc(res_in[k % RES], 16)

                for k in range(RES - 1):
                    load(k)
                for k in range(STEPS):
                    if k + RES - 1 < STEPS:
                        load(k + RES - 1)
                    hold(sp, o_ready, s * STEPS + (k + 1), sp_passed)
                    sp.dma_start(res_view(d["out"][0], s, k), res[k % RES][:, :, :].rearrange("p w c -> p (w c)"))\
                        .then_inc(res_free[k % RES], 16)
            for r in range(RES):
                sp.wait_ge(res_free[r], (STRIPS * STEPS // RES + 1) * 16)
            for a0, na, h0 in ((0, R, N - R), (R, R + 1, 0)):
                for a in range(na):
                    for c0, ncol, w0 in ((0, R, N - R), (R, R + 1, 0)):
                        p0 = (a0 + a) * TAPS + c0
                        sp.dma_start(d["out"][0, h0 + a, w0:w0 + ncol, :], b["corner"][p0:p0 + ncol, :])\
                            .then_inc(corner_out, 16)
            sp.wait_ge(corner_out, 2 * TAPS * 16)

        @block.tensor
        def _(pe):
            pe.sem_inc(group_done, 2)
            with pe.Fori(0, STRIPS) as s:
                for c in range(C):
                    q, g, cl = c // CCH, c // TG, c % CCH
                    if cl == 0:
                        pe.wait_ge(x_ready, s * NCC + (q + 1))
                    if c % TG == 0:
                        pe.wait_ge(tk_in[g % 2], s * (GROUPS // 2 * BH * 16) + (g // 2 + 1) * BH * 16)
                        pe.wait_ge(u_ready, s * GROUPS + (g + 1))
                    for i, (cols, rows) in enumerate((cols, rows) for cols in cols3 for rows in rows3):
                        mr, nr, orow, arow = rows
                        mc, ncol, ocol, side = cols
                        src = (xl if side else xc)[q % 2]
                        last = nc.tensor.matmul(
                            cp[g % 2][:, c % TG, :, orow:orow + nr, ocol:ocol + ncol],
                            src[:, arow:arow + SROWS, :, cl].rearrange("p a b -> p (a b)"),
                            tk[g % 2][:, c % TG, :, mr:mr + nr, mc:mc + ncol],
                            start=(i == 0), stop=(i == 8))
                    if c % TG == TG - 1:
                        last.then_inc(group_done, 1)
                    if cl == CCH - 1:
                        pe.wait_ge(group_done, s * GROUPS + (g + 3))
                        pe.sem_inc(x_free, 1)

                pe.wait_ge(h_ready, s * (C // SUB) + (C // SUB + 2))

                def project(k):
                    pe.wait_ge(ht_ready, s * STEPS + (k + 1))
                    if k >= 2:
                        pe.wait_ge(o_ready, s * STEPS + (k - 1))
                    for j in range(QW):
                        last = nc.tensor.matmul(op[k % 2][:, (QW - 1 - j) * C:(QW - j) * C],
                                                ht[k % 2][:, j * P:(j + 1) * P], b["w2"][:, :], start=True, stop=True)
                    last.then_inc(o_done, 1)

                for k in range(STEPS):
                    if k >= 2:
                        pe.wait_ge(ht_ready, s * STEPS + (k - 1))
                    for j in range(QW):
                        last = nc.tensor.transpose(tp[k % 2][:, j * P:(j + 1) * P], h[:, :, k * QW + j], b["ident"][:, :])
                    last.then_inc(t_done, 1)
                    if k >= 1:
                        project(k - 1)
                project(STEPS - 1)

        @block.scalar
        def _(act):
            act.wait_ge(eps_ready, 1)
            with act.Fori(0, STRIPS) as s:
                for n in range(C // SUB):
                    act.wait_ge(h_ready, s * (C // SUB) + (n + 1))
                    for j in range(SUB // TG):
                        g = n * (SUB // TG) + j
                        act.wait_ge(group_done, s * GROUPS + (g + 3))
                        act.activation(u[n % 2][:, j * TG:(j + 1) * TG, :],
                                       cp[g % 2][:, :, 0, :, :].rearrange("p c a b -> p c (a b)"), ACT.Tanh, scale=0.5)\
                            .then_inc(tanh_done, 1)
                    act.wait_ge(h_ready, s * (C // SUB) + (n + 2))
                    act.wait_ge(u_ready, s * GROUPS + ((n + 1) * (SUB // TG) + 2))
                    act.activation(soft[:, :, :], u[n % 2][:, :, :], ACT.Abs).then_inc(soft_own, 1)
                    act.wait_ge(soft_own, s * (2 * C // SUB) + (2 * n + 1))
                    act.activation(soft[:, :, :], soft[:, :, :], ACT.Exp, scale=-1.0).then_inc(soft_own, 1)
                    act.wait_ge(soft_own, s * (2 * C // SUB) + (2 * n + 2))
                    act.activation(soft[:, :, :], soft[:, :, :], ACT.Ln, bias=1.0).then_inc(soft_ready, 1)
                for k in range(STEPS):
                    act.wait_ge(t_done, s * STEPS + (k + 1))
                    if k >= 2:
                        act.wait_ge(o_done, s * STEPS + (k - 1))
                    act.activation(ht[k % 2][:, :], tp[k % 2][:, :], ACT.Identity, scale=scan, bias=eps[:, :])\
                        .then_inc(ht_ready, 1)

        @block.vector
        def _(dve):
            dve.sem_inc(u_ready, 2)
            dve.sem_inc(h_ready, 2)
            with dve.Fori(0, STRIPS) as s:
                for n in range(C // SUB):
                    for j in range(SUB // TG):
                        g = n * (SUB // TG) + j
                        part = u[n % 2][:, j * TG:(j + 1) * TG, :]
                        dve.wait_ge(tanh_done, s * GROUPS + (g + 1))
                        dve.scalar_tensor_tensor(part, part, 1.0, cp[g % 2][:, :, 1, :, :].rearrange("p c a b -> p c (a b)"),
                                                 ALU.add, ALU.mult).then_inc(u_ready, 1)
                    dve.wait_ge(soft_ready, s * (C // SUB) + (n + 1))
                    dve.scalar_tensor_tensor(h[:, n * SUB:(n + 1) * SUB, :], u[n % 2][:, :, :], 0.0, soft[:, :, :],
                                             ALU.max, ALU.add).then_inc(h_ready, 1)
                for k in range(STEPS):
                    r = res[k % RES]
                    dve.wait_ge(res_in[k % RES], s * (STEPS // RES * 16) + (k // RES + 1) * 16)
                    dve.tensor_tensor(r[:, :, :], r[:, :, :], bcast_rows(b["bout"][:, :], QW), ALU.add).then_inc(res_own, 1)
                    dve.wait_ge(res_own, s * STEPS + (k + 1))
                    dve.wait_ge(o_done, s * STEPS + (k + 1))
                    dve.tensor_tensor(r[:, :, :].rearrange("p w c -> p (w c)"), r[:, :, :].rearrange("p w c -> p (w c)"),
                                      op[k % 2][:, :], ALU.add).then_inc(o_ready, 1)


def block_attention_then_gated_convolution(nc, x, mask, gamma, beta, wq, wk, wv, wb, wg, wo,
                                           kA, kB, gB, w2, bout, taps, out):
    d = {
        "x": x, "mask": mask, "gamma": gamma.rearrange("(c o) -> c o", o=1), "beta": beta.rearrange("(c o) -> c o", o=1),
        "wq": wq, "wk": wk, "wv": wv, "wb": wb, "wg": wg, "wo": wo, "w2": w2, "kA": kA, "bout": bout,
        "kB": kB, "gB": gB, "taps": taps, "out": out,
        "flat": nc.dram_tensor("flat_kernels", (C, 2, FLAT), F32).ap(),
        "znt": nc.dram_tensor("zn_transposed", (C, N * N), F32).ap(),
        "x1": nc.dram_tensor("x1_rows", (N, N, C), F32).ap(),
        "square": nc.dram_tensor("corner_square", (2 * TAPS - 1, 2 * TAPS - 1, C), F32).ap(),
        "x1h": nc.dram_tensor("x1_halo", (NCC, HPAD, BW, WB, CCH), F32).ap(),
    }
    with ExitStack() as ctx:
        def sb(name, shape, dt=F32):
            return ctx.enter_context(nc.sbuf_tensor(name, shape, dt))

        b = {"w2": sb("w2", [C, C]), "bout": sb("bout", [P, C]), "ident": sb("ident", [P, P])}
        b["gn_a"], b["gn_b"], b["mean0"] = sb("gn_a", [P, C]), sb("gn_b", [P, C]), sb("mean0", [P, C])
        b["corner"] = sb("corner", [TAPS * TAPS, C])
        middle = ctx.enter_context(ExitStack())
        with ExitStack() as inner:
            def sbi(name, shape, dt=F32, to=inner):
                return to.enter_context(nc.sbuf_tensor(name, shape, dt))

            b["mean_w"] = sbi("mean_w", [P, P], to=middle)
            b["acc"] = sbi("acc", [P, 2, WT * C], to=middle)
            for name in ("wq", "wk", "wv", "wg", "wo"):
                b[name] = sbi(name, [C, C])
            b["wb"] = sbi("wb", [C, HEADS])
            b["gamma"], b["beta"] = sbi("gamma", [C, 1]), sbi("beta", [C, 1])
            b["mask8"] = sbi("mask8", [P, N], U8)
            b["half"] = sbi("half", [P, N])
            b["pow"] = sbi("pow", [P, 8])
            b["nbias"] = sbi("nbias", [P, WT, HEADS, N])
            setup_stage(nc, d, b)
            stats_stage(nc, d, b)
            norm_stage(nc, d, b)
            attention_stage(nc, d, b)
        corner_stage(nc, d, b)
        middle.close()
        conv_stage(nc, d, b)


def kernel(**inputs):
    import numpy as _np
    import concourse.bacc as _bacc
    from concourse import mybir as _mybir
    from concourse.bass_utils import run_bass_kernel_spmd as _run

    def rotated(k):
        return k[:, ::-1, ::-1].reshape(C, TAPS * TAPS)

    first, second = "L0_conv_", "L1_conv_"
    gate_a, gate_b, b_kernel = (rotated(_np.asarray(inputs[second + n])) for n in ("gate_A_kernel", "gate_B_kernel", "B_kernel"))
    given = [
        ("x", inputs["x"]),
        ("mask", _np.asarray(inputs[first + "single_mask"]).reshape(-1)),
        ("gamma", inputs[first + "ln_gamma"]),
        ("beta", inputs[first + "ln_beta"]),
        ("wq", inputs[first + "Wq"]),
        ("wk", inputs[first + "Wk"]),
        ("wv", inputs[first + "Wv"]),
        ("wb", inputs[first + "Wb"]),
        ("wg", inputs[first + "Wg"]),
        ("wo", inputs[first + "Wout"]),
        ("kA", _np.asarray(inputs[second + "A_kernel"]).reshape(C, TAPS * TAPS).T),
        ("kB", b_kernel),
        ("gB", gate_b),
        ("w2", inputs[second + "W_out"]),
        ("bout", inputs[second + "b_out"]),
        ("taps", _np.stack([gate_a.T, gate_b.T, b_kernel.T])),
    ]
    nc = _bacc.Bacc("TRN2", target_bir_lowering=False, num_devices=1)
    arrays, args = {}, []
    for name, a in given:
        a = _np.ascontiguousarray(a)
        arrays[f"in_{name}_dram"] = a
        args.append(nc.dram_tensor(f"in_{name}_dram", a.shape, _mybir.dt.from_np(a.dtype), kind="ExternalInput").ap())
    args.append(nc.dram_tensor("out_dram", (1, N, N, C), F32, kind="ExternalOutput").ap())
    block_attention_then_gated_convolution(nc, *args)
    r = _run(nc, [arrays], core_ids=[0])
    return r.results[0]["out_dram"]
```

```python
from contextlib import ExitStack

import concourse.bass as bass
from concourse import mybir

F32 = mybir.dt.float32
F16 = mybir.dt.float16
U8 = mybir.dt.uint8
U32 = mybir.dt.uint32
ALU = mybir.AluOpType
ACT = mybir.ActivationFunctionType
AX = mybir.AxisListType
ds = bass.ds

P = 128
C = 128
N = 256
HEADS, DH = 4, 32
G, GC = 32, 4
TAPS = 7
R = TAPS // 2
GN_EPS, LN_EPS, SP_EPS = 1e-5, 1e-5, 1e-6
NEG = -1e9
WT = N // P

BH, BW = 8, 16
assert BH * BW == P
HB, WB = N // BH, N // BW
PITCH = BW + 2 * R
WROWS = BH + 2 * R
WIN = WROWS * PITCH
TAPROWS = TAPS * 2 * PITCH
FLAT = TAPROWS + BW
XSCALE = 16.0
KTOP = 256.0
EXPONENT = 0x7F800000
CCH = 32
NCC = C // CCH
SROWS = 8
STRIPS = HB // SROWS
HPAD = N + 2 * BH


class Chain:

    def __init__(self, eng, sem, base=0):
        self.eng, self.sem, self.base, self.n = eng, sem, base, 0

    def link(self, ins):
        self.n += 1
        ins.then_inc(self.sem, 1)

    def wait(self):
        self.eng.wait_ge(self.sem, self.base + self.n)

    def step(self, ins):
        self.link(ins)
        self.wait()


def hold(eng, sem, value, passed):
    eng.wait_ge(sem, value)
    eng.sem_inc(passed, 1)


def bcast_rows(t, n):
    return t.unsqueeze(1).to_broadcast([t.shape[0], n, t.shape[1]])


def pair(t, step):
    return bass.AP(t.tensor, t.offset, [list(x) for x in t.ap[:-1]] + [[step, 2], list(t.ap[-1])])


def setup_stage(nc, d, b):
    with ExitStack() as ctx:
        def sem(name):
            return ctx.enter_context(nc.semaphore(name))

        def sb(name, shape, dt=F32):
            return ctx.enter_context(nc.sbuf_tensor(name, shape, dt))

        raw = sb("su_raw", [C, 2, TAPS * TAPS])
        scaled = sb("su_scaled", [C, 2, TAPS * TAPS])
        flat = sb("su_flat", [C, 2, FLAT], F16)
        peak = sb("su_peak", [C, 2])
        peaks = sb("su_peaks", [P, C, 2])
        top = sb("su_top", [P, 2])
        power = sb("su_power", [P, 2])
        inv = sb("su_inv", [P, 2])
        w_in, pool_chain, chain = sem("w_in"), sem("su_pool"), sem("su_chain")
        raw_in, peak_ready, peaks_in, flat_ready, flat_out = (sem(f"su_{x}") for x in
                                                              ("raw", "peak", "peaks", "flat", "flato"))
        block = ctx.enter_context(nc.Block())

        @block.sync
        def _(sp):
            for k, name in enumerate(("gB", "kB")):
                sp.dma_start(raw[:, k, :], d[name]).then_inc(raw_in, 16)
            for name in ("wq", "wk", "wv", "wg", "wo", "w2", "wb"):
                sp.dma_start(b[name][:, :], d[name]).then_inc(w_in, 16)
            sp.dma_start(b["gamma"][:, :], d["gamma"]).then_inc(w_in, 16)
            sp.dma_start(b["beta"][:, :], d["beta"]).then_inc(w_in, 16)
            sp.dma_start(b["bout"][:, :], d["bout"].partition_broadcast(P)).then_inc(w_in, 16)
            sp.dma_start(b["mask8"][:, :], d["mask"].partition_broadcast(P)).then_inc(w_in, 16)
            sp.wait_ge(w_in, 16 * 11)
            sp.wait_ge(peak_ready, 1)
            sp.dma_start(d["peaks"], peak[:, :]).then_inc(peaks_in, 16)
            sp.wait_ge(peaks_in, 16)
            sp.dma_start(peaks[:, :, :].rearrange("p c k -> p (c k)"),
                         d["peaks"].rearrange("c k -> (c k)").partition_broadcast(P)).then_inc(peaks_in, 16)
            sp.wait_ge(flat_ready, 5)
            sp.dma_start(d["flat"], flat[:, :, :]).then_inc(flat_out, 16)
            sp.wait_ge(flat_out, 16)

        @block.vector
        def _(dve):
            ch = Chain(dve, chain)
            dve.memset(flat[:, :, :], 0.0).then_inc(flat_ready, 1)
            dve.wait_ge(raw_in, 32)
            ch.step(dve.scalar_tensor_tensor(scaled[:, :, :], raw[:, :, :], -1.0, raw[:, :, :], ALU.mult, ALU.max))
            dve.tensor_reduce(peak[:, :], scaled[:, :, :], AX.X, ALU.max).then_inc(peak_ready, 1)
            dve.wait_ge(peaks_in, 32)
            ch.step(dve.tensor_reduce(top[:, :], peaks[:, :, :].rearrange("p c k -> p k c"), AX.X, ALU.max))
            ch.step(dve.tensor_scalar(top[:, :], top[:, :], 1e-30, None, ALU.max))
            ch.step(dve.tensor_scalar(power[:, :].bitcast(U32), top[:, :].bitcast(U32), EXPONENT, None, ALU.bitwise_and))
            ch.step(dve.reciprocal(inv[:, :], power[:, :]))
            ch.step(dve.tensor_scalar(b["kscale"][:, :], power[:, :], 1.0 / (XSCALE * KTOP), None, ALU.mult))
            for k in range(2):
                ch.link(dve.tensor_scalar(scaled[:, k, :], raw[:, k, :], inv[:, k:k + 1], KTOP, ALU.mult, ALU.mult))
            dve.wait_ge(chain, ch.n)
            dve.wait_ge(flat_ready, 1)
            high, low = (flat[:, h, 0:TAPROWS].rearrange("p (t k u) -> p t k u", k=2, u=PITCH)[:, :, :, PITCH - TAPS:PITCH]
                         for h in range(2))
            for k in range(2):
                taps = scaled[:, k, :].rearrange("p (t u) -> p t u", u=TAPS)
                dve.tensor_copy(high[:, :, k, :], taps).then_inc(flat_ready, 1)
                dve.wait_ge(flat_ready, 2 + 2 * k)
                dve.tensor_tensor(low[:, :, k, :], taps, high[:, :, k, :],
                                  ALU.subtract).then_inc(flat_ready, 1)

        @block.gpsimd
        def _(pool):
            ch = Chain(pool, pool_chain)
            ch.link(pool.memset(b["ident"][:, :], 0.0))
            ch.link(pool.memset(b["mean_w"][:, :], 1.0 / P))
            ch.link(pool.memset(b["half"][:, :], 0.5))
            ch.link(pool.memset(b["pow"][:, :], -0.5))
            ch.step(pool.memset(b["acc"][:, :, :], 0.0))
            ch.step(pool.affine_select(out=b["ident"][:, :], in_=b["ident"][:, :], compare_op=ALU.not_equal,
                                       fill=1.0, base=0, pattern=[[-1, P]], channel_multiplier=1))


def stats_stage(nc, d, b):
    TOK = N * N // P
    TT = 64
    NT = TOK // TT
    xs = d["x"].rearrange("o h w c -> (o h w c)").rearrange("(p t c) -> p t c", p=P, c=C)
    with ExitStack() as ctx:
        def sem(name):
            return ctx.enter_context(nc.semaphore(name))

        def sb(name, shape):
            return ctx.enter_context(nc.sbuf_tensor(name, shape, F32))

        xt = [sb(f"st_x{s}", [P, TT, C]) for s in range(2)]
        st = sb("st_st", [P, G, NT, 6])
        mv = sb("st_mv", [P, G, 2])
        me = sb("st_me", [P, 2, G])
        tot = sb("st_tot", [P, 2, G])
        rs = sb("st_rs", [P, 4, G])
        ps = ctx.enter_context(nc.psum_tensor("st_ps", [P, 2, G], F32))
        loaded = [sem(f"st_loaded{s}") for s in range(2)]
        used, chain, sp_passed = sem("st_used"), sem("st_chain"), sem("st_spp")
        me_ready, sum_ready, var_ready, std_ready = sem("st_me"), sem("st_sum"), sem("st_var"), sem("st_std")
        block = ctx.enter_context(nc.Block())

        @block.sync
        def _(sp):
            for s in range(2):
                sp.dma_start(xt[s][:, :, :], xs[:, s * TT:(s + 1) * TT, :]).then_inc(loaded[s], 16)
            with sp.Fori(0, NT // 2 - 1) as n:
                for s in range(2):
                    hold(sp, used, n * 2 + s + 1, sp_passed)
                    sp.dma_start(xt[s][:, :, :], xs[:, ds(n * (2 * TT) + (2 + s) * TT, TT), :])\
                        .then_inc(loaded[s], 16)

        @block.vector
        def _(dve):
            with dve.Fori(0, NT // 2) as n:
                for s in range(2):
                    dve.wait_ge(loaded[s], n * 16 + 16)
                    for g in range(G):
                        last = dve.bn_stats(st[:, g, ds(n * 2 + s, 1), :].rearrange("p a b -> p (a b)"),
                                            xt[s][:, :, g * GC:(g + 1) * GC])
                    last.then_inc(used, 1)
            dve.wait_ge(used, NT)
            ch = Chain(dve, chain)
            for g in range(G):
                last = dve.bn_aggr(mv[:, g, :], st[:, g, :, :].rearrange("p a b -> p (a b)"))
            ch.step(last)
            ch.link(dve.tensor_copy(me[:, 0, :], mv[:, :, 0]))
            ch.step(dve.tensor_tensor(me[:, 1, :], mv[:, :, 0], mv[:, :, 0], ALU.mult))
            dve.tensor_tensor(me[:, 1, :], me[:, 1, :], mv[:, :, 1], ALU.add).then_inc(me_ready, 1)
            dve.wait_ge(sum_ready, 1)
            ch.step(dve.tensor_copy(tot[:, :, :], ps[:, :, :]))
            ch.step(dve.tensor_tensor(rs[:, 0, :], tot[:, 0, :], tot[:, 0, :], ALU.mult))
            ch.step(dve.tensor_tensor(rs[:, 1, :], tot[:, 1, :], rs[:, 0, :], ALU.subtract))
            dve.tensor_scalar(rs[:, 2, :], rs[:, 1, :], GN_EPS, None, ALU.add).then_inc(var_ready, 1)
            dve.wait_ge(std_ready, 1)
            ch.step(dve.reciprocal(rs[:, 0, :], rs[:, 3, :]))
            ch.step(dve.tensor_tensor(rs[:, 1, :], tot[:, 0, :], rs[:, 0, :], ALU.mult))
            for t, src, by in ((b["gn_a"], rs[:, 0, :], 1.0), (b["gn_b"], rs[:, 1, :], -1.0), (b["mean0"], tot[:, 0, :], 1.0)):
                ch.link(dve.tensor_scalar(t[:, :].rearrange("p (g c) -> p g c", c=GC),
                                          src.unsqueeze(2).to_broadcast([P, G, GC]), by, None, ALU.mult))

        @block.tensor
        def _(pe):
            pe.wait_ge(me_ready, 1)
            nc.tensor.matmul(ps[:, :, :].rearrange("p a g -> p (a g)"), b["mean_w"][:, :],
                             me[:, :, :].rearrange("p a g -> p (a g)"), start=True, stop=True).then_inc(sum_ready, 1)

        @block.scalar
        def _(act):
            act.wait_ge(var_ready, 1)
            act.activation(rs[:, 3, :], rs[:, 2, :], ACT.Sqrt).then_inc(std_ready, 1)


def norm_stage(nc, d, b):
    RQ = 4
    T = RQ * WT
    NQ = N // RQ
    xv = d["x"].rearrange("o r (t w) c -> w (o r t) c", t=WT)
    with ExitStack() as ctx:
        def sem(name):
            return ctx.enter_context(nc.semaphore(name))

        def sb(name, shape):
            return ctx.enter_context(nc.sbuf_tensor(name, shape, F32))

        xt = [sb(f"no_x{s}", [P, T, C]) for s in range(3)]
        xn = [sb(f"no_n{s}", [P, T, C]) for s in range(2)]
        st = sb("no_st", [P, 2, T, 6])
        mv = sb("no_mv", [P, 2, T, 2])
        ve = sb("no_ve", [P, 2, T])
        rstd = sb("no_rstd", [P, 2, T])
        zt = [sb(f"no_z{s}", [P, T * P]) for s in range(2)]
        bias_t = sb("no_bt", [P, WT, HEADS, N])
        bias_q = sb("no_bq", [P, WT, HEADS, N])
        negm = sb("no_negm", [P, N])
        zp = [ctx.enter_context(nc.psum_tensor(f"no_zp{k}", [P, 512], F32)) for k in range(4)]
        bp = [ctx.enter_context(nc.psum_tensor(f"no_bp{k}", [P, RQ, WT, HEADS], F32)) for k in range(2)]
        loaded = [sem(f"no_loaded{s}") for s in range(2)]
        stored = [sem(f"no_stored{s}") for s in range(2)]
        scaled, centred, mv_ready, rstd_ready, normed = (sem(f"no_{x}") for x in
                                                         ("scaled", "centred", "mv", "rstd", "normed"))
        z_psum, z_ready, b_psum, b_read = (sem(f"no_{x}") for x in ("zpsum", "zready", "bpsum", "bread"))
        pool_own, dve_own = sem("no_pool"), sem("no_dve")
        tr_ready, neg_ready = sem("no_tr"), sem("no_neg")
        tr_read = sem("no_trread")
        sp_passed, dve_passed, pool_passed = sem("no_spp"), sem("no_dvep"), sem("no_poolp")

        def pool_rstd(pool, n, s):
            hold(pool, mv_ready, n + 1, pool_passed)
            pool.tensor_scalar(ve[:, s, :], mv[:, s, :, 1], LN_EPS, None, ALU.add).then_inc(pool_own, 1)
            pool.wait_ge(pool_own, n + 1)
            pool.tensor_tensor(rstd[:, s, :], ve[:, s, :], b["pow"][:, 0:T], ALU.pow).then_inc(rstd_ready, 1)

        def dve_stats(dve, n, s):
            dve.wait_ge(scaled, n + 1)
            dve.tensor_tensor(xn[s][:, :, :], xn[s][:, :, :], bcast_rows(b["gn_b"][:, :], T), ALU.add)\
                .then_inc(centred, 1)
            dve.wait_ge(centred, n + 1)
            for t in range(T):
                last = dve.bn_stats(st[:, s, t, :], xn[s][:, t, :])
            last.then_inc(dve_own, 1)
            hold(dve, dve_own, n + 1, dve_passed)
            for t in range(T):
                last = dve.bn_aggr(mv[:, s, t, :], st[:, s, t, :])
            last.then_inc(mv_ready, 1)

        def dve_normalise(dve, n, s):
            dve.wait_ge(rstd_ready, n + 1)
            for t in range(T):
                last = dve.tensor_scalar(xn[s][:, t, :], xn[s][:, t, :], mv[:, s, t, 0:1], rstd[:, s, t:t + 1],
                                         ALU.subtract, ALU.mult)
            last.then_inc(normed, 1)

        def dve_bias(dve, n, s):
            dve.wait_ge(b_psum, n + 1)
            for t in range(WT):
                last = dve.tensor_scalar(bias_t[:, t, :, ds(n * RQ, RQ)].rearrange("p h r -> p r h"),
                                         bp[s][:, :, t, :], -1.0, None, ALU.mult)
            last.then_inc(b_read, 1)

        def pe_transpose(pe, n, s):
            pe.wait_ge(normed, n + 1)
            for k in range(2):
                for t in range(4):
                    last = nc.tensor.transpose(zp[2 * s + k][:, t * P:(t + 1) * P], xn[s][:, 4 * k + t, :], b["ident"][:, :])
                last.then_inc(z_psum, 1)

        def pe_bias(pe, n, s):
            pe.wait_ge(z_ready, n * 2 + 2)
            for t in range(T):
                last = nc.tensor.matmul(bp[s][:, t // WT, t % WT, :], zt[s][:, t * P:(t + 1) * P], b["wb"][:, :],
                                        start=True, stop=True)
            last.then_inc(b_psum, 1)

        block = ctx.enter_context(nc.Block())

        @block.sync
        def _(sp):
            for s in range(2):
                sp.dma_start(xt[s][:, :, :], xv[:, s * T:(s + 1) * T, :]).then_inc(loaded[s], 16)
            with sp.Fori(0, NQ // 2 - 1) as n:
                for s in range(2):
                    hold(sp, scaled, n * 2 + s + 1, sp_passed)
                    sp.dma_start(xt[s][:, :, :], xv[:, ds(n * (2 * T) + (2 + s) * T, T), :]).then_inc(loaded[s], 16)

        @block.gpsimd
        def _(pool):
            def scale(n, s, half, first):
                pool.wait_ge(loaded[s], half * 16 + 16)
                if not first:
                    pool.wait_ge(z_psum, n * 2 - 2)
                pool.tensor_tensor(xn[s][:, :, :], xt[s][:, :, :], bcast_rows(b["gn_a"][:, :], T), ALU.mult)\
                    .then_inc(scaled, 1)

            scale(0, 0, 0, True)
            scale(1, 1, 0, True)
            with pool.Fori(0, NQ // 2 - 1) as m:
                for s in range(2):
                    pool_rstd(pool, m * 2 + s, s)
                    scale(m * 2 + (s + 2), s, m + 1, False)
            for s in range(2):
                pool_rstd(pool, NQ - 2 + s, s)

        @block.vector
        def _(dve):
            dve_stats(dve, 0, 0)
            dve_stats(dve, 1, 1)
            dve_normalise(dve, 0, 0)
            with dve.Fori(0, NQ // 2 - 1) as m:
                for s in range(2):
                    dve_stats(dve, m * 2 + (s + 2), s)
                    dve_normalise(dve, m * 2 + (s + 1), 1 - s)
                    dve_bias(dve, m * 2 + s, s)
            dve_normalise(dve, NQ - 1, 1)
            dve_bias(dve, NQ - 2, 0)
            dve_bias(dve, NQ - 1, 1)
            dve.tensor_scalar(negm[:, :], b["mask8"][:, :], NEG, -NEG, ALU.mult, ALU.add).then_inc(neg_ready, 1)
            dve.wait_ge(b_read, NQ)
            for k in range(WT):
                for h in range(HEADS):
                    dve.tensor_copy(bias_q[:, k, h, :].rearrange("p (t m b) -> p t m b", t=WT, b=WB),
                                    bias_t[:, k, h, :].rearrange("p (b t m) -> p t m b", t=WT, b=WB)).then_inc(neg_ready, 1)
            dve.wait_ge(neg_ready, 1)
            for h in range(HEADS):
                dve.wait_ge(tr_ready, h + 1)
                for j in range(WT):
                    last = dve.tensor_tensor(b["nbias"][:, j, h, :], zp[h % 2][:, j * N:(j + 1) * N], negm[:, :], ALU.add)
                last.then_inc(tr_read, 1)

        @block.tensor
        def _(pe):
            pe_transpose(pe, 0, 0)
            pe_transpose(pe, 1, 1)
            pe_bias(pe, 0, 0)
            pe_bias(pe, 1, 1)
            with pe.Fori(1, NQ // 2) as m:
                for s in range(2):
                    pe.wait_ge(z_ready, m * 4 + (2 * s - 2))
                    pe_transpose(pe, m * 2 + s, s)
                    pe.wait_ge(b_read, m * 2 + (s - 1))
                    pe_bias(pe, m * 2 + s, s)
            pe.wait_ge(neg_ready, 1 + WT * HEADS)
            for h in range(HEADS):
                if h >= 2:
                    pe.wait_ge(tr_read, h - 1)
                for j in range(WT):
                    for k in range(WT):
                        last = nc.tensor.transpose(zp[h % 2][:, j * N + k * P:j * N + (k + 1) * P],
                                                   bias_q[:, k, h, j * P:(j + 1) * P], b["ident"][:, :])
                last.then_inc(tr_ready, 1)

        @block.scalar
        def _(act):
            def copy_out(n, s, m):
                for k in range(2):
                    act.wait_ge(z_psum, n * 2 + k + 1)
                    act.activation(zt[s][:, k * 512:(k + 1) * 512], zp[2 * s + k][:, :], ACT.Identity,
                                   bias=b["beta"][:, :], scale=b["gamma"][:, :]).then_inc(z_ready, 1)
                act.wait_ge(z_ready, n * 2 + 2)
                act.dma_start(d["znt"][:, ds(n * (T * P), T * P)], zt[s][:, :]).then_inc(stored[s], 16)

            copy_out(0, 0, 0)
            copy_out(1, 1, 0)
            with act.Fori(1, NQ // 2) as m:
                for s in range(2):
                    act.wait_ge(stored[s], m * 16)
                    act.wait_ge(b_psum, m * 2 + (s - 1))
                    copy_out(m * 2 + s, s, m)
            for s in range(2):
                act.wait_ge(stored[s], NQ // 2 * 16)


def attention_stage(nc, d, b):
    xv = [d["x"][0].rearrange("r (b t m) c -> t r m b c", t=WT, m=BW // WT)[t] for t in range(WT)]
    nat = [d["x1"].rearrange("r (b t m) c -> t r m b c", t=WT, m=BW // WT)[t] for t in range(WT)]

    def row_of(v, r):
        return v[r] if isinstance(r, int) else v[ds(r, 1)].squeeze(0)

    halo = [d["x1h"].rearrange("q r m b c -> r (m b) q c")[:, t * P:(t + 1) * P, :, :] for t in range(WT)]
    QSCALE = -1.0 / float(DH) ** 0.5
    with ExitStack() as ctx:
        def sem(name):
            return ctx.enter_context(nc.semaphore(name))

        def sb(name, shape):
            return ctx.enter_context(nc.sbuf_tensor(name, shape, F32))

        def pb(name, shape):
            return ctx.enter_context(nc.psum_tensor(name, shape, F32))

        znt = [sb(f"at_znt{s}", [P, N]) for s in range(2)]
        xin = [sb(f"at_x{s}", [P, WT, C]) for s in range(2)]
        qt = [sb(f"at_q{s}", [P, N]) for s in range(2)]
        kt = [sb(f"at_k{s}", [P, N]) for s in range(2)]
        gt = [sb(f"at_gate{s}", [P, N]) for s in range(3)]
        v = [sb(f"at_v{s}", [P, WT, C]) for s in range(3)]
        probs = [sb(f"at_p{s}", [P, HEADS, WT, N]) for s in range(2)]
        top = [sb(f"at_top{s}", [P, WT, HEADS]) for s in range(2)]
        tot = [sb(f"at_tot{s}", [P, WT, HEADS]) for s in range(2)]
        rec = [sb(f"at_rec{s}", [P, WT * HEADS]) for s in range(2)]
        rb = [sb(f"at_rb{s}", [P, WT * HEADS, DH]) for s in range(2)]
        pt = [sb(f"at_pt{k}", [P, WT, N]) for k in range(2)]
        g1 = sb("at_g1", [P, N])
        og = [sb(f"at_og{s}", [P, N]) for s in range(2)]
        x1 = [sb(f"at_x1{s}", [P, WT, C]) for s in range(2)]
        dev = sb("at_dev", [P, WT, C])
        sq = sb("at_sq", [P, WT, C])

        s_ps = [pb(f"at_s{k}", [P, WT, N]) for k in range(2)]
        pt_ps = [pb(f"at_ptp{k}", [P, WT, N]) for k in range(2)]
        qg_ps, kv_ps, or_ps = pb("at_qg", [P, 2, N]), pb("at_kv", [P, 2, N]), pb("at_or", [P, 2, N])
        w_ps = pb("at_w", [P, 2, N])

        znt_in = [sem(f"at_znt_in{s}") for s in range(2)]
        x_in = [sem(f"at_x_in{s}") for s in range(2)]
        stored = [sem(f"at_stored{s}") for s in range(2)]
        qg_done, kv_done = sem("at_qg_done"), sem("at_kv_done")
        q_ready, k_ready, g_ready, v_ready = (sem(f"at_{x}_ready") for x in "qkgv")
        s_done, s_read, p_ready = sem("at_s_done"), sem("at_s_read"), sem("at_p_ready")
        pt_done, pt_even, pt_odd, o_done = sem("at_pt_done"), sem("at_pt_even"), sem("at_pt_odd"), sem("at_o_done")
        rec_ready, rb_ready, r_done, og_ready = sem("at_rec"), sem("at_rb"), sem("at_r_done"), sem("at_og")
        g1_ready = sem("at_g1_ready")
        w_done, x1_ready, acc_done, pool_own = sem("at_w_done"), sem("at_x1_ready"), sem("at_acc"), sem("at_pool")
        sp_passed, dve_passed = sem("at_spp"), sem("at_dvep")
        STORES = 4

        block = ctx.enter_context(nc.Block())

        def rows(eng, step):
            lead = 4
            body = 6
            turns = (N - 1 - lead) // body
            for i in range(lead):
                step(i, i)
            with eng.Fori(0, turns) as m:
                for u in range(body):
                    step(m * body + (lead + u), lead + u)
            for i in range(lead + turns * body, N + 2):
                step(i, i)

        def full(i):
            return isinstance(i, int)

        @block.sync
        def _(sp):
            sp.dma_start(znt[0][:, :], d["znt"][:, 0:N]).then_inc(znt_in[0], 16)
            sp.dma_start(znt[1][:, :], d["znt"][:, N:2 * N]).then_inc(znt_in[1], 16)
            for t in range(2):
                for j in range(WT):
                    sp.dma_start(xin[t][:, j, :], row_of(xv[j], t)).then_inc(x_in[t], 16)

            def store(r, u):
                s = u % 2
                hold(sp, x1_ready, r + 1, sp_passed)
                for t in range(WT):
                    sp.dma_start(row_of(nat[t], r), x1[s][:, t, :]).then_inc(stored[s], 16)
                    sp.dma_start(row_of(halo[t], r + BH), x1[s][:, t, :].rearrange("p (q c) -> p q c", c=CCH))\
                        .then_inc(stored[s], 16)

            def step(i, u):
                if not full(i) or i + 2 < N:
                    hold(sp, kv_done, i + 1, sp_passed)
                    sp.dma_start(znt[u % 2][:, :], d["znt"][:, ds(i * N + 2 * N, N)]).then_inc(znt_in[u % 2], 16)
                if u >= 2:
                    store(i - 2, u)
                    if not full(i) or i < N:
                        for j in range(WT):
                            sp.dma_start(xin[u % 2][:, j, :], row_of(xv[j], i)).then_inc(x_in[u % 2], 16)

            rows(sp, step)
            for s in range(2):
                sp.wait_ge(stored[s], N // 2 * STORES * 16)

        @block.tensor
        def _(pe):
            def project(r, u):
                s = u % 2
                pe.wait_ge(znt_in[s], (r + (2 - s)) * 8)
                queries = znt[s][:, :].rearrange("p (b t m) -> p t m b", t=WT, m=BW // WT)
                if u >= 1:
                    pe.wait_ge(g_ready, r)
                nc.tensor.matmul(qg_ps[:, 0, :], b["wq"][:, :], queries, start=True, stop=True)
                nc.tensor.matmul(qg_ps[:, 1, :], b["wg"][:, :], queries, start=True, stop=True).then_inc(qg_done, 1)
                if u >= 1:
                    pe.wait_ge(v_ready, r)
                nc.tensor.matmul(kv_ps[:, 0, :], b["wk"][:, :], znt[s][:, :], start=True, stop=True)
                for t in range(WT):
                    last = nc.tensor.matmul(kv_ps[:, 1, t * P:(t + 1) * P], znt[s][:, t * P:(t + 1) * P], b["wv"][:, :],
                                            start=True, stop=True)
                last.then_inc(kv_done, 1)

            def scores(r, u, h):
                s = u % 2
                if h == 0:
                    pe.wait_ge(q_ready, r + 1)
                    pe.wait_ge(k_ready, r + 1)
                if u >= 1 or h >= 2:
                    pe.wait_ge(s_read, r * HEADS + (h - 1))
                lo = h * DH
                for j in range(WT):
                    last = nc.tensor.matmul(s_ps[h % 2][:, j, :], qt[s][lo:lo + DH, j * P:(j + 1) * P], kt[s][lo:lo + DH, :],
                                            start=True, stop=True)
                last.then_inc(s_done, 1)

            def transposes(r, u, h):
                s = u % 2
                pe.wait_ge(p_ready, r * HEADS + (h + 1))
                if u >= 1 or h >= 2:
                    if h % 2 == 0:
                        pe.wait_ge(pt_even, r * 2 + h // 2)
                    else:
                        pe.wait_ge(pt_odd, r * 2 + h // 2)
                for k in range(WT):
                    for j in range(WT):
                        last = nc.tensor.transpose(pt_ps[h % 2][:, k, j * P:(j + 1) * P],
                                                   probs[s][:, h, j, k * P:(k + 1) * P], b["ident"][:, :])
                last.then_inc(pt_done, 1)

            def values(r, u, h):
                if h == 0:
                    pe.wait_ge(v_ready, r + 1)
                    if u >= 1:
                        pe.wait_ge(og_ready, r)
                if h % 2 == 0:
                    pe.wait_ge(pt_even, r * 2 + (h // 2 + 1))
                else:
                    pe.wait_ge(pt_odd, r * 2 + (h // 2 + 1))
                lo = h * DH
                for k in range(WT):
                    last = nc.tensor.matmul(or_ps[lo:lo + DH, 0, :], v[u % 3][:, k, lo:lo + DH], pt[h % 2][:, k, :],
                                            start=(k == 0), stop=(k == WT - 1), tile_position=(0, lo))
                last.then_inc(o_done, 1)

            def sums(r, u):
                pe.wait_ge(rb_ready, r + 1)
                for j in range(WT):
                    last = nc.tensor.transpose(or_ps[:, 1, j * P:(j + 1) * P],
                                               rb[u % 2][:, j * HEADS:(j + 1) * HEADS, :].rearrange("p h c -> p (h c)"),
                                               b["ident"][:, :])
                last.then_inc(r_done, 1)

            def output(r, u):
                pe.wait_ge(og_ready, r + 1)
                if u >= 1:
                    pe.wait_ge(x1_ready, r)
                for j in range(WT):
                    last = nc.tensor.matmul(w_ps[:, 0, j * P:(j + 1) * P], og[u % 2][:, j * P:(j + 1) * P], b["wo"][:, :],
                                            start=True, stop=True)
                last.then_inc(w_done, 1)

            project(0, 0)

            def step(i, u):
                now = not full(i) or i < N
                back = u >= 1 and (not full(i) or i - 1 < N)
                for h in range(HEADS):
                    if now:
                        scores(i, u, h)
                    if back:
                        transposes(i - 1, u - 1, h)
                        if h >= 1:
                            values(i - 1, u - 1, h - 1)
                    if h == 2:
                        if not full(i) or i + 1 < N:
                            project(i + 1, u + 1)
                        if u >= 2:
                            output(i - 2, u - 2)
                if back:
                    values(i - 1, u - 1, HEADS - 1)
                    sums(i - 1, u - 1)

            rows(pe, step)

        @block.vector
        def _(dve):
            def key_value(r, u):
                dve.wait_ge(kv_done, r + 1)
                if u >= 2:
                    dve.wait_ge(s_done, (r - 1) * HEADS)
                dve.tensor_copy(kt[u % 2][:, :], kv_ps[:, 0, :]).then_inc(k_ready, 1)
                if u >= 3:
                    dve.wait_ge(o_done, (r - 2) * HEADS)
                dve.tensor_copy(v[u % 3][:, :, :].rearrange("p t c -> p (t c)"), kv_ps[:, 1, :]).then_inc(v_ready, 1)

            def bias_max(r, u, h):
                if u >= 2:
                    dve.wait_ge(pt_done, r * HEADS + (h + 1 - 2 * HEADS))
                hold(dve, s_done, r * HEADS + (h + 1), dve_passed)
                for j in range(WT):
                    last = dve.tensor_tensor_reduce(out=probs[u % 2][:, h, j, :], in0=s_ps[h % 2][:, j, :],
                                                    in1=b["nbias"][:, j, h, :], scale=1.0, scalar=3.0e38,
                                                    op0=ALU.add, op1=ALU.min, accum_out=top[u % 2][:, j, h:h + 1])
                last.then_inc(s_read, 1)

            def copy_pt(r, u, h):
                dve.wait_ge(pt_done, r * HEADS + (h + 1))
                if u >= 1 or h >= 2:
                    dve.wait_ge(o_done, r * HEADS + (h - 1))
                dve.tensor_copy(pt[h % 2][:, :, :], pt_ps[h % 2][:, :, :]).then_inc(pt_odd, 1)

            def reciprocals(r, u):
                dve.wait_ge(p_ready, r * HEADS + HEADS)
                if u >= 2:
                    dve.wait_ge(rb_ready, r - 1)
                dve.reciprocal(rec[u % 2][:, :], tot[u % 2][:, :, :].rearrange("p t h -> p (t h)")).then_inc(rec_ready, 1)

            def gate(r, u):
                dve.wait_ge(r_done, r + 1)
                dve.wait_ge(g_ready, r + 1)
                dve.scalar_tensor_tensor(g1[:, :], gt[u % 3][:, :], 1.0, or_ps[:, 1, :], ALU.add, ALU.mult)\
                    .then_inc(g1_ready, 1)
                dve.wait_ge(g1_ready, r + 1)
                dve.wait_ge(o_done, r * HEADS + HEADS)
                if u >= 2:
                    dve.wait_ge(w_done, r - 1)
                dve.tensor_tensor(og[u % 2][:, :], g1[:, :], or_ps[:, 0, :], ALU.mult).then_inc(og_ready, 1)

            def residual(r, u):
                s = u % 2
                dve.wait_ge(w_done, r + 1)
                dve.wait_ge(x_in[s], (r + (2 - s)) * 16)
                if u >= 2:
                    dve.wait_ge(stored[s], (r - s) * (8 * STORES))
                    dve.wait_ge(acc_done, r - 1)
                dve.tensor_tensor(x1[s][:, :, :].rearrange("p t c -> p (t c)"), w_ps[:, 0, :],
                                  xin[s][:, :, :].rearrange("p t c -> p (t c)"), ALU.add).then_inc(x1_ready, 1)

            key_value(0, 0)

            def step(i, u):
                now = not full(i) or i < N
                back = u >= 1 and (not full(i) or i - 1 < N)
                if back:
                    reciprocals(i - 1, u - 1)
                for h in range(HEADS):
                    if now:
                        bias_max(i, u, h)
                    if back and h % 2:
                        copy_pt(i - 1, u - 1, h)
                    if h == 2:
                        if not full(i) or i + 1 < N:
                            key_value(i + 1, u + 1)
                        if u >= 2:
                            residual(i - 2, u - 2)
                if back:
                    gate(i - 1, u - 1)

            rows(dve, step)

        @block.scalar
        def _(act):
            def query_gate(r, u):
                act.wait_ge(qg_done, r + 1)
                if u >= 2:
                    act.wait_ge(s_done, (r - 1) * HEADS)
                act.activation(qt[u % 2][:, :], qg_ps[:, 0, :], ACT.Copy, scale=QSCALE).then_inc(q_ready, 1)
                if u >= 3:
                    act.wait_ge(g1_ready, r - 2)
                act.activation(gt[u % 3][:, :], qg_ps[:, 1, :], ACT.Tanh, scale=0.5).then_inc(g_ready, 1)

            def exponentials(r, u, h):
                act.wait_ge(s_read, r * HEADS + (h + 1))
                if u >= 2 and h == 0:
                    act.wait_ge(rec_ready, r - 1)
                for j in range(WT):
                    row = probs[u % 2][:, h, j, :]
                    last = act.activation(row, row, ACT.Exp, scale=-1.0, bias=top[u % 2][:, j, h:h + 1],
                                          accum_out=tot[u % 2][:, j, h:h + 1])
                last.then_inc(p_ready, 1)

            def copy_pt(r, u, h):
                act.wait_ge(pt_done, r * HEADS + (h + 1))
                if u >= 1 or h >= 2:
                    act.wait_ge(o_done, r * HEADS + (h - 1))
                act.activation(pt[h % 2][:, :, :], pt_ps[h % 2][:, :, :], ACT.Copy).then_inc(pt_even, 1)

            query_gate(0, 0)

            def step(i, u):
                now = not full(i) or i < N
                back = u >= 1 and (not full(i) or i - 1 < N)
                for h in range(HEADS):
                    if back and h % 2 == 0:
                        copy_pt(i - 1, u - 1, h)
                    if now:
                        exponentials(i, u, h)
                    if h == 2 and (not full(i) or i + 1 < N):
                        query_gate(i + 1, u + 1)

            rows(act, step)

        @block.gpsimd
        def _(pool):
            def spread(r, u):
                pool.wait_ge(rec_ready, r + 1)
                if u >= 2:
                    pool.wait_ge(r_done, r - 1)
                pool.tensor_tensor(rb[u % 2][:, :, :], rec[u % 2][:, :].unsqueeze(2).to_broadcast([P, WT * HEADS, DH]),
                                   b["half"][:, :].rearrange("p (a c) -> p a c", c=DH), ALU.mult).then_inc(rb_ready, 1)

            def accumulate(r, u):
                s = u % 2
                pool.wait_ge(x1_ready, r + 1)
                pool.tensor_tensor(dev[:, :, :], x1[s][:, :, :], bcast_rows(b["mean0"][:, :], WT), ALU.subtract)\
                    .then_inc(acc_done, 1)
                pool.wait_ge(acc_done, r + 1)
                pool.tensor_tensor(sq[:, :, :], dev[:, :, :], dev[:, :, :], ALU.mult).then_inc(pool_own, 1)
                pool.tensor_tensor(b["acc"][:, 0, :], b["acc"][:, 0, :], dev[:, :, :].rearrange("p t c -> p (t c)"), ALU.add)\
                    .then_inc(pool_own, 1)
                pool.wait_ge(pool_own, r * 3 + 2)
                pool.tensor_tensor(b["acc"][:, 1, :], b["acc"][:, 1, :], sq[:, :, :].rearrange("p t c -> p (t c)"), ALU.add)\
                    .then_inc(pool_own, 1)
                pool.wait_ge(pool_own, r * 3 + 3)

            def step(i, u):
                if u >= 1 and (not full(i) or i - 1 < N):
                    spread(i - 1, u - 1)
                if u >= 2:
                    accumulate(i - 2, u - 2)

            rows(pool, step)


def corner_stage(nc, d, b):
    K2 = TAPS * TAPS
    S = 2 * TAPS - 1
    SC = 1.0 / (N * N // P * GC)
    with ExitStack() as ctx:
        def sem(name):
            return ctx.enter_context(nc.semaphore(name))

        def sb(name, shape):
            return ctx.enter_context(nc.sbuf_tensor(name, shape, F32))

        sums = sb("co_sums", [P, 2, C])
        gsum = sb("co_gsum", [P, 2, G])
        tot = sb("co_tot", [P, 2, G])
        rs = sb("co_rs", [P, 4, G])
        m0 = sb("co_m0", [P, G])
        patch = sb("co_patch", [K2, K2, C])
        kern = [sb(f"co_kern{i}", [K2, K2, C]) for i in range(3)]
        conv = sb("co_conv", [K2, 3, C])
        at = sb("co_at", [K2, C])
        x1c = sb("co_x1", [K2, C])
        w = [sb(f"co_w{i}", [K2, C]) for i in range(8)]
        ht = sb("co_ht", [C, K2])
        ps = ctx.enter_context(nc.psum_tensor("co_ps", [P, 2, G], F32))
        tp = ctx.enter_context(nc.psum_tensor("co_tp", [C, K2], F32))
        op = ctx.enter_context(nc.psum_tensor("co_op", [K2, C], F32))
        halo_done, square_done, patch_in, kern_in, small_in = (sem(f"co_{x}") for x in
                                                               ("halo", "square", "patch", "kern", "small"))
        chain, gsum_ready, mean_ready, var_ready, std_ready = (sem(f"co_{x}") for x in
                                                               ("chain", "gsumr", "meanr", "varr", "stdr"))
        conv_ready, gates, b_ready, act_own, sp_ready, h_ready, t_done, ht_ready, o_done = (
            sem(f"co_{x}") for x in ("convr", "gates", "br", "acto", "spr", "hr", "td", "htr", "od"))
        block = ctx.enter_context(nc.Block())

        @block.sync
        def _(sp):
            sq = d["square"]
            for dst, src, n in ((0, N - R - R, R + R), (R + R, 0, R + R + 1)):
                for dst2, src2, n2 in ((0, N - R - R, R + R), (R + R, 0, R + R + 1)):
                    sp.dma_start(sq[dst:dst + n, dst2:dst2 + n2, :], d["x1"][src:src + n, src2:src2 + n2, :])\
                        .then_inc(square_done, 16)
            for i in range(3):
                sp.dma_start(kern[i][:, :, :].rearrange("p t c -> p (t c)"), d["taps"][i].rearrange("t c -> (t c)")
                             .partition_broadcast(K2)).then_inc(kern_in, 16)
            sp.dma_start(at[:, :], d["kA"]).then_inc(small_in, 16)
            sp.wait_ge(square_done, 64)
            sp.dma_start(x1c[:, :], sq[R:R + TAPS, R:R + TAPS, :]).then_inc(small_in, 16)
            for a in range(TAPS):
                rows = sq[a:a + TAPS].rearrange("t u c -> t (u c)")
                window = bass.AP(rows.tensor, rows.offset, [[C, TAPS], [S * C, TAPS], [1, TAPS * C]])
                sp.dma_start(patch[a * TAPS:(a + 1) * TAPS, :, :], window).then_inc(patch_in, 16)
            sp.dma_start(d["x1h"][:, 0:BH], d["x1h"][:, N:N + BH]).then_inc(halo_done, 16)
            sp.dma_start(d["x1h"][:, N + BH:HPAD], d["x1h"][:, BH:2 * BH]).then_inc(halo_done, 16)
            sp.wait_ge(halo_done, 32)

        @block.vector
        def _(dve):
            ch = Chain(dve, chain)
            ch.step(dve.tensor_tensor(sums[:, :, :], b["acc"][:, :, 0:C], b["acc"][:, :, C:2 * C], ALU.add))
            dve.tensor_reduce(gsum[:, :, :], sums[:, :, :].rearrange("p a (g c) -> p a g c", c=GC), AX.X, ALU.add)\
                .then_inc(gsum_ready, 1)
            dve.wait_ge(mean_ready, 1)
            ch.step(dve.tensor_scalar(tot[:, :, :], ps[:, :, :], SC, None, ALU.mult))
            ch.step(dve.tensor_tensor(rs[:, 0, :], tot[:, 0, :], tot[:, 0, :], ALU.mult))
            ch.step(dve.tensor_tensor(rs[:, 1, :], tot[:, 1, :], rs[:, 0, :], ALU.subtract))
            dve.tensor_scalar(rs[:, 2, :], rs[:, 1, :], GN_EPS, None, ALU.add).then_inc(var_ready, 1)
            ch.step(dve.tensor_tensor(m0[:, :], tot[:, 0, :], b["mean0"][:, :].rearrange("p (g c) -> p g c", c=GC)[:, :, 0],
                                      ALU.add))
            dve.wait_ge(std_ready, 1)
            ch.step(dve.reciprocal(rs[:, 0, :], rs[:, 3, :]))
            for t, src in ((b["gn_a"], rs[:, 0, :]), (b["mean0"], m0[:, :])):
                ch.step(dve.tensor_scalar(t[:, :].rearrange("p (g c) -> p g c", c=GC),
                                          src.unsqueeze(2).to_broadcast([P, G, GC]), 1.0, None, ALU.mult))
            ch.step(dve.tensor_scalar(b["xscale"][:, :], b["gn_a"][:, :], XSCALE, None, ALU.mult))
            dve.wait_ge(patch_in, 16 * TAPS)
            ch.step(dve.tensor_tensor(patch[:, :, :], patch[:, :, :], bcast_rows(b["mean0"][0:K2, :], K2), ALU.subtract))
            ch.step(dve.tensor_tensor(patch[:, :, :], patch[:, :, :], bcast_rows(b["gn_a"][0:K2, :], K2), ALU.mult))
            dve.wait_ge(kern_in, 48)
            for i in range(3):
                ch.step(dve.tensor_tensor(kern[i][:, :, :], kern[i][:, :, :], patch[:, :, :], ALU.mult))
                dve.tensor_reduce(conv[:, i, :], kern[i][:, :, :].rearrange("p t c -> p c t"), AX.X, ALU.add)\
                    .then_inc(conv_ready, 1)
            dve.wait_ge(gates, 2)
            dve.wait_ge(small_in, 32)
            ch.step(dve.tensor_tensor(w[2][:, :], at[:, :], w[0][:, :], ALU.mult))
            dve.tensor_tensor(w[3][:, :], conv[:, 2, :], w[1][:, :], ALU.mult).then_inc(b_ready, 1)
            dve.wait_ge(sp_ready, 3)
            ch.step(dve.scalar_tensor_tensor(w[6][:, :], w[3][:, :], 0.0, w[6][:, :], ALU.max, ALU.add))
            ch.step(dve.tensor_scalar(w[6][:, :], w[6][:, :], SP_EPS, None, ALU.add))
            ch.step(dve.tensor_tensor(w[6][:, :], w[6][:, :], w[4][:, :], ALU.mult))
            for i in range(3):
                ch.step(dve.scalar_tensor_tensor(w[6][:, :], w[5][:, :], 1.0, w[6][:, :], ALU.add, ALU.mult))
                if i < 2:
                    ch.step(dve.tensor_tensor(w[5][:, :], w[5][:, :], w[5][:, :], ALU.mult))
            ch.step(dve.tensor_copy(w[7][:, :], w[6][:, :]))
            dve.tensor_tensor(x1c[:, :], x1c[:, :], b["bout"][0:K2, :], ALU.add).then_inc(h_ready, 1)
            dve.wait_ge(t_done, 1)
            dve.tensor_copy(ht[:, :], tp[:, :]).then_inc(ht_ready, 1)
            dve.wait_ge(o_done, 1)
            ch.step(dve.tensor_tensor(b["corner"][:, :], op[:, :], x1c[:, :], ALU.add))

        @block.scalar
        def _(act):
            act.wait_ge(var_ready, 1)
            act.activation(rs[:, 3, :], rs[:, 2, :], ACT.Sqrt).then_inc(std_ready, 1)
            for i in range(2):
                act.wait_ge(conv_ready, i + 1)
                act.activation(w[i][:, :], conv[:, i, :], ACT.Sigmoid).then_inc(gates, 1)
            act.wait_ge(b_ready, 1)
            act.activation(w[4][:, :], w[2][:, :], ACT.Sigmoid).then_inc(sp_ready, 1)
            act.activation(w[5][:, :], w[2][:, :], ACT.Sigmoid, scale=-1.0).then_inc(sp_ready, 1)
            act.activation(w[6][:, :], w[3][:, :], ACT.Abs).then_inc(act_own, 1)
            act.wait_ge(act_own, 1)
            act.activation(w[6][:, :], w[6][:, :], ACT.Exp, scale=-1.0).then_inc(act_own, 1)
            act.wait_ge(act_own, 2)
            act.activation(w[6][:, :], w[6][:, :], ACT.Ln, bias=1.0).then_inc(sp_ready, 1)

        @block.tensor
        def _(pe):
            pe.wait_ge(gsum_ready, 1)
            nc.tensor.matmul(ps[:, :, :].rearrange("p a g -> p (a g)"), b["mean_w"][:, :],
                             gsum[:, :, :].rearrange("p a g -> p (a g)"), start=True, stop=True).then_inc(mean_ready, 1)
            pe.wait_ge(h_ready, 1)
            nc.tensor.transpose(tp[:, :], w[7][:, :], b["ident"][0:K2, 0:K2]).then_inc(t_done, 1)
            pe.wait_ge(ht_ready, 1)
            nc.tensor.matmul(op[:, :], ht[:, :], b["w2"][:, :], start=True, stop=True).then_inc(o_done, 1)


def conv_stage(nc, d, b):
    TG = 8
    TGS = CCH // TG
    EG = 4
    SUB = 16
    SUBS = CCH // SUB
    EGS = SUB // EG
    XR = SROWS + 2
    XP = 2
    PIECES = XR // XP
    STEPS = NCC * STRIPS
    rows3 = ((R, BH, 0, 1), (0, R, BH - R, 0), (R + BH, R, 0, 2))
    with ExitStack() as ctx:
        def sem(name):
            return ctx.enter_context(nc.semaphore(name))

        def sb(name, shape, dt=F32):
            return ctx.enter_context(nc.sbuf_tensor(name, shape, dt))

        raw = [sb(f"cv_raw{s}", [P, XP, WB, CCH]) for s in range(2)]
        xc = [sb(f"cv_xc{s}", [P, 2, XR, WB, CCH], F16) for s in range(2)]
        xl = [sb(f"cv_xl{s}", [P, 2, XR, WB, CCH], F16) for s in range(2)]
        tk = [sb(f"cv_tk{g}", [P, TG, 2, WROWS, 2, PITCH], F16) for g in range(TGS)]
        h = [sb(f"cv_h{s}", [P, SUB, P]) for s in range(2)]
        soft = sb("cv_soft", [P, SUB, P])
        cp = [ctx.enter_context(nc.psum_tensor(f"cv_cp{s}", [P, EG, BH, 2, BW], F32)) for s in range(EGS)]

        raw_in = [sem(f"cv_raw_in{s}") for s in range(2)]
        xl_in = [sem(f"cv_xl_in{s}") for s in range(2)]
        tk_in = [sem(f"cv_tk_in{g}") for g in range(TGS)]
        stored = [sem(f"cv_stored{s}") for s in range(2)]
        centred, scaled, high_ready, low_ready, zeroed = (sem(f"cv_{x}") for x in ("cen", "sca", "hi", "lo", "zero"))
        group_done, group_used = sem("cv_group"), sem("cv_gused")
        GPS = CCH // EG
        gate_done, mag_ready, soft_own, soft_ready, h_ready = (sem(f"cv_{x}") for x in
                                                               ("gate", "mag", "softo", "softr", "hr"))
        sp_passed, pool_passed, act_passed = sem("cv_spp"), sem("cv_poolp"), sem("cv_actp")
        SIDES = 4 * R
        block = ctx.enter_context(nc.Block())

        @block.sync
        def _(sp):
            sp.sem_inc(low_ready, 2)

            def load(q, s, j):
                k = (s * PIECES + j) % 2
                hold(sp, low_ready, q * (STRIPS * PIECES) + (s * PIECES + j + 1), sp_passed)
                v = d["x1h"][ds(q, 1), (s * SROWS + j * XP) * BH:(s * SROWS + (j + 1) * XP) * BH].squeeze(0)
                v = v.rearrange("(a h) m b c -> h m a (b c)", h=BH).rearrange("h m a x -> (h m) a x")
                sp.dma_start(raw[k][:, :, :, :].rearrange("p a b c -> p a (b c)"), v).then_inc(raw_in[k], 16)

            def sides(q, s):
                k = s % 2
                hold(sp, low_ready, q * (STRIPS * PIECES) + ((s + 1) * PIECES + 2), sp_passed)
                for r in range(R):
                    for m, far, near in ((r, (0, WB - 1, 1, WB), (WB - 1, WB, 0, 1)),
                                         (BW - R + r, (1, WB, 0, WB - 1), (0, 1, WB - 1, WB))):
                        to = xl[k][m:m + (BH - 1) * BW + 1:BW].rearrange("p h a b c -> p (h a) b c")
                        of = xc[k][m:m + (BH - 1) * BW + 1:BW].rearrange("p h a b c -> p (h a) b c")
                        for t0, t1, f0, f1 in (far, near):
                            sp.dma_start(to[:, :, t0:t1, :].rearrange("p a b c -> p a (b c)"),
                                         of[:, :, f0:f1, :].rearrange("p a b c -> p a (b c)")).then_inc(xl_in[k], 16)

            def kernels(q, g):
                hold(sp, group_done, q * (STRIPS * GPS) + (g + 1) * (TG // EG), sp_passed)
                for hm in range(BH):
                    taps = bass.AP(d["flat"].tensor, q * (CCH * 2 * FLAT) + g * TG * 2 * FLAT,
                                   [[1, BW], [FLAT, TG * 2], [1, TAPROWS]])
                    sp.dma_start(tk[g][hm * BW:(hm + 1) * BW, :, :, BH - 1 - hm:BH - 1 - hm + TAPS]
                                 .rearrange("p c h r k u -> p (c h) (r k u)"), taps).then_inc(tk_in[g], 16)

            sp.sem_inc(group_done, GPS)
            sp.wait_ge(zeroed, TGS + 2)
            with sp.Fori(0, NCC) as q:
                for s in range(STRIPS):
                    if s == 1:
                        load(q, s, 0)
                        load(q, s, 1)
                        kernels(q, TGS - 1)
                    for j in range(2 if s == 1 else 0, PIECES):
                        load(q, s, j)
                    sides(q, s)
                    if s == 0:
                        for g in range(TGS - 1):
                            kernels(q, g)

        @block.gpsimd
        def _(pool):
            for g in range(TGS):
                pool.memset(tk[g][:, :, :, :, :, :], 0.0).then_inc(zeroed, 1)
            for s in range(2):
                pool.memset(xl[s][:, :, :, :, :], 0.0).then_inc(zeroed, 1)
            with pool.Fori(0, NCC) as q:
                mean, scale = (b[name][:, ds(q * CCH, CCH)].unsqueeze(1).to_broadcast([P, XP * WB, CCH])
                               for name in ("mean0", "xscale"))
                with pool.Fori(0, STRIPS // 2) as m:
                    for i in range(2 * PIECES):
                        flat = raw[i % 2][:, :, :, :].rearrange("p a b c -> p (a b) c")
                        hold(pool, raw_in[i % 2], q * (STRIPS // 2 * PIECES * 16) + (m * (PIECES * 16) + (i // 2 + 1) * 16),
                             pool_passed)
                        pool.tensor_tensor(flat, flat, mean, ALU.subtract).then_inc(centred, 1)
                        hold(pool, centred, q * (STRIPS * PIECES) + (m * (2 * PIECES) + (i + 1)), pool_passed)
                        pool.tensor_tensor(flat, flat, scale, ALU.mult).then_inc(scaled, 1)

        @block.tensor
        def _(pe):
            def products(k, cl, out):
                t = tk[cl // TG][:, cl % TG]
                last = None
                for high, parts in ((0, (0, 1)), (1, (0,))):
                    for mr, nr, orow, arow in rows3:
                        for side, x in enumerate((xc[k], xl[k])):
                            blocks = x[:, high, arow:arow + SROWS, :, cl].rearrange("p a b -> p (a b)")
                            for part in parts:
                                taps = t[:, part, mr:mr + nr].rearrange("p r k u -> p (r k) u")
                                to = out[:, orow:orow + nr].rearrange("p r k u -> p (r k) u")
                                if side:
                                    taps = pair(taps[:, :, 0:R], R + BW)
                                    to = pair(to[:, :, BW - R:BW], R - BW)
                                else:
                                    taps = taps[:, :, R:R + BW]
                                last = nc.tensor.matmul(to, blocks, taps, start=last is None,
                                                        stop=(high == 1 and arow == 2 and side == 1))
                return last

            pe.sem_inc(group_used, EGS)
            with pe.Fori(0, NCC) as q:
                with pe.Fori(0, STRIPS // 2) as m:
                    for k in range(2):
                        pe.wait_ge(low_ready, q * (STRIPS * PIECES) + (m * (2 * PIECES) + ((k + 1) * PIECES + 2)))
                        pe.wait_ge(xl_in[k], q * (STRIPS // 2 * SIDES * 16) + (m * (SIDES * 16) + SIDES * 16))
                        for cl in range(CCH):
                            g = cl // EG
                            if cl % TG == 0:
                                pe.wait_ge(tk_in[cl // TG], q * (BH * 16) + BH * 16)
                            if cl % EG == 0:
                                pe.wait_ge(group_used, q * (STRIPS * GPS) + (m * (2 * GPS) + (k * GPS + g + 1)))
                            last = products(k, cl, cp[g % EGS][:, cl % EG])
                            if cl % EG == EG - 1:
                                last.then_inc(group_done, 1)

        def split(eng, m, k, j, n):
            i = (k + 1) * PIECES + j
            x = xc[(k + 1) % 2][:, :, j * XP:(j + 1) * XP]
            of = raw[i % 2][:, :, :, :]
            if n == "high":
                if j == 0:
                    hold(eng, group_done, m * (2 * GPS) + (k + 1) * GPS, act_passed)
                hold(eng, scaled, m * (2 * PIECES) + (i + 1), act_passed)
                eng.activation(x[:, 0], of, ACT.Copy).then_inc(high_ready, 1)
            else:
                eng.wait_ge(high_ready, m * (2 * PIECES) + (i + 1))
                eng.tensor_tensor(x[:, 1], of, x[:, 0], ALU.subtract).then_inc(low_ready, 1)

        @block.scalar
        def _(act):
            def gate(m, k, g):
                if g % EGS == 0:
                    act.wait_ge(stored[g // EGS], m * (2 * 16) + (k + 1) * 16)
                act.wait_ge(group_done, m * (2 * GPS) + ((k + 1) * GPS + g + 1))
                act.activation(h[g // EGS][:, g % EGS * EG:(g % EGS + 1) * EG, :].rearrange("p c (a b) -> p c a b", b=BW),
                               cp[g % EGS][:, :, :, 0, :], ACT.Sigmoid,
                               scale=b["kscale"][:, 0:1]).then_inc(gate_done, 1)

            def logarithm(m, k, v):
                n = m * (2 * SUBS) + (k * SUBS + v)
                act.wait_ge(mag_ready, n + 1)
                act.activation(soft[:, :, :], soft[:, :, :], ACT.Exp, scale=-1.0).then_inc(soft_own, 1)
                act.wait_ge(soft_own, n + 1)
                act.activation(soft[:, :, :], soft[:, :, :], ACT.Ln, bias=1.0).then_inc(soft_ready, 1)

            def store(n, m, k, v):
                act.wait_ge(h_ready, m * (2 * SUBS) + (k * SUBS + v + 1))
                act.dma_start(d["h"][n, :, v * SUB:(v + 1) * SUB, :] if isinstance(n, int) else
                              d["h"][ds(n, 1), :, v * SUB:(v + 1) * SUB, :].squeeze(0), h[v][:, :, :]).then_inc(stored[v], 16)

            def steps(m, last):
                for k in range(2):
                    more = not (last and k == 1)
                    before = {0: (0, 1), 2: (2,), 4: (3,), 5: (4,)}
                    for g in range(GPS):
                        if more:
                            for j in before.get(g, ()):
                                split(act, m, k, j, "high")
                        gate(m, k, g)
                        if g % EGS == EGS - 1:
                            logarithm(m, k, g // EGS)
                        if g == EGS + 1:
                            store(m * 2 + k, m, k, 0)
                        if g == 1 and k == 1:
                            store(m * 2, m, 0, 1)
                        if g == 1 and k == 0 and not (isinstance(m, int) and m == 0):
                            store(m * 2 - 1, m - 1, 1, 1)
                if last:
                    store(m * 2 + 1, m, 1, 1)

            for s in range(2):
                act.sem_inc(stored[s], 16)
            for j in range(PIECES):
                split(act, 0, -1, j, "high")
            steps(0, False)
            with act.Fori(1, STEPS // 2 - 1) as m:
                steps(m, False)
            steps(STEPS // 2 - 1, True)
            for s in range(2):
                act.wait_ge(stored[s], STEPS * 16 + 16)

        @block.vector
        def _(dve):
            def hidden(m, k, g):
                dve.wait_ge(gate_done, m * (2 * GPS) + (k * GPS + g + 1))
                part = h[g // EGS][:, g % EGS * EG:(g % EGS + 1) * EG, :].rearrange("p c (a b) -> p c a b", b=BW)
                dve.scalar_tensor_tensor(part, cp[g % EGS][:, :, :, 1, :],
                                         b["kscale"][:, 1:2], part, ALU.mult, ALU.mult).then_inc(group_used, 1)

            def magnitude(m, k, v):
                n = m * (2 * SUBS) + (k * SUBS + v)
                dve.wait_ge(group_used, m * (2 * GPS) + (k * GPS + (v + 1) * EGS + EGS))
                if not (isinstance(n, int) and n == 0):
                    dve.wait_ge(h_ready, n)
                dve.scalar_tensor_tensor(soft[:, :, :], h[v][:, :, :], -1.0, h[v][:, :, :], ALU.mult, ALU.max)\
                    .then_inc(mag_ready, 1)

            def softplus(m, k, v):
                dve.wait_ge(soft_ready, m * (2 * SUBS) + (k * SUBS + v + 1))
                dve.scalar_tensor_tensor(h[v][:, :, :], h[v][:, :, :], 0.0, soft[:, :, :], ALU.max, ALU.add)\
                    .then_inc(h_ready, 1)

            def steps(m, last):
                for k in range(2):
                    more = not (last and k == 1)
                    before = {0: (0, 1), 2: (2,), 4: (3,), 5: (4,)}
                    for g in range(GPS):
                        if more:
                            for j in before.get(g, ()):
                                split(dve, m, k, j, "low")
                        hidden(m, k, g)
                        if g % EGS == EGS - 1:
                            magnitude(m, k, g // EGS)
                            softplus(m, k, g // EGS)

            for j in range(PIECES):
                split(dve, 0, -1, j, "low")
            steps(0, False)
            with dve.Fori(1, STEPS // 2 - 1) as m:
                steps(m, False)
            steps(STEPS // 2 - 1, True)


def output_stage(nc, d, b):
    QW = 4
    STEPS = P // QW
    RES = 4
    scan = 1.0 - 0.5 ** 8
    with ExitStack() as ctx:
        def sem(name):
            return ctx.enter_context(nc.semaphore(name))

        def sb(name, shape):
            return ctx.enter_context(nc.sbuf_tensor(name, shape, F32))

        h = [sb(f"ou_h{s}", [P, C, P]) for s in range(2)]
        ht = [sb(f"ou_ht{s}", [P, QW * P]) for s in range(2)]
        res = [sb(f"ou_res{s}", [P, QW, C]) for s in range(RES)]
        eps = sb("ou_eps", [P, 1])
        tp = [ctx.enter_context(nc.psum_tensor(f"ou_tp{s}", [P, QW * P], F32)) for s in range(2)]
        op = [ctx.enter_context(nc.psum_tensor(f"ou_op{s}", [P, QW * C], F32)) for s in range(2)]
        h_in = [sem(f"ou_h_in{s}") for s in range(2)]
        res_in = [sem(f"ou_res_in{s}") for s in range(RES)]
        res_free = [sem(f"ou_res_free{s}") for s in range(RES)]
        t_done, ht_ready, o_done, o_ready, biased = (sem(f"ou_{x}") for x in ("t", "htr", "o", "or", "bia"))
        eps_ready, corner_out = sem("ou_epsr"), sem("ou_corner")
        sp_passed, pool_passed = sem("ou_spp"), sem("ou_poolp")
        block = ctx.enter_context(nc.Block())

        def res_view(t, s, k):
            hm, wm = BH - 1 - k // (BW // QW), BW - QW - (k % (BW // QW)) * QW
            v = t.rearrange("(i h) (j w) c -> h i j w c", h=BH, w=BW)[hm]
            return v[ds(s * SROWS, SROWS), :, wm:wm + QW, :].rearrange("i j w c -> i j (w c)")

        @block.sync
        def _(sp):
            for r in range(RES):
                sp.sem_inc(res_free[r], 16)
            sp.sem_inc(t_done, 2 * STEPS)
            with sp.Fori(0, STRIPS // 2) as m:
                def load(i):
                    k = i % STEPS
                    hold(sp, res_free[k % RES], m * (2 * STEPS // RES * 16) + (i // RES + 1) * 16, sp_passed)
                    sp.dma_start(res[k % RES][:, :, :].rearrange("p w c -> p (w c)"), res_view(d["x1"], m * 2 + i // STEPS, k))\
                        .then_inc(res_in[k % RES], 16)

                for i in range(RES - 1):
                    load(i)
                for i in range(2 * STEPS):
                    if i + RES - 1 < 2 * STEPS:
                        load(i + RES - 1)
                    hold(sp, o_ready, m * (2 * STEPS) + (i + 1), sp_passed)
                    sp.dma_start(res_view(d["out"][0], m * 2 + i // STEPS, i % STEPS),
                                 res[i % RES][:, :, :].rearrange("p w c -> p (w c)")).then_inc(res_free[i % RES], 16)
            for r in range(RES):
                sp.wait_ge(res_free[r], (STRIPS * STEPS // RES + 1) * 16)
            for a0, na, h0 in ((0, R, N - R), (R, R + 1, 0)):
                for a in range(na):
                    for c0, ncol, w0 in ((0, R, N - R), (R, R + 1, 0)):
                        p0 = (a0 + a) * TAPS + c0
                        sp.dma_start(d["out"][0, h0 + a, w0:w0 + ncol, :], b["corner"][p0:p0 + ncol, :])\
                            .then_inc(corner_out, 16)
            sp.wait_ge(corner_out, 2 * TAPS * 16)

        @block.gpsimd
        def _(pool):
            pool.memset(eps[:, :], scan * SP_EPS).then_inc(eps_ready, 1)
            with pool.Fori(0, STRIPS // 2) as m:
                for s in range(2):
                    hold(pool, t_done, m * (2 * STEPS) + (s + 1) * STEPS, pool_passed)
                    for q in range(NCC):
                        pool.dma_start(h[s][:, q * CCH:(q + 1) * CCH, :],
                                       d["h"][ds(m * 2 + (q * STRIPS + s), 1)].squeeze(0)).then_inc(h_in[s], 16)

                    for k in range(STEPS):
                        i = s * STEPS + k
                        r = res[k % RES]
                        hold(pool, res_in[k % RES], m * (2 * STEPS // RES * 16) + (i // RES + 1) * 16, pool_passed)
                        pool.tensor_tensor(r[:, :, :], r[:, :, :], bcast_rows(b["bout"][:, :], QW), ALU.add).then_inc(biased, 1)

        @block.tensor
        def _(pe):
            with pe.Fori(0, STRIPS // 2) as m:
                base = m * (2 * STEPS)

                def project(i):
                    pe.wait_ge(ht_ready, base + (i + 1))
                    if i >= 2:
                        pe.wait_ge(o_ready, base + (i - 1))
                    for j in range(QW):
                        last = nc.tensor.matmul(op[i % 2][:, (QW - 1 - j) * C:(QW - j) * C],
                                                ht[i % 2][:, j * P:(j + 1) * P], b["w2"][:, :], start=True, stop=True)
                    last.then_inc(o_done, 1)

                for i in range(2 * STEPS):
                    if i % STEPS == 0:
                        pe.wait_ge(h_in[i // STEPS], m * (NCC * 16) + NCC * 16)
                    if i >= 2:
                        pe.wait_ge(ht_ready, base + (i - 1))
                    for j in range(QW):
                        last = nc.tensor.transpose(tp[i % 2][:, j * P:(j + 1) * P],
                                                   h[i // STEPS][:, :, i % STEPS * QW + j], b["ident"][:, :])
                    last.then_inc(t_done, 1)
                    if i >= 1:
                        project(i - 1)
                project(2 * STEPS - 1)
                pe.wait_ge(o_ready, base + 2 * STEPS)

        @block.scalar
        def _(act):
            act.wait_ge(eps_ready, 1)
            with act.Fori(0, STRIPS // 2) as m:
                for i in range(2 * STEPS):
                    act.wait_ge(t_done, m * (2 * STEPS) + (2 * STEPS + i + 1))
                    if i >= 2:
                        act.wait_ge(o_done, m * (2 * STEPS) + (i - 1))
                    act.activation(ht[i % 2][:, :], tp[i % 2][:, :], ACT.Identity, scale=scan, bias=eps[:, :])\
                        .then_inc(ht_ready, 1)

        @block.vector
        def _(dve):
            with dve.Fori(0, STRIPS // 2) as m:
                for i in range(2 * STEPS):
                    r = res[i % RES][:, :, :].rearrange("p w c -> p (w c)")
                    dve.wait_ge(biased, m * (2 * STEPS) + (i + 1))
                    dve.wait_ge(o_done, m * (2 * STEPS) + (i + 1))
                    dve.tensor_tensor(r, r, op[i % 2][:, :], ALU.add).then_inc(o_ready, 1)


def block_attention_then_gated_convolution(nc, x, mask, gamma, beta, wq, wk, wv, wb, wg, wo,
                                           kA, kB, gB, w2, bout, taps, out):
    d = {
        "x": x, "mask": mask, "gamma": gamma.rearrange("(c o) -> c o", o=1), "beta": beta.rearrange("(c o) -> c o", o=1),
        "wq": wq, "wk": wk, "wv": wv, "wb": wb, "wg": wg, "wo": wo, "w2": w2, "kA": kA, "bout": bout,
        "kB": kB, "gB": gB, "taps": taps, "out": out,
        "flat": nc.dram_tensor("flat_kernels", (C, 2, FLAT), F16).ap(),
        "peaks": nc.dram_tensor("kernel_peaks", (C, 2), F32).ap(),
        "h": nc.dram_tensor("hidden", (NCC * STRIPS, P, CCH, P), F32).ap(),
        "znt": nc.dram_tensor("zn_transposed", (C, N * N), F32).ap(),
        "x1": nc.dram_tensor("x1_rows", (N, N, C), F32).ap(),
        "square": nc.dram_tensor("corner_square", (2 * TAPS - 1, 2 * TAPS - 1, C), F32).ap(),
        "x1h": nc.dram_tensor("x1_halo", (NCC, HPAD, BW, WB, CCH), F32).ap(),
    }
    with ExitStack() as ctx:
        def sb(name, shape, dt=F32):
            return ctx.enter_context(nc.sbuf_tensor(name, shape, dt))

        b = {"w2": sb("w2", [C, C]), "bout": sb("bout", [P, C]), "ident": sb("ident", [P, P])}
        b["gn_a"], b["gn_b"], b["mean0"] = sb("gn_a", [P, C]), sb("gn_b", [P, C]), sb("mean0", [P, C])
        b["xscale"], b["kscale"] = sb("xscale", [P, C]), sb("kscale", [P, 2])
        b["corner"] = sb("corner", [TAPS * TAPS, C])
        middle = ctx.enter_context(ExitStack())
        with ExitStack() as inner:
            def sbi(name, shape, dt=F32, to=inner):
                return to.enter_context(nc.sbuf_tensor(name, shape, dt))

            b["mean_w"] = sbi("mean_w", [P, P], to=middle)
            b["acc"] = sbi("acc", [P, 2, WT * C], to=middle)
            for name in ("wq", "wk", "wv", "wg", "wo"):
                b[name] = sbi(name, [C, C])
            b["wb"] = sbi("wb", [C, HEADS])
            b["gamma"], b["beta"] = sbi("gamma", [C, 1]), sbi("beta", [C, 1])
            b["mask8"] = sbi("mask8", [P, N], U8)
            b["half"] = sbi("half", [P, N])
            b["pow"] = sbi("pow", [P, 8])
            b["nbias"] = sbi("nbias", [P, WT, HEADS, N])
            setup_stage(nc, d, b)
            stats_stage(nc, d, b)
            norm_stage(nc, d, b)
            attention_stage(nc, d, b)
        corner_stage(nc, d, b)
        middle.close()
        conv_stage(nc, d, b)
        output_stage(nc, d, b)


def kernel(**inputs):
    import numpy as _np
    import concourse.bacc as _bacc
    from concourse import mybir as _mybir
    from concourse.bass_utils import run_bass_kernel_spmd as _run

    def rotated(k):
        return k[:, ::-1, ::-1].reshape(C, TAPS * TAPS)

    first, second = "L0_conv_", "L1_conv_"
    gate_a, gate_b, b_kernel = (rotated(_np.asarray(inputs[second + n])) for n in ("gate_A_kernel", "gate_B_kernel", "B_kernel"))
    given = [
        ("x", inputs["x"]),
        ("mask", _np.asarray(inputs[first + "single_mask"]).reshape(-1)),
        ("gamma", inputs[first + "ln_gamma"]),
        ("beta", inputs[first + "ln_beta"]),
        ("wq", inputs[first + "Wq"]),
        ("wk", inputs[first + "Wk"]),
        ("wv", inputs[first + "Wv"]),
        ("wb", inputs[first + "Wb"]),
        ("wg", inputs[first + "Wg"]),
        ("wo", inputs[first + "Wout"]),
        ("kA", _np.asarray(inputs[second + "A_kernel"]).reshape(C, TAPS * TAPS).T),
        ("kB", b_kernel),
        ("gB", gate_b),
        ("w2", inputs[second + "W_out"]),
        ("bout", inputs[second + "b_out"]),
        ("taps", _np.stack([gate_a.T, gate_b.T, b_kernel.T])),
    ]
    nc = _bacc.Bacc("TRN2", target_bir_lowering=False, num_devices=1)
    arrays, args = {}, []
    for name, a in given:
        a = _np.ascontiguousarray(a)
        arrays[f"in_{name}_dram"] = a
        args.append(nc.dram_tensor(f"in_{name}_dram", a.shape, _mybir.dt.from_np(a.dtype), kind="ExternalInput").ap())
    args.append(nc.dram_tensor("out_dram", (1, N, N, C), F32, kind="ExternalOutput").ap())
    block_attention_then_gated_convolution(nc, *args)
    r = _run(nc, [arrays], core_ids=[0])
    return r.results[0]["out_dram"]
```

```python
from contextlib import ExitStack

import concourse.bass as bass
from concourse import mybir

F32 = mybir.dt.float32
F16 = mybir.dt.float16
U8 = mybir.dt.uint8
U32 = mybir.dt.uint32
ALU = mybir.AluOpType
ACT = mybir.ActivationFunctionType
AX = mybir.AxisListType
ds = bass.ds

P = 128
C = 128
N = 256
HEADS, DH = 4, 32
G, GC = 32, 4
TAPS = 7
R = TAPS // 2
GN_EPS, LN_EPS, SP_EPS = 1e-5, 1e-5, 1e-6
NEG = -1e9
WT = N // P

BH, BW = 8, 16
assert BH * BW == P
HB, WB = N // BH, N // BW
PITCH = BW + 2 * R
WROWS = BH + 2 * R
TAPROWS = TAPS * 2 * PITCH
FLAT = TAPROWS + BW
XSCALE = 16.0
KTOP = 256.0
QKTOP = 64.0
EXPONENT = 0x7F800000
CCH = 32
NCC = C // CCH
SROWS = 8
STRIPS = HB // SROWS
HPAD = N + 2 * BH


class Chain:

    def __init__(self, eng, sem, base=0):
        self.eng, self.sem, self.base, self.n = eng, sem, base, 0

    def link(self, ins):
        self.n += 1
        ins.then_inc(self.sem, 1)

    def wait(self):
        self.eng.wait_ge(self.sem, self.base + self.n)

    def step(self, ins):
        self.link(ins)
        self.wait()


def hold(eng, sem, value, passed):
    eng.wait_ge(sem, value)
    eng.sem_inc(passed, 1)


def bcast_rows(t, n):
    return t.unsqueeze(1).to_broadcast([t.shape[0], n, t.shape[1]])


def pair(t, step):
    return bass.AP(t.tensor, t.offset, [list(x) for x in t.ap[:-1]] + [[step, 2], list(t.ap[-1])])


def setup_stage(nc, d, b):
    with ExitStack() as ctx:
        def sem(name):
            return ctx.enter_context(nc.semaphore(name))

        def sb(name, shape, dt=F32):
            return ctx.enter_context(nc.sbuf_tensor(name, shape, dt))

        raw = sb("su_raw", [C, 2, TAPS * TAPS])
        scaled = sb("su_scaled", [C, 2, TAPS * TAPS])
        flat = sb("su_flat", [C, 2, FLAT], F16)
        wabs = sb("su_wabs", [C, 2, C])
        reach = sb("su_reach", [C, 3])
        peak = sb("su_peak", [C, 4])
        peaks = sb("su_peaks", [P, C, 4])
        top = sb("su_top", [P, 4])
        power = sb("su_power", [P, 4])
        inv = sb("su_inv", [P, 4])
        w_in, pool_chain, chain = sem("w_in"), sem("su_pool"), sem("su_chain")
        raw_in, peak_ready, peaks_in, flat_ready, flat_out = (sem(f"su_{x}") for x in
                                                              ("raw", "peak", "peaks", "flat", "flato"))
        block = ctx.enter_context(nc.Block())

        @block.sync
        def _(sp):
            for k, name in enumerate(("gB", "kB")):
                sp.dma_start(raw[:, k, :], d[name]).then_inc(raw_in, 16)
            for name in ("wq", "wk", "wv", "wg", "wo", "w2", "wb"):
                sp.dma_start(b[name][:, :], d[name]).then_inc(w_in, 16)
            sp.dma_start(b["gamma"][:, :], d["gamma"]).then_inc(w_in, 16)
            sp.dma_start(b["beta"][:, :], d["beta"]).then_inc(w_in, 16)
            sp.dma_start(b["bout"][:, :], d["bout"].partition_broadcast(P)).then_inc(w_in, 16)
            sp.dma_start(b["mask8"][:, :], d["mask"].partition_broadcast(P)).then_inc(w_in, 16)
            sp.wait_ge(w_in, 16 * 11)
            sp.wait_ge(peak_ready, 1)
            sp.dma_start(d["peaks"], peak[:, :]).then_inc(peaks_in, 16)
            sp.wait_ge(peaks_in, 16)
            sp.dma_start(peaks[:, :, :].rearrange("p c k -> p (c k)"),
                         d["peaks"].rearrange("c k -> (c k)").partition_broadcast(P)).then_inc(peaks_in, 16)
            sp.wait_ge(flat_ready, 5)
            sp.dma_start(d["flat"], flat[:, :, :]).then_inc(flat_out, 16)
            sp.wait_ge(flat_out, 16)

        @block.vector
        def _(dve):
            ch = Chain(dve, chain)
            dve.memset(flat[:, :, :], 0.0).then_inc(flat_ready, 1)
            dve.wait_ge(raw_in, 32)
            ch.step(dve.scalar_tensor_tensor(scaled[:, :, :], raw[:, :, :], -1.0, raw[:, :, :], ALU.mult, ALU.max))
            ch.link(dve.tensor_reduce(peak[:, 0:2], scaled[:, :, :], AX.X, ALU.max))
            dve.wait_ge(w_in, 16 * 11)
            for k, name in enumerate(("gamma", "beta")):
                ch.link(dve.scalar_tensor_tensor(reach[:, k:k + 1], b[name][:, :], -1.0, b[name][:, :], ALU.mult, ALU.max))
            for k, name in enumerate(("wq", "wk")):
                ch.step(dve.scalar_tensor_tensor(wabs[:, k, :], b[name][:, :], -1.0, b[name][:, :], ALU.mult, ALU.max))
            ch.link(dve.tensor_tensor(reach[:, 2:3], reach[:, 0:1], reach[:, 1:2], ALU.add))
            ch.step(dve.tensor_reduce(peak[:, 2:4], wabs[:, :, :], AX.X, ALU.max))
            dve.tensor_scalar(peak[:, 2:4], peak[:, 2:4], reach[:, 2:3], None, ALU.mult).then_inc(peak_ready, 1)
            dve.wait_ge(peaks_in, 32)
            ch.step(dve.tensor_reduce(top[:, :], peaks[:, :, :].rearrange("p c k -> p k c"), AX.X, ALU.max))
            ch.step(dve.tensor_scalar(top[:, :], top[:, :], 1e-9, None, ALU.max))
            ch.step(dve.tensor_scalar(power[:, :].bitcast(U32), top[:, :].bitcast(U32), EXPONENT, None, ALU.bitwise_and))
            ch.step(dve.reciprocal(inv[:, :], power[:, :]))
            ch.link(dve.tensor_scalar(b["kscale"][:, :], power[:, 0:2], 1.0 / (XSCALE * KTOP), None, ALU.mult))
            for k, name, by in ((2, "wq", -QKTOP / float(DH) ** 0.5), (3, "wk", QKTOP)):
                ch.link(dve.tensor_scalar(b[name][:, :], b[name][:, :], inv[:, k:k + 1], by, ALU.mult, ALU.mult))
            for name, of, by in (("fs", power, 1.0 / QKTOP ** 2), ("fs_inv", inv, QKTOP ** 2)):
                ch.link(dve.tensor_scalar(b[name][:, :], of[:, 2:3], of[:, 3:4], by, ALU.mult, ALU.mult))
            for k in range(2):
                ch.link(dve.tensor_scalar(scaled[:, k, :], raw[:, k, :], inv[:, k:k + 1], KTOP, ALU.mult, ALU.mult))
            dve.wait_ge(chain, ch.n)
            dve.wait_ge(flat_ready, 1)
            high, low = (flat[:, h, 0:TAPROWS].rearrange("p (t k u) -> p t k u", k=2, u=PITCH)[:, :, :, PITCH - TAPS:PITCH]
                         for h in range(2))
            for k in range(2):
                taps = scaled[:, k, :].rearrange("p (t u) -> p t u", u=TAPS)
                dve.tensor_copy(high[:, :, k, :], taps).then_inc(flat_ready, 1)
                dve.wait_ge(flat_ready, 2 + 2 * k)
                dve.tensor_tensor(low[:, :, k, :], taps, high[:, :, k, :],
                                  ALU.subtract).then_inc(flat_ready, 1)

        @block.gpsimd
        def _(pool):
            ch = Chain(pool, pool_chain)
            ch.link(pool.memset(b["ident"][:, :], 0.0))
            ch.link(pool.memset(b["mean_w"][:, :], 1.0 / P))
            ch.link(pool.memset(b["half"][:, :], 0.5))
            ch.link(pool.memset(b["pow"][:, :], -0.5))
            ch.step(pool.memset(b["acc"][:, :, :], 0.0))
            ch.step(pool.affine_select(out=b["ident"][:, :], in_=b["ident"][:, :], compare_op=ALU.not_equal,
                                       fill=1.0, base=0, pattern=[[-1, P]], channel_multiplier=1))


def stats_stage(nc, d, b):
    TOK = N * N // P
    TT = 64
    NT = TOK // TT
    xs = d["x"].rearrange("o h w c -> (o h w c)").rearrange("(p t c) -> p t c", p=P, c=C)
    with ExitStack() as ctx:
        def sem(name):
            return ctx.enter_context(nc.semaphore(name))

        def sb(name, shape):
            return ctx.enter_context(nc.sbuf_tensor(name, shape, F32))

        xt = [sb(f"st_x{s}", [P, TT, C]) for s in range(2)]
        st = sb("st_st", [P, G, NT, 6])
        mv = sb("st_mv", [P, G, 2])
        me = sb("st_me", [P, 2, G])
        tot = sb("st_tot", [P, 2, G])
        rs = sb("st_rs", [P, 4, G])
        ps = ctx.enter_context(nc.psum_tensor("st_ps", [P, 2, G], F32))
        loaded = [sem(f"st_loaded{s}") for s in range(2)]
        used, chain, sp_passed = sem("st_used"), sem("st_chain"), sem("st_spp")
        me_ready, sum_ready, var_ready, std_ready = sem("st_me"), sem("st_sum"), sem("st_var"), sem("st_std")
        block = ctx.enter_context(nc.Block())

        @block.sync
        def _(sp):
            for s in range(2):
                sp.dma_start(xt[s][:, :, :], xs[:, s * TT:(s + 1) * TT, :]).then_inc(loaded[s], 16)
            with sp.Fori(0, NT // 2 - 1) as n:
                for s in range(2):
                    hold(sp, used, n * 2 + s + 1, sp_passed)
                    sp.dma_start(xt[s][:, :, :], xs[:, ds(n * (2 * TT) + (2 + s) * TT, TT), :])\
                        .then_inc(loaded[s], 16)

        @block.vector
        def _(dve):
            with dve.Fori(0, NT // 2) as n:
                for s in range(2):
                    dve.wait_ge(loaded[s], n * 16 + 16)
                    for g in range(G):
                        last = dve.bn_stats(st[:, g, ds(n * 2 + s, 1), :].rearrange("p a b -> p (a b)"),
                                            xt[s][:, :, g * GC:(g + 1) * GC])
                    last.then_inc(used, 1)
            dve.wait_ge(used, NT)
            ch = Chain(dve, chain)
            for g in range(G):
                last = dve.bn_aggr(mv[:, g, :], st[:, g, :, :].rearrange("p a b -> p (a b)"))
            ch.step(last)
            ch.link(dve.tensor_copy(me[:, 0, :], mv[:, :, 0]))
            ch.step(dve.tensor_tensor(me[:, 1, :], mv[:, :, 0], mv[:, :, 0], ALU.mult))
            dve.tensor_tensor(me[:, 1, :], me[:, 1, :], mv[:, :, 1], ALU.add).then_inc(me_ready, 1)
            dve.wait_ge(sum_ready, 1)
            ch.step(dve.tensor_copy(tot[:, :, :], ps[:, :, :]))
            ch.step(dve.tensor_tensor(rs[:, 0, :], tot[:, 0, :], tot[:, 0, :], ALU.mult))
            ch.step(dve.tensor_tensor(rs[:, 1, :], tot[:, 1, :], rs[:, 0, :], ALU.subtract))
            dve.tensor_scalar(rs[:, 2, :], rs[:, 1, :], GN_EPS, None, ALU.add).then_inc(var_ready, 1)
            dve.wait_ge(std_ready, 1)
            ch.step(dve.reciprocal(rs[:, 0, :], rs[:, 3, :]))
            ch.step(dve.tensor_tensor(rs[:, 1, :], tot[:, 0, :], rs[:, 0, :], ALU.mult))
            for t, src, by in ((b["gn_a"], rs[:, 0, :], 1.0), (b["gn_b"], rs[:, 1, :], -1.0), (b["mean0"], tot[:, 0, :], 1.0)):
                ch.link(dve.tensor_scalar(t[:, :].rearrange("p (g c) -> p g c", c=GC),
                                          src.unsqueeze(2).to_broadcast([P, G, GC]), by, None, ALU.mult))

        @block.tensor
        def _(pe):
            pe.wait_ge(me_ready, 1)
            nc.tensor.matmul(ps[:, :, :].rearrange("p a g -> p (a g)"), b["mean_w"][:, :],
                             me[:, :, :].rearrange("p a g -> p (a g)"), start=True, stop=True).then_inc(sum_ready, 1)

        @block.scalar
        def _(act):
            act.wait_ge(var_ready, 1)
            act.activation(rs[:, 3, :], rs[:, 2, :], ACT.Sqrt).then_inc(std_ready, 1)


def norm_stage(nc, d, b):
    RQ = 4
    T = RQ * WT
    NQ = N // RQ
    TD = 5
    RING = 4
    xv = d["x"].rearrange("o r (t w) c -> w (o r t) c", t=WT)
    with ExitStack() as ctx:
        def sem(name):
            return ctx.enter_context(nc.semaphore(name))

        def sb(name, shape):
            return ctx.enter_context(nc.sbuf_tensor(name, shape, F32))

        xt = [sb(f"no_x{s}", [P, T, C]) for s in range(RING)]
        xn = [sb(f"no_n{s}", [P, T, C]) for s in range(RING)]
        st = sb("no_st", [P, 2, T, 6])
        mv = sb("no_mv", [P, 2, T, 2])
        ve = sb("no_ve", [P, 2, T])
        rstd = sb("no_rstd", [P, 2, T])
        nmean = sb("no_nmean", [P, 2, T])
        shift = sb("no_shift", [P, 2, T])
        zt = [sb(f"no_z{s}", [P, T * P]) for s in range(2)]
        bias_t = sb("no_bt", [P, WT, HEADS, N])
        bias_q = sb("no_bq", [P, WT, HEADS, N])
        negm = sb("no_negm", [P, N])
        zp = [ctx.enter_context(nc.psum_tensor(f"no_zp{k}", [P, 512], F32)) for k in range(4)]
        bp = [ctx.enter_context(nc.psum_tensor(f"no_bp{k}", [P, RQ, WT, HEADS], F32)) for k in range(2)]
        loaded = [sem(f"no_loaded{s}") for s in range(RING)]
        stored = [sem(f"no_stored{s}") for s in range(2)]
        scaled, centred, mv_ready, rstd_ready, normed = (sem(f"no_{x}") for x in
                                                         ("scaled", "centred", "mv", "rstd", "normed"))
        z_psum, z_ready, b_psum, b_read = (sem(f"no_{x}") for x in ("zpsum", "zready", "bpsum", "bread"))
        pool_own, dve_own = sem("no_pool"), sem("no_dve")
        tr_ready, neg_ready = sem("no_tr"), sem("no_neg")
        tr_read = sem("no_trread")
        shift_ready, act_normed = sem("no_shiftr"), sem("no_actn")
        sp_passed, dve_passed, pool_passed = sem("no_spp"), sem("no_dvep"), sem("no_poolp")


        def pool_scale(pool, n, s, turn, first):
            pool.wait_ge(loaded[s], turn * 16 + 16)
            if not first:
                pool.wait_ge(z_psum, n * 2 - 2 * (RING - 1))
            pool.tensor_tensor(xn[s][:, :, :], xt[s][:, :, :], bcast_rows(b["gn_a"][:, :], T), ALU.mult)\
                .then_inc(scaled, 1)

        def pool_rstd(pool, n, s):
            hold(pool, mv_ready, n + 1, pool_passed)
            pool.tensor_scalar(ve[:, s % 2, :], mv[:, s % 2, :, 1], LN_EPS, None, ALU.add).then_inc(pool_own, 1)
            pool.tensor_scalar(nmean[:, s % 2, :], mv[:, s % 2, :, 0], -1.0, None, ALU.mult).then_inc(pool_own, 1)
            pool.wait_ge(pool_own, n * 2 + 2)
            pool.tensor_tensor(rstd[:, s % 2, :], ve[:, s % 2, :], b["pow"][:, 0:T], ALU.pow).then_inc(rstd_ready, 1)
            pool.wait_ge(rstd_ready, n + 1)
            pool.tensor_tensor(shift[:, s % 2, :], nmean[:, s % 2, :], rstd[:, s % 2, :], ALU.mult).then_inc(shift_ready, 1)

        def dve_stats(dve, n, s):
            dve.wait_ge(scaled, n + 1)
            dve.tensor_tensor(xn[s][:, :, :], xn[s][:, :, :], bcast_rows(b["gn_b"][:, :], T), ALU.add)\
                .then_inc(centred, 1)
            dve.wait_ge(centred, n + 1)
            for t in range(T):
                last = dve.bn_stats(st[:, s % 2, t, :], xn[s][:, t, :])
            last.then_inc(dve_own, 1)

        def dve_moments(dve, n, s, first):
            if not first:
                dve.wait_ge(act_normed, n - 1)
            hold(dve, dve_own, n + 1, dve_passed)
            for t in range(T):
                last = dve.bn_aggr(mv[:, s % 2, t, :], st[:, s % 2, t, :])
            last.then_inc(mv_ready, 1)

        def dve_normalise(dve, n, s):
            dve.wait_ge(rstd_ready, n + 1)
            for t in range(TD):
                last = dve.tensor_scalar(xn[s][:, t, :], xn[s][:, t, :], mv[:, s % 2, t, 0:1], rstd[:, s % 2, t:t + 1],
                                         ALU.subtract, ALU.mult)
            last.then_inc(normed, 1)

        def dve_bias(dve, n, s):
            dve.wait_ge(b_psum, n + 1)
            for t in range(WT):
                last = dve.tensor_scalar(bias_t[:, t, :, ds(n * RQ, RQ)].rearrange("p h r -> p r h"),
                                         bp[s % 2][:, :, t, :], -1.0, None, ALU.mult)
            last.then_inc(b_read, 1)

        def pe_transpose(pe, n, s, first):
            if not first:
                pe.wait_ge(z_ready, n * 2 - 2)
            pe.wait_ge(normed, n + 1)
            pe.wait_ge(act_normed, n + 1)
            for k in range(2):
                for t in range(4):
                    last = nc.tensor.transpose(zp[2 * (s % 2) + k][:, t * P:(t + 1) * P], xn[s][:, 4 * k + t, :],
                                               b["ident"][:, :])
                last.then_inc(z_psum, 1)

        def pe_bias(pe, n, s, first):
            if not first:
                pe.wait_ge(b_read, n - 1)
            pe.wait_ge(z_ready, n * 2 + 2)
            for t in range(T):
                last = nc.tensor.matmul(bp[s % 2][:, t // WT, t % WT, :], zt[s % 2][:, t * P:(t + 1) * P], b["wb"][:, :],
                                        start=True, stop=True)
            last.then_inc(b_psum, 1)

        block = ctx.enter_context(nc.Block())

        @block.sync
        def _(sp):
            for s in range(RING):
                sp.dma_start(xt[s][:, :, :], xv[:, s * T:(s + 1) * T, :]).then_inc(loaded[s], 16)
            with sp.Fori(0, NQ // RING - 1) as m:
                for s in range(RING):
                    hold(sp, scaled, m * RING + (s + 1), sp_passed)
                    sp.dma_start(xt[s][:, :, :], xv[:, ds(m * (RING * T) + (RING + s) * T, T), :]).then_inc(loaded[s], 16)

        @block.gpsimd
        def _(pool):
            pool_scale(pool, 0, 0, 0, True)
            pool_scale(pool, 1, 1, 0, True)
            for s in range(2):
                pool_rstd(pool, s, s)
                pool_scale(pool, s + 2, s + 2, 0, True)
            with pool.Fori(1, NQ // RING) as m:
                for s in range(RING):
                    pool_rstd(pool, m * RING + (s - 2), (s - 2) % RING)
                    pool_scale(pool, m * RING + s, s, m, False)
            pool_rstd(pool, NQ - 2, RING - 2)
            pool_rstd(pool, NQ - 1, RING - 1)

        @block.vector
        def _(dve):
            for s in range(RING):
                dve_stats(dve, s, s)
                if s >= 1:
                    dve_normalise(dve, s - 1, s - 1)
                if s >= 3:
                    dve_bias(dve, s - 3, s - 3)
                dve_moments(dve, s, s, s < 2)
            with dve.Fori(1, NQ // RING) as m:
                for s in range(RING):
                    dve_stats(dve, m * RING + s, s)
                    dve_normalise(dve, m * RING + (s - 1), (s - 1) % RING)
                    dve_bias(dve, m * RING + (s - 3), (s - 3) % RING)
                    dve_moments(dve, m * RING + s, s, False)
            dve_normalise(dve, NQ - 1, RING - 1)
            dve_bias(dve, NQ - 3, RING - 3)
            dve_bias(dve, NQ - 2, RING - 2)
            dve_bias(dve, NQ - 1, RING - 1)
            dve.tensor_scalar(negm[:, :], b["mask8"][:, :], NEG, -NEG, ALU.mult, ALU.add).then_inc(neg_ready, 1)
            dve.wait_ge(b_read, NQ)
            for k in range(WT):
                for h in range(HEADS):
                    dve.tensor_copy(bias_q[:, k, h, :].rearrange("p (t m b) -> p t m b", t=WT, b=WB),
                                    bias_t[:, k, h, :].rearrange("p (b t m) -> p t m b", t=WT, b=WB)).then_inc(neg_ready, 1)
            dve.wait_ge(neg_ready, 1)
            for h in range(HEADS):
                dve.wait_ge(tr_ready, h + 1)
                for j in range(WT):
                    last = dve.tensor_tensor(b["nbias"][:, j, h, :], zp[h % 2][:, j * N:(j + 1) * N], negm[:, :], ALU.add)
                last.then_inc(tr_read, 1)
            dve.wait_ge(tr_read, HEADS)
            dve.tensor_scalar(b["nbias"][:, :, :, :], b["nbias"][:, :, :, :], b["fs_inv"][:, 0:1], None, ALU.mult)

        @block.tensor
        def _(pe):
            for s in range(RING):
                pe_transpose(pe, s, s, s < 2)
                if s >= 1:
                    pe_bias(pe, s - 1, s - 1, s - 1 < 2)
            with pe.Fori(1, NQ // RING) as m:
                for s in range(RING):
                    pe_transpose(pe, m * RING + s, s, False)
                    pe_bias(pe, m * RING + (s - 1), (s - 1) % RING, False)
            pe_bias(pe, NQ - 1, RING - 1, False)
            pe.wait_ge(neg_ready, 1 + WT * HEADS)
            for h in range(HEADS):
                if h >= 2:
                    pe.wait_ge(tr_read, h - 1)
                for j in range(WT):
                    for k in range(WT):
                        last = nc.tensor.transpose(zp[h % 2][:, j * N + k * P:j * N + (k + 1) * P],
                                                   bias_q[:, k, h, j * P:(j + 1) * P], b["ident"][:, :])
                last.then_inc(tr_ready, 1)

        @block.scalar
        def _(act):
            def normalise(n, s):
                act.wait_ge(shift_ready, n + 1)
                for t in range(TD, T):
                    last = act.activation(xn[s][:, t, :], xn[s][:, t, :], ACT.Identity, bias=shift[:, s % 2, t:t + 1],
                                          scale=rstd[:, s % 2, t:t + 1])
                last.then_inc(act_normed, 1)

            def copy_out(n, s):
                for k in range(2):
                    act.wait_ge(z_psum, n * 2 + k + 1)
                    act.activation(zt[s][:, k * 512:(k + 1) * 512], zp[2 * s + k][:, :], ACT.Identity,
                                   bias=b["beta"][:, :], scale=b["gamma"][:, :]).then_inc(z_ready, 1)
                act.wait_ge(z_ready, n * 2 + 2)
                act.dma_start(d["znt"][:, ds(n * (T * P), T * P)], zt[s][:, :]).then_inc(stored[s], 16)

            for s in range(RING):
                normalise(s, s)
                if s >= 2:
                    act.wait_ge(stored[s % 2], s // 2 * 16)
                    act.wait_ge(b_psum, s - 1)
                copy_out(s, s % 2)
            with act.Fori(1, NQ // RING) as m:
                for s in range(RING):
                    normalise(m * RING + s, s)
                    act.wait_ge(stored[s % 2], m * (RING // 2 * 16) + s // 2 * 16)
                    act.wait_ge(b_psum, m * RING + (s - 1))
                    copy_out(m * RING + s, s % 2)
            for s in range(2):
                act.wait_ge(stored[s], NQ // 2 * 16)


def attention_stage(nc, d, b):
    xv = [d["x"][0].rearrange("r (b t m) c -> t r m b c", t=WT, m=BW // WT)[t] for t in range(WT)]
    nat = [d["x1"].rearrange("r (b t m) c -> t r m b c", t=WT, m=BW // WT)[t] for t in range(WT)]

    def row_of(v, r):
        return v[r] if isinstance(r, int) else v[ds(r, 1)].squeeze(0)

    halo = [d["x1h"].rearrange("q r m b c -> r (m b) q c")[:, t * P:(t + 1) * P, :, :] for t in range(WT)]
    AHEAD = 4
    PAIRS = 3
    PAIRINGS = ((0, 0), (0, 1), (1, 0), (1, 1))
    with ExitStack() as ctx:
        def sem(name):
            return ctx.enter_context(nc.semaphore(name))

        def sb(name, shape, dt=F32):
            return ctx.enter_context(nc.sbuf_tensor(name, shape, dt))

        def pb(name, shape):
            return ctx.enter_context(nc.psum_tensor(name, shape, F32))

        znt = [sb(f"at_znt{s}", [P, N]) for s in range(2)]
        xin = [sb(f"at_x{s}", [P, WT, C]) for s in range(2)]
        qk = [sb(f"at_qk{s}", [P, 2, 2, 2, N], F16) for s in range(PAIRS)]
        stack = [sb(f"at_stack{s}", [P, 2, HEADS, 2, N], F16) for s in range(PAIRS)]
        gt = [sb(f"at_gate{s}", [P, N]) for s in range(6)]
        v = [sb(f"at_v{s}", [P, WT, C]) for s in range(6)]
        probs = [sb(f"at_p{s}", [P, HEADS, WT, N]) for s in range(2)]
        top = [sb(f"at_top{s}", [P, WT, HEADS]) for s in range(2)]
        tot = [sb(f"at_tot{s}", [P, WT, HEADS]) for s in range(2)]
        rec = [sb(f"at_rec{s}", [P, WT * HEADS]) for s in range(2)]
        rb = [sb(f"at_rb{s}", [P, WT * HEADS, DH]) for s in range(2)]
        pt = [sb(f"at_pt{k}", [P, WT, N]) for k in range(2)]
        g1 = sb("at_g1", [P, N])
        og = [sb(f"at_og{s}", [P, N]) for s in range(2)]
        x1 = [sb(f"at_x1{s}", [P, WT, C]) for s in range(2)]
        dev = sb("at_dev", [P, WT, C])
        sq = sb("at_sq", [P, WT, C])

        s_ps = [pb(f"at_s{k}", [P, WT, N]) for k in range(2)]
        pt_ps = [pb(f"at_ptp{k}", [P, WT, N]) for k in range(2)]
        qk_ps, gv_ps, or_ps = pb("at_qkp", [P, 2, N]), pb("at_gv", [P, 2, N]), pb("at_or", [P, 2, N])
        w_ps = pb("at_w", [P, 2, N])

        znt_in = [sem(f"at_znt_in{s}") for s in range(2)]
        x_in = [sem(f"at_x_in{s}") for s in range(2)]
        stored = [sem(f"at_stored{s}") for s in range(2)]
        split_out = [sem(f"at_split_out{s}") for s in range(PAIRS)]
        stack_in = [sem(f"at_stack_in{s}") for s in range(PAIRS)]
        qk_done, gv_done = sem("at_qk_done"), sem("at_gv_done")
        high_ready, low_ready, g_ready, v_ready = (sem(f"at_{x}_ready") for x in ("high", "low", "g", "v"))
        s_done, s_read, p_ready = sem("at_s_done"), sem("at_s_read"), sem("at_p_ready")
        pt_done, pt_even, pt_odd, o_done = sem("at_pt_done"), sem("at_pt_even"), sem("at_pt_odd"), sem("at_o_done")
        rec_ready, rb_ready, r_done, og_ready = sem("at_rec"), sem("at_rb"), sem("at_r_done"), sem("at_og")
        g1_ready = sem("at_g1_ready")
        w_done, x1_ready, acc_done, pool_own = sem("at_w_done"), sem("at_x1_ready"), sem("at_acc"), sem("at_pool")
        sp_passed, dve_passed = sem("at_spp"), sem("at_dvep")
        STORES = 4

        block = ctx.enter_context(nc.Block())

        def rows(eng, step):
            lead = 4
            body = 6
            turns = (N - AHEAD - lead) // body
            for i in range(lead):
                step(i, i, 0)
            with eng.Fori(0, turns) as m:
                for u in range(body):
                    step(m * body + (lead + u), lead + u, m)
            for i in range(lead + turns * body, N + 2):
                step(i, i, 0)

        def before(i, n):
            return not isinstance(i, int) or i < n

        @block.sync
        def _(sp):
            def load(r, u):
                sp.dma_start(znt[u % 2][:, :], d["znt"][:, ds(r * N, N)]).then_inc(znt_in[u % 2], 16)

            def keep(r, u):
                k = u // 2 % PAIRS
                hold(sp, low_ready, r + 1, sp_passed)
                for h in range(HEADS):
                    sp.dma_start(d["split"][k, :, :, :, h].rearrange("p x a n -> p (x a) n"),
                                 qk[k][h * DH:(h + 1) * DH, :, :, :, :].rearrange("p x a r n -> p (x a) (r n)"))\
                        .then_inc(split_out[k], 16)

            def spread(r, u, t):
                k, turn = u // 2 % PAIRS, u // (2 * PAIRS)
                hold(sp, split_out[k], t * (HEADS * 16) + (turn + 1) * (HEADS * 16), sp_passed)
                if u >= 2 * PAIRS:
                    hold(sp, s_done, r * HEADS - (2 * PAIRS - 1) * HEADS, sp_passed)
                for g, (query, key) in enumerate(PAIRINGS):
                    of = d["split"][k, :, 0, query]
                    size = HEADS * 2 * N
                    both = bass.AP(of.tensor, of.offset, [list(of.ap[0]), [(2 + key - query) * size, 2], [1, size]])
                    sp.dma_start(stack[k][g * DH:(g + 1) * DH].rearrange("p x h r n -> p x (h r n)"), both)\
                        .then_inc(stack_in[k], 16)

            load(0, 0)
            load(1, 1)
            for t in range(2):
                for j in range(WT):
                    sp.dma_start(xin[t][:, j, :], row_of(xv[j], t)).then_inc(x_in[t], 16)
            for r in range(AHEAD):
                sp.wait_ge(gv_done, r + 1)
                load(r + 2, r)
                if r % 2:
                    keep(r, r)
            spread(1, 1, 0)

            def store(r, u):
                s = u % 2
                hold(sp, x1_ready, r + 1, sp_passed)
                for t in range(WT):
                    sp.dma_start(row_of(nat[t], r), x1[s][:, t, :]).then_inc(stored[s], 16)
                    sp.dma_start(row_of(halo[t], r + BH), x1[s][:, t, :].rearrange("p (q c) -> p q c", c=CCH))\
                        .then_inc(stored[s], 16)

            def step(i, u, t):
                if (u + AHEAD) % 2 == 0 and before(i, N - AHEAD + 1):
                    spread(i + AHEAD - 1, u + AHEAD - 1, t)
                if before(i, N - AHEAD):
                    hold(sp, gv_done, i + (AHEAD + 1), sp_passed)
                    if before(i, N - AHEAD - 2):
                        load(i + (AHEAD + 2), u + AHEAD + 2)
                    if (u + AHEAD) % 2:
                        keep(i + AHEAD, u + AHEAD)
                if u >= 2:
                    store(i - 2, u)
                    if before(i, N):
                        for j in range(WT):
                            sp.dma_start(xin[u % 2][:, j, :], row_of(xv[j], i)).then_inc(x_in[u % 2], 16)

            rows(sp, step)
            for s in range(2):
                sp.wait_ge(stored[s], N // 2 * STORES * 16)

        @block.tensor
        def _(pe):
            def project_qk(r, u):
                s = u % 2
                pe.wait_ge(znt_in[s], (r + (2 - s)) * 8)
                queries = znt[s][:, :].rearrange("p (b t m) -> p t m b", t=WT, m=BW // WT)
                if u >= 1:
                    pe.wait_ge(low_ready, r)
                nc.tensor.matmul(qk_ps[:, 0, :], b["wq"][:, :], queries, start=True, stop=True)
                nc.tensor.matmul(qk_ps[:, 1, :], b["wk"][:, :], znt[s][:, :], start=True, stop=True).then_inc(qk_done, 1)

            def project_gv(r, u):
                s = u % 2
                queries = znt[s][:, :].rearrange("p (b t m) -> p t m b", t=WT, m=BW // WT)
                if u >= 1:
                    pe.wait_ge(v_ready, r)
                nc.tensor.matmul(gv_ps[:, 0, :], b["wg"][:, :], queries, start=True, stop=True)
                for t in range(WT):
                    last = nc.tensor.matmul(gv_ps[:, 1, t * P:(t + 1) * P], znt[s][:, t * P:(t + 1) * P], b["wv"][:, :],
                                            start=True, stop=True)
                last.then_inc(gv_done, 1)

            def scores(r, u, h, t):
                k, row = u // 2 % PAIRS, u % 2
                if h == 0:
                    pe.wait_ge(stack_in[k], t * (len(PAIRINGS) * 16) + (u // (2 * PAIRS) + 1) * (len(PAIRINGS) * 16))
                if u >= 1 or h >= 2:
                    pe.wait_ge(s_read, r * HEADS + (h - 1))
                for j in range(WT):
                    last = nc.tensor.matmul(s_ps[h % 2][:, j, :], stack[k][:, 0, h, row, j * P:(j + 1) * P],
                                            stack[k][:, 1, h, row, :], start=True, stop=True)
                last.then_inc(s_done, 1)

            def transposes(r, u, h):
                s = u % 2
                pe.wait_ge(p_ready, r * HEADS + (h + 1))
                if u >= 1 or h >= 2:
                    if h % 2 == 0:
                        pe.wait_ge(pt_even, r * 2 + h // 2)
                    else:
                        pe.wait_ge(pt_odd, r * 2 + h // 2)
                for k in range(WT):
                    for j in range(WT):
                        last = nc.tensor.transpose(pt_ps[h % 2][:, k, j * P:(j + 1) * P],
                                                   probs[s][:, h, j, k * P:(k + 1) * P], b["ident"][:, :])
                last.then_inc(pt_done, 1)

            def values(r, u, h):
                if h == 0:
                    pe.wait_ge(v_ready, r + 1)
                    if u >= 1:
                        pe.wait_ge(og_ready, r)
                if h % 2 == 0:
                    pe.wait_ge(pt_even, r * 2 + (h // 2 + 1))
                else:
                    pe.wait_ge(pt_odd, r * 2 + (h // 2 + 1))
                lo = h * DH
                for k in range(WT):
                    last = nc.tensor.matmul(or_ps[lo:lo + DH, 0, :], v[u % 6][:, k, lo:lo + DH], pt[h % 2][:, k, :],
                                            start=(k == 0), stop=(k == WT - 1), tile_position=(0, lo))
                last.then_inc(o_done, 1)

            def sums(r, u):
                pe.wait_ge(rb_ready, r + 1)
                for j in range(WT):
                    last = nc.tensor.transpose(or_ps[:, 1, j * P:(j + 1) * P],
                                               rb[u % 2][:, j * HEADS:(j + 1) * HEADS, :].rearrange("p h c -> p (h c)"),
                                               b["ident"][:, :])
                last.then_inc(r_done, 1)

            def output(r, u):
                pe.wait_ge(og_ready, r + 1)
                if u >= 1:
                    pe.wait_ge(x1_ready, r)
                for j in range(WT):
                    last = nc.tensor.matmul(w_ps[:, 0, j * P:(j + 1) * P], og[u % 2][:, j * P:(j + 1) * P], b["wo"][:, :],
                                            start=True, stop=True)
                last.then_inc(w_done, 1)

            for r in range(AHEAD):
                project_qk(r, r)
                project_gv(r, r)
            scores(0, 0, 0, 0)

            def step(i, u, t):
                back = u >= 1 and before(i, N + 1)
                for h in range(HEADS):
                    if h < HEADS - 1 and before(i, N):
                        scores(i, u, h + 1, t)
                    if h == HEADS - 1 and before(i, N - 1):
                        scores(i + 1, u + 1, 0, t)
                    if back:
                        transposes(i - 1, u - 1, h)
                        if h >= 1:
                            values(i - 1, u - 1, h - 1)
                    if h == 1 and u >= 2:
                        output(i - 2, u - 2)
                    if h == 0 and before(i, N - AHEAD):
                        project_qk(i + AHEAD, u + AHEAD)
                    if h == 2 and before(i, N - AHEAD):
                        project_gv(i + AHEAD, u + AHEAD)
                if back:
                    values(i - 1, u - 1, HEADS - 1)
                    sums(i - 1, u - 1)

            rows(pe, step)

        @block.vector
        def _(dve):
            def low_part(r, u):
                part = qk[u // 2 % PAIRS][:, :, :, u % 2, :].rearrange("p x a n -> p a x n")
                dve.wait_ge(high_ready, r + 1)
                dve.tensor_tensor(part[:, 1], qk_ps[:, :, :], part[:, 0], ALU.subtract).then_inc(low_ready, 1)

            def value(r, u):
                dve.wait_ge(gv_done, r + 1)
                dve.wait_ge(g_ready, r + 1)
                if u >= 6:
                    dve.wait_ge(o_done, (r - 5) * HEADS)
                dve.tensor_copy(v[u % 6][:, :, :].rearrange("p t c -> p (t c)"), gv_ps[:, 1, :]).then_inc(v_ready, 1)

            def bias_max(r, u, h):
                if u >= 2:
                    dve.wait_ge(pt_done, r * HEADS + (h + 1 - 2 * HEADS))
                hold(dve, s_done, r * HEADS + (h + 1), dve_passed)
                for j in range(WT):
                    last = dve.tensor_tensor_reduce(out=probs[u % 2][:, h, j, :], in0=s_ps[h % 2][:, j, :],
                                                    in1=b["nbias"][:, j, h, :], scale=b["fs"][:, 0:1], scalar=3.0e38,
                                                    op0=ALU.add, op1=ALU.min, accum_out=top[u % 2][:, j, h:h + 1])
                last.then_inc(s_read, 1)

            def copy_pt(r, u, h):
                dve.wait_ge(pt_done, r * HEADS + (h + 1))
                if u >= 1 or h >= 2:
                    dve.wait_ge(o_done, r * HEADS + (h - 1))
                dve.tensor_copy(pt[h % 2][:, :, :], pt_ps[h % 2][:, :, :]).then_inc(pt_odd, 1)

            def reciprocals(r, u):
                dve.wait_ge(p_ready, r * HEADS + HEADS)
                if u >= 2:
                    dve.wait_ge(rb_ready, r - 1)
                dve.reciprocal(rec[u % 2][:, :], tot[u % 2][:, :, :].rearrange("p t h -> p (t h)")).then_inc(rec_ready, 1)

            def gate(r, u):
                dve.wait_ge(r_done, r + 1)
                dve.wait_ge(g_ready, r + 1)
                dve.scalar_tensor_tensor(g1[:, :], gt[u % 6][:, :], 1.0, or_ps[:, 1, :], ALU.add, ALU.mult)\
                    .then_inc(g1_ready, 1)
                dve.wait_ge(g1_ready, r + 1)
                dve.wait_ge(o_done, r * HEADS + HEADS)
                if u >= 2:
                    dve.wait_ge(w_done, r - 1)
                dve.tensor_tensor(og[u % 2][:, :], g1[:, :], or_ps[:, 0, :], ALU.mult).then_inc(og_ready, 1)

            def residual(r, u):
                s = u % 2
                dve.wait_ge(w_done, r + 1)
                dve.wait_ge(x_in[s], (r + (2 - s)) * 16)
                if u >= 2:
                    dve.wait_ge(stored[s], (r - s) * (8 * STORES))
                    dve.wait_ge(acc_done, r - 1)
                dve.tensor_tensor(x1[s][:, :, :].rearrange("p t c -> p (t c)"), w_ps[:, 0, :],
                                  xin[s][:, :, :].rearrange("p t c -> p (t c)"), ALU.add).then_inc(x1_ready, 1)

            for r in range(AHEAD):
                low_part(r, r)
                value(r, r)

            def step(i, u, t):
                back = u >= 1 and before(i, N + 1)
                for h in range(HEADS):
                    if before(i, N):
                        bias_max(i, u, h)
                    if h == 0 and u >= 2:
                        gate(i - 2, u - 2)
                    if h == 0 and back:
                        reciprocals(i - 1, u - 1)
                    if h == 1 and before(i, N - AHEAD):
                        low_part(i + AHEAD, u + AHEAD)
                    if back and h % 2:
                        copy_pt(i - 1, u - 1, h)
                    if h == 2 and u >= 2:
                        residual(i - 2, u - 2)
                if before(i, N - AHEAD):
                    value(i + AHEAD, u + AHEAD)

            rows(dve, step)

        @block.scalar
        def _(act):
            def high_part(r, u):
                act.wait_ge(qk_done, r + 1)
                if u >= 2 * PAIRS:
                    act.wait_ge(s_done, (r - (2 * PAIRS - 1)) * HEADS)
                act.activation(qk[u // 2 % PAIRS][:, :, 0, u % 2, :], qk_ps[:, :, :], ACT.Copy).then_inc(high_ready, 1)

            def gate(r, u):
                act.wait_ge(gv_done, r + 1)
                if u >= 6:
                    act.wait_ge(g1_ready, r - 5)
                act.activation(gt[u % 6][:, :], gv_ps[:, 0, :], ACT.Tanh, scale=0.5).then_inc(g_ready, 1)

            def exponentials(r, u, h):
                act.wait_ge(s_read, r * HEADS + (h + 1))
                if u >= 2 and h == 0:
                    act.wait_ge(rec_ready, r - 1)
                for j in range(WT):
                    row = probs[u % 2][:, h, j, :]
                    last = act.activation(row, row, ACT.Exp, scale=-1.0, bias=top[u % 2][:, j, h:h + 1],
                                          accum_out=tot[u % 2][:, j, h:h + 1])
                last.then_inc(p_ready, 1)

            def copy_pt(r, u, h):
                act.wait_ge(pt_done, r * HEADS + (h + 1))
                if u >= 1 or h >= 2:
                    act.wait_ge(o_done, r * HEADS + (h - 1))
                act.activation(pt[h % 2][:, :, :], pt_ps[h % 2][:, :, :], ACT.Copy).then_inc(pt_even, 1)

            for r in range(AHEAD):
                high_part(r, r)
                gate(r, r)

            def step(i, u, t):
                back = u >= 1 and before(i, N + 1)
                for h in range(HEADS):
                    if back and h % 2 == 0:
                        copy_pt(i - 1, u - 1, h)
                    if before(i, N):
                        exponentials(i, u, h)
                    if h == 0 and before(i, N - AHEAD):
                        high_part(i + AHEAD, u + AHEAD)
                    if h == 2 and before(i, N - AHEAD):
                        gate(i + AHEAD, u + AHEAD)

            rows(act, step)

        @block.gpsimd
        def _(pool):
            def spread(r, u):
                pool.wait_ge(rec_ready, r + 1)
                if u >= 2:
                    pool.wait_ge(r_done, r - 1)
                pool.tensor_tensor(rb[u % 2][:, :, :], rec[u % 2][:, :].unsqueeze(2).to_broadcast([P, WT * HEADS, DH]),
                                   b["half"][:, :].rearrange("p (a c) -> p a c", c=DH), ALU.mult).then_inc(rb_ready, 1)

            def accumulate(r, u):
                flat_dev, flat_sq = (x[:, :, :].rearrange("p t c -> p (t c)") for x in (dev, sq))
                pool.wait_ge(x1_ready, r + 1)
                if u >= 1:
                    pool.wait_ge(pool_own, r * 3)
                pool.tensor_tensor(dev[:, :, :], x1[u % 2][:, :, :], bcast_rows(b["mean0"][:, :], WT), ALU.subtract)\
                    .then_inc(acc_done, 1)
                pool.wait_ge(acc_done, r + 1)
                pool.tensor_tensor(sq[:, :, :], dev[:, :, :], dev[:, :, :], ALU.mult).then_inc(pool_own, 1)
                pool.tensor_tensor(b["acc"][:, 0, :], b["acc"][:, 0, :], flat_dev, ALU.add).then_inc(pool_own, 1)
                pool.wait_ge(pool_own, r * 3 + 2)
                pool.tensor_tensor(b["acc"][:, 1, :], b["acc"][:, 1, :], flat_sq, ALU.add).then_inc(pool_own, 1)

            def step(i, u, t):
                if u >= 1 and before(i, N + 1):
                    spread(i - 1, u - 1)
                if u >= 2:
                    accumulate(i - 2, u - 2)

            rows(pool, step)
            pool.wait_ge(pool_own, N * 3)


def corner_stage(nc, d, b):
    K2 = TAPS * TAPS
    S = 2 * TAPS - 1
    SC = 1.0 / (N * N // P * GC)
    with ExitStack() as ctx:
        def sem(name):
            return ctx.enter_context(nc.semaphore(name))

        def sb(name, shape):
            return ctx.enter_context(nc.sbuf_tensor(name, shape, F32))

        sums = sb("co_sums", [P, 2, C])
        gsum = sb("co_gsum", [P, 2, G])
        tot = sb("co_tot", [P, 2, G])
        rs = sb("co_rs", [P, 4, G])
        m0 = sb("co_m0", [P, G])
        patch = sb("co_patch", [K2, K2, C])
        kern = [sb(f"co_kern{i}", [K2, K2, C]) for i in range(3)]
        conv = sb("co_conv", [K2, 3, C])
        at = sb("co_at", [K2, C])
        x1c = sb("co_x1", [K2, C])
        w = [sb(f"co_w{i}", [K2, C]) for i in range(8)]
        ht = sb("co_ht", [C, K2])
        ps = ctx.enter_context(nc.psum_tensor("co_ps", [P, 2, G], F32))
        tp = ctx.enter_context(nc.psum_tensor("co_tp", [C, K2], F32))
        op = ctx.enter_context(nc.psum_tensor("co_op", [K2, C], F32))
        halo_done, square_done, patch_in, kern_in, small_in = (sem(f"co_{x}") for x in
                                                               ("halo", "square", "patch", "kern", "small"))
        chain, gsum_ready, mean_ready, var_ready, std_ready = (sem(f"co_{x}") for x in
                                                               ("chain", "gsumr", "meanr", "varr", "stdr"))
        conv_ready, gates, b_ready, act_own, sp_ready, h_ready, t_done, ht_ready, o_done = (
            sem(f"co_{x}") for x in ("convr", "gates", "br", "acto", "spr", "hr", "td", "htr", "od"))
        block = ctx.enter_context(nc.Block())

        @block.sync
        def _(sp):
            sq = d["square"]
            for dst, src, n in ((0, N - R - R, R + R), (R + R, 0, R + R + 1)):
                for dst2, src2, n2 in ((0, N - R - R, R + R), (R + R, 0, R + R + 1)):
                    sp.dma_start(sq[dst:dst + n, dst2:dst2 + n2, :], d["x1"][src:src + n, src2:src2 + n2, :])\
                        .then_inc(square_done, 16)
            for i in range(3):
                sp.dma_start(kern[i][:, :, :].rearrange("p t c -> p (t c)"), d["taps"][i].rearrange("t c -> (t c)")
                             .partition_broadcast(K2)).then_inc(kern_in, 16)
            sp.dma_start(at[:, :], d["kA"]).then_inc(small_in, 16)
            sp.wait_ge(square_done, 64)
            sp.dma_start(x1c[:, :], sq[R:R + TAPS, R:R + TAPS, :]).then_inc(small_in, 16)
            for a in range(TAPS):
                rows = sq[a:a + TAPS].rearrange("t u c -> t (u c)")
                window = bass.AP(rows.tensor, rows.offset, [[C, TAPS], [S * C, TAPS], [1, TAPS * C]])
                sp.dma_start(patch[a * TAPS:(a + 1) * TAPS, :, :], window).then_inc(patch_in, 16)
            sp.dma_start(d["x1h"][:, 0:BH], d["x1h"][:, N:N + BH]).then_inc(halo_done, 16)
            sp.dma_start(d["x1h"][:, N + BH:HPAD], d["x1h"][:, BH:2 * BH]).then_inc(halo_done, 16)
            sp.wait_ge(halo_done, 32)

        @block.vector
        def _(dve):
            ch = Chain(dve, chain)
            ch.step(dve.tensor_tensor(sums[:, :, :], b["acc"][:, :, 0:C], b["acc"][:, :, C:2 * C], ALU.add))
            dve.tensor_reduce(gsum[:, :, :], sums[:, :, :].rearrange("p a (g c) -> p a g c", c=GC), AX.X, ALU.add)\
                .then_inc(gsum_ready, 1)
            dve.wait_ge(mean_ready, 1)
            ch.step(dve.tensor_scalar(tot[:, :, :], ps[:, :, :], SC, None, ALU.mult))
            ch.step(dve.tensor_tensor(rs[:, 0, :], tot[:, 0, :], tot[:, 0, :], ALU.mult))
            ch.step(dve.tensor_tensor(rs[:, 1, :], tot[:, 1, :], rs[:, 0, :], ALU.subtract))
            dve.tensor_scalar(rs[:, 2, :], rs[:, 1, :], GN_EPS, None, ALU.add).then_inc(var_ready, 1)
            ch.step(dve.tensor_tensor(m0[:, :], tot[:, 0, :], b["mean0"][:, :].rearrange("p (g c) -> p g c", c=GC)[:, :, 0],
                                      ALU.add))
            dve.wait_ge(std_ready, 1)
            ch.step(dve.reciprocal(rs[:, 0, :], rs[:, 3, :]))
            for t, src in ((b["gn_a"], rs[:, 0, :]), (b["mean0"], m0[:, :])):
                ch.step(dve.tensor_scalar(t[:, :].rearrange("p (g c) -> p g c", c=GC),
                                          src.unsqueeze(2).to_broadcast([P, G, GC]), 1.0, None, ALU.mult))
            ch.step(dve.tensor_scalar(b["xscale"][:, :], b["gn_a"][:, :], XSCALE, None, ALU.mult))
            dve.wait_ge(patch_in, 16 * TAPS)
            ch.step(dve.tensor_tensor(patch[:, :, :], patch[:, :, :], bcast_rows(b["mean0"][0:K2, :], K2), ALU.subtract))
            ch.step(dve.tensor_tensor(patch[:, :, :], patch[:, :, :], bcast_rows(b["gn_a"][0:K2, :], K2), ALU.mult))
            dve.wait_ge(kern_in, 48)
            for i in range(3):
                ch.step(dve.tensor_tensor(kern[i][:, :, :], kern[i][:, :, :], patch[:, :, :], ALU.mult))
                dve.tensor_reduce(conv[:, i, :], kern[i][:, :, :].rearrange("p t c -> p c t"), AX.X, ALU.add)\
                    .then_inc(conv_ready, 1)
            dve.wait_ge(gates, 2)
            dve.wait_ge(small_in, 32)
            ch.step(dve.tensor_tensor(w[2][:, :], at[:, :], w[0][:, :], ALU.mult))
            dve.tensor_tensor(w[3][:, :], conv[:, 2, :], w[1][:, :], ALU.mult).then_inc(b_ready, 1)
            dve.wait_ge(sp_ready, 3)
            ch.step(dve.scalar_tensor_tensor(w[6][:, :], w[3][:, :], 0.0, w[6][:, :], ALU.max, ALU.add))
            ch.step(dve.tensor_scalar(w[6][:, :], w[6][:, :], SP_EPS, None, ALU.add))
            ch.step(dve.tensor_tensor(w[6][:, :], w[6][:, :], w[4][:, :], ALU.mult))
            for i in range(3):
                ch.step(dve.scalar_tensor_tensor(w[6][:, :], w[5][:, :], 1.0, w[6][:, :], ALU.add, ALU.mult))
                if i < 2:
                    ch.step(dve.tensor_tensor(w[5][:, :], w[5][:, :], w[5][:, :], ALU.mult))
            ch.step(dve.tensor_copy(w[7][:, :], w[6][:, :]))
            dve.tensor_tensor(x1c[:, :], x1c[:, :], b["bout"][0:K2, :], ALU.add).then_inc(h_ready, 1)
            dve.wait_ge(t_done, 1)
            dve.tensor_copy(ht[:, :], tp[:, :]).then_inc(ht_ready, 1)
            dve.wait_ge(o_done, 1)
            ch.step(dve.tensor_tensor(b["corner"][:, :], op[:, :], x1c[:, :], ALU.add))

        @block.scalar
        def _(act):
            act.wait_ge(var_ready, 1)
            act.activation(rs[:, 3, :], rs[:, 2, :], ACT.Sqrt).then_inc(std_ready, 1)
            for i in range(2):
                act.wait_ge(conv_ready, i + 1)
                act.activation(w[i][:, :], conv[:, i, :], ACT.Sigmoid).then_inc(gates, 1)
            act.wait_ge(b_ready, 1)
            act.activation(w[4][:, :], w[2][:, :], ACT.Sigmoid).then_inc(sp_ready, 1)
            act.activation(w[5][:, :], w[2][:, :], ACT.Sigmoid, scale=-1.0).then_inc(sp_ready, 1)
            act.activation(w[6][:, :], w[3][:, :], ACT.Abs).then_inc(act_own, 1)
            act.wait_ge(act_own, 1)
            act.activation(w[6][:, :], w[6][:, :], ACT.Exp, scale=-1.0).then_inc(act_own, 1)
            act.wait_ge(act_own, 2)
            act.activation(w[6][:, :], w[6][:, :], ACT.Ln, bias=1.0).then_inc(sp_ready, 1)

        @block.tensor
        def _(pe):
            pe.wait_ge(gsum_ready, 1)
            nc.tensor.matmul(ps[:, :, :].rearrange("p a g -> p (a g)"), b["mean_w"][:, :],
                             gsum[:, :, :].rearrange("p a g -> p (a g)"), start=True, stop=True).then_inc(mean_ready, 1)
            pe.wait_ge(h_ready, 1)
            nc.tensor.transpose(tp[:, :], w[7][:, :], b["ident"][0:K2, 0:K2]).then_inc(t_done, 1)
            pe.wait_ge(ht_ready, 1)
            nc.tensor.matmul(op[:, :], ht[:, :], b["w2"][:, :], start=True, stop=True).then_inc(o_done, 1)


def conv_stage(nc, d, b):
    TG = 8
    TGS = CCH // TG
    EG = 4
    SUB = 16
    SUBS = CCH // SUB
    EGS = SUB // EG
    XR = SROWS + 2
    XP = 2
    PIECES = XR // XP
    STEPS = NCC * STRIPS
    rows3 = ((R, BH, 0, 1), (0, R, BH - R, 0), (R + BH, R, 0, 2))
    with ExitStack() as ctx:
        def sem(name):
            return ctx.enter_context(nc.semaphore(name))

        def sb(name, shape, dt=F32):
            return ctx.enter_context(nc.sbuf_tensor(name, shape, dt))

        raw = [sb(f"cv_raw{j}", [P, XP, WB, CCH]) for j in range(PIECES)]
        xc = [sb(f"cv_xc{s}", [P, 2, XR, WB, CCH], F16) for s in range(2)]
        xl = [sb(f"cv_xl{s}", [P, 2, XR, WB, CCH], F16) for s in range(2)]
        tk = [sb(f"cv_tk{g}", [P, TG, 2, WROWS, 2, PITCH], F16) for g in range(TGS)]
        h = [sb(f"cv_h{s}", [P, SUB, P]) for s in range(2)]
        soft = sb("cv_soft", [P, SUB, P])
        cp = [ctx.enter_context(nc.psum_tensor(f"cv_cp{s}", [P, EG, BH, 2, BW], F32)) for s in range(EGS)]

        raw_in = [sem(f"cv_raw_in{j}") for j in range(PIECES)]
        xl_in = [sem(f"cv_xl_in{s}") for s in range(2)]
        tk_in = [sem(f"cv_tk_in{g}") for g in range(TGS)]
        stored = [sem(f"cv_stored{s}") for s in range(2)]
        centred, scaled, high_ready, low_ready, zeroed = (sem(f"cv_{x}") for x in ("cen", "sca", "hi", "lo", "zero"))
        group_done, group_used = sem("cv_group"), sem("cv_gused")
        GPS = CCH // EG
        gate_done, mag_ready, soft_own, soft_ready, h_ready = (sem(f"cv_{x}") for x in
                                                               ("gate", "mag", "softo", "softr", "hr"))
        sp_passed, pool_passed, act_passed = sem("cv_spp"), sem("cv_poolp"), sem("cv_actp")
        SIDES = 4 * R
        SPLIT_BEFORE = {0: (0, 1), 1: (2,), 2: (3,), 3: (4,)}
        block = ctx.enter_context(nc.Block())

        @block.sync
        def _(sp):
            sp.sem_inc(low_ready, PIECES)

            def load(q, s, j):
                hold(sp, low_ready, q * (STRIPS * PIECES) + (s * PIECES + j + 1), sp_passed)
                v = d["x1h"][ds(q + s // STRIPS, 1), (s % STRIPS * SROWS + j * XP) * BH:(s % STRIPS * SROWS + (j + 1) * XP) * BH].squeeze(0)
                v = v.rearrange("(a h) m b c -> h m a (b c)", h=BH).rearrange("h m a x -> (h m) a x")
                sp.dma_start(raw[j][:, :, :, :].rearrange("p a b c -> p a (b c)"), v).then_inc(raw_in[j], 16)

            def sides(q, s):
                k = s % 2
                sp.wait_ge(zeroed, 1 if k == 0 else TGS + 2)
                hold(sp, low_ready, q * (STRIPS * PIECES) + ((s + 2) * PIECES), sp_passed)
                for r in range(R):
                    for m, far, near in ((r, (0, WB - 1, 1, WB), (WB - 1, WB, 0, 1)),
                                         (BW - R + r, (1, WB, 0, WB - 1), (0, 1, WB - 1, WB))):
                        to = xl[k][m:m + (BH - 1) * BW + 1:BW].rearrange("p h a b c -> p (h a) b c")
                        of = xc[k][m:m + (BH - 1) * BW + 1:BW].rearrange("p h a b c -> p (h a) b c")
                        for t0, t1, f0, f1 in (far, near):
                            sp.dma_start(to[:, :, t0:t1, :].rearrange("p a b c -> p a (b c)"),
                                         of[:, :, f0:f1, :].rearrange("p a b c -> p a (b c)")).then_inc(xl_in[k], 16)

            def kernels(q, g):
                sp.wait_ge(zeroed, g + 2)
                hold(sp, group_done, q * (STRIPS * GPS) + (g + 1) * (TG // EG), sp_passed)
                for hm in range(BH):
                    taps = bass.AP(d["flat"].tensor, q * (CCH * 2 * FLAT) + g * TG * 2 * FLAT,
                                   [[1, BW], [FLAT, TG * 2], [1, TAPROWS]])
                    sp.dma_start(tk[g][hm * BW:(hm + 1) * BW, :, :, BH - 1 - hm:BH - 1 - hm + TAPS]
                                 .rearrange("p c h r k u -> p (c h) (r k u)"), taps).then_inc(tk_in[g], 16)

            sp.sem_inc(group_done, GPS)
            def chunk(q, last):
                for s in range(STRIPS):
                    if not (last and s == STRIPS - 1):
                        for j in range(PIECES):
                            load(q, s + 1, j)
                            if s == 0 and j == 1:
                                kernels(q, 0)
                    sides(q, s)
                    if s == 0:
                        for g in range(1, TGS):
                            kernels(q, g)

            for j in range(PIECES):
                load(0, 0, j)
            with sp.Fori(0, NCC - 1) as q:
                chunk(q, False)
            chunk(NCC - 1, True)

        @block.gpsimd
        def _(pool):
            with pool.Fori(0, NCC) as q:
                mean, scale = (b[name][:, ds(q * CCH, CCH)].unsqueeze(1).to_broadcast([P, XP * WB, CCH])
                               for name in ("mean0", "xscale"))
                with pool.Fori(0, STRIPS) as m:
                    for j in range(PIECES):
                        flat = raw[j][:, :, :, :].rearrange("p a b c -> p (a b) c")
                        hold(pool, raw_in[j], q * (STRIPS * 16) + (m * 16 + 16), pool_passed)
                        pool.tensor_tensor(flat, flat, mean, ALU.subtract).then_inc(centred, 1)
                        hold(pool, centred, q * (STRIPS * PIECES) + (m * PIECES + (j + 1)), pool_passed)
                        pool.tensor_tensor(flat, flat, scale, ALU.mult).then_inc(scaled, 1)

        @block.tensor
        def _(pe):
            def products(k, cl, out):
                t = tk[cl // TG][:, cl % TG]
                last = None
                for high, parts in ((0, (0, 1)), (1, (0,))):
                    for mr, nr, orow, arow in rows3:
                        for side, x in enumerate((xc[k], xl[k])):
                            blocks = x[:, high, arow:arow + SROWS, :, cl].rearrange("p a b -> p (a b)")
                            for part in parts:
                                taps = t[:, part, mr:mr + nr].rearrange("p r k u -> p (r k) u")
                                to = out[:, orow:orow + nr].rearrange("p r k u -> p (r k) u")
                                if side:
                                    taps = pair(taps[:, :, 0:R], R + BW)
                                    to = pair(to[:, :, BW - R:BW], R - BW)
                                else:
                                    taps = taps[:, :, R:R + BW]
                                last = nc.tensor.matmul(to, blocks, taps, start=last is None,
                                                        stop=(high == 1 and arow == 2 and side == 1))
                return last

            pe.sem_inc(group_used, EGS)
            with pe.Fori(0, NCC) as q:
                with pe.Fori(0, STRIPS // 2) as m:
                    for k in range(2):
                        pe.wait_ge(low_ready, q * (STRIPS * PIECES) + (m * (2 * PIECES) + (k + 2) * PIECES))
                        pe.wait_ge(xl_in[k], q * (STRIPS // 2 * SIDES * 16) + (m * (SIDES * 16) + SIDES * 16))
                        for cl in range(CCH):
                            g = cl // EG
                            if cl % TG == 0:
                                pe.wait_ge(tk_in[cl // TG], q * (BH * 16) + BH * 16)
                            if cl % EG == 0:
                                pe.wait_ge(group_used, q * (STRIPS * GPS) + (m * (2 * GPS) + (k * GPS + g + 1)))
                            last = products(k, cl, cp[g % EGS][:, cl % EG])
                            if cl % EG == EG - 1:
                                last.then_inc(group_done, 1)

        def split(eng, m, k, j, n):
            i = (k + 1) * PIECES + j
            x = xc[(k + 1) % 2][:, :, j * XP:(j + 1) * XP]
            of = raw[j][:, :, :, :]
            if n == "high":
                if j == 0:
                    hold(eng, group_done, m * (2 * GPS) + (k + 1) * GPS, act_passed)
                hold(eng, scaled, m * (2 * PIECES) + (i + 1), act_passed)
                eng.activation(x[:, 0], of, ACT.Copy).then_inc(high_ready, 1)
            else:
                eng.wait_ge(high_ready, m * (2 * PIECES) + (i + 1))
                eng.tensor_tensor(x[:, 1], of, x[:, 0], ALU.subtract).then_inc(low_ready, 1)

        @block.scalar
        def _(act):
            def gate(m, k, g):
                if g % EGS == 0:
                    act.wait_ge(stored[g // EGS], m * (2 * 16) + (k + 1) * 16)
                act.wait_ge(group_done, m * (2 * GPS) + ((k + 1) * GPS + g + 1))
                act.activation(h[g // EGS][:, g % EGS * EG:(g % EGS + 1) * EG, :].rearrange("p c (a b) -> p c a b", b=BW),
                               cp[g % EGS][:, :, :, 0, :], ACT.Sigmoid,
                               scale=b["kscale"][:, 0:1]).then_inc(gate_done, 1)

            def logarithm(m, k, v):
                n = m * (2 * SUBS) + (k * SUBS + v)
                act.wait_ge(mag_ready, n + 1)
                act.activation(soft[:, :, :], soft[:, :, :], ACT.Exp, scale=-1.0).then_inc(soft_own, 1)
                act.wait_ge(soft_own, n + 1)
                act.activation(soft[:, :, :], soft[:, :, :], ACT.Ln, bias=1.0).then_inc(soft_ready, 1)

            def store(n, m, k, v):
                act.wait_ge(h_ready, m * (2 * SUBS) + (k * SUBS + v + 1))
                act.dma_start(d["h"][n, :, v * SUB:(v + 1) * SUB, :] if isinstance(n, int) else
                              d["h"][ds(n, 1), :, v * SUB:(v + 1) * SUB, :].squeeze(0), h[v][:, :, :]).then_inc(stored[v], 16)

            def steps(m, last):
                for k in range(2):
                    more = not (last and k == 1)
                    for g in range(GPS):
                        if more:
                            for j in SPLIT_BEFORE.get(g, ()):
                                split(act, m, k, j, "high")
                        gate(m, k, g)
                        if g % EGS == EGS - 1:
                            logarithm(m, k, g // EGS)
                        if g == EGS + 1:
                            store(m * 2 + k, m, k, 0)
                        if g == 1 and k == 1:
                            store(m * 2, m, 0, 1)
                        if g == 1 and k == 0 and not (isinstance(m, int) and m == 0):
                            store(m * 2 - 1, m - 1, 1, 1)
                if last:
                    store(m * 2 + 1, m, 1, 1)

            for s in range(2):
                act.sem_inc(stored[s], 16)
            for j in range(PIECES):
                split(act, 0, -1, j, "high")
            steps(0, False)
            with act.Fori(1, STEPS // 2 - 1) as m:
                steps(m, False)
            steps(STEPS // 2 - 1, True)
            for s in range(2):
                act.wait_ge(stored[s], STEPS * 16 + 16)

        @block.vector
        def _(dve):
            def hidden(m, k, g):
                dve.wait_ge(gate_done, m * (2 * GPS) + (k * GPS + g + 1))
                part = h[g // EGS][:, g % EGS * EG:(g % EGS + 1) * EG, :].rearrange("p c (a b) -> p c a b", b=BW)
                dve.scalar_tensor_tensor(part, cp[g % EGS][:, :, :, 1, :],
                                         b["kscale"][:, 1:2], part, ALU.mult, ALU.mult).then_inc(group_used, 1)

            def magnitude(m, k, v):
                n = m * (2 * SUBS) + (k * SUBS + v)
                dve.wait_ge(group_used, m * (2 * GPS) + (k * GPS + (v + 1) * EGS + EGS))
                if not (isinstance(n, int) and n == 0):
                    dve.wait_ge(h_ready, n)
                dve.scalar_tensor_tensor(soft[:, :, :], h[v][:, :, :], -1.0, h[v][:, :, :], ALU.mult, ALU.max)\
                    .then_inc(mag_ready, 1)

            def softplus(m, k, v):
                dve.wait_ge(soft_ready, m * (2 * SUBS) + (k * SUBS + v + 1))
                dve.scalar_tensor_tensor(h[v][:, :, :], h[v][:, :, :], 0.0, soft[:, :, :], ALU.max, ALU.add)\
                    .then_inc(h_ready, 1)

            def steps(m, last):
                for k in range(2):
                    more = not (last and k == 1)
                    for g in range(GPS):
                        if more:
                            for j in SPLIT_BEFORE.get(g, ()):
                                split(dve, m, k, j, "low")
                        hidden(m, k, g)
                        if g % EGS == EGS - 1:
                            magnitude(m, k, g // EGS)
                            softplus(m, k, g // EGS)

            dve.memset(xl[0][:, :, :, :, :], 0.0).then_inc(zeroed, 1)
            zeros_before = {0: (0,), 2: (1,)}
            for j in range(PIECES):
                for g in zeros_before.get(j, ()):
                    dve.memset(tk[g][:, :, :, :, :, :], 0.0).then_inc(zeroed, 1)
                split(dve, 0, -1, j, "low")
            for g in range(2, TGS):
                dve.memset(tk[g][:, :, :, :, :, :], 0.0).then_inc(zeroed, 1)
            dve.memset(xl[1][:, :, :, :, :], 0.0).then_inc(zeroed, 1)
            steps(0, False)
            with dve.Fori(1, STEPS // 2 - 1) as m:
                steps(m, False)
            steps(STEPS // 2 - 1, True)


def output_stage(nc, d, b):
    QW = 4
    STEPS = P // QW
    RES = 8
    scan = 1.0 - 0.5 ** 8
    with ExitStack() as ctx:
        def sem(name):
            return ctx.enter_context(nc.semaphore(name))

        def sb(name, shape):
            return ctx.enter_context(nc.sbuf_tensor(name, shape, F32))

        h = [sb(f"ou_h{s}", [P, C, P]) for s in range(2)]
        ht = [sb(f"ou_ht{s}", [P, QW * P]) for s in range(2)]
        res = [sb(f"ou_res{s}", [P, QW, C]) for s in range(RES)]
        eps = sb("ou_eps", [P, 1])
        tp = [ctx.enter_context(nc.psum_tensor(f"ou_tp{s}", [P, QW * P], F32)) for s in range(2)]
        op = [ctx.enter_context(nc.psum_tensor(f"ou_op{s}", [P, QW * C], F32)) for s in range(2)]
        h_in = [sem(f"ou_h_in{s}") for s in range(2)]
        res_in = [sem(f"ou_res_in{s}") for s in range(RES)]
        res_free = [sem(f"ou_res_free{s}") for s in range(RES)]
        t_done, ht_ready, o_done, o_ready, biased = (sem(f"ou_{x}") for x in ("t", "htr", "o", "or", "bia"))
        eps_ready, corner_out = sem("ou_epsr"), sem("ou_corner")
        sp_passed, pool_passed = sem("ou_spp"), sem("ou_poolp")
        block = ctx.enter_context(nc.Block())

        def res_view(t, s, k):
            hm, wm = BH - 1 - k // (BW // QW), BW - QW - (k % (BW // QW)) * QW
            v = t.rearrange("(i h) (j w) c -> h i j w c", h=BH, w=BW)[hm]
            return v[ds(s * SROWS, SROWS), :, wm:wm + QW, :].rearrange("i j w c -> i j (w c)")

        @block.sync
        def _(sp):
            for r in range(RES):
                sp.sem_inc(res_free[r], 16)
            with sp.Fori(0, STRIPS // 2) as m:
                def load(i):
                    k = i % STEPS
                    hold(sp, res_free[k % RES], m * (2 * STEPS // RES * 16) + (i // RES + 1) * 16, sp_passed)
                    sp.dma_start(res[k % RES][:, :, :].rearrange("p w c -> p (w c)"), res_view(d["x1"], m * 2 + i // STEPS, k))\
                        .then_inc(res_in[k % RES], 16)

                for i in range(RES // 2):
                    load(i)
                for i in range(2 * STEPS):
                    if i + RES // 2 < 2 * STEPS:
                        load(i + RES // 2)
                    hold(sp, o_ready, m * (2 * STEPS) + (i + 1), sp_passed)
                    sp.dma_start(res_view(d["out"][0], m * 2 + i // STEPS, i % STEPS),
                                 res[i % RES][:, :, :].rearrange("p w c -> p (w c)")).then_inc(res_free[i % RES], 16)
            for r in range(RES):
                sp.wait_ge(res_free[r], (STRIPS * STEPS // RES + 1) * 16)
            for a0, na, h0 in ((0, R, N - R), (R, R + 1, 0)):
                for a in range(na):
                    for c0, ncol, w0 in ((0, R, N - R), (R, R + 1, 0)):
                        p0 = (a0 + a) * TAPS + c0
                        sp.dma_start(d["out"][0, h0 + a, w0:w0 + ncol, :], b["corner"][p0:p0 + ncol, :])\
                            .then_inc(corner_out, 16)
            sp.wait_ge(corner_out, 2 * TAPS * 16)

        @block.gpsimd
        def _(pool):
            pool.memset(eps[:, :], scan * SP_EPS).then_inc(eps_ready, 1)
            with pool.Fori(0, STRIPS // 2) as m:
                for i in range(2 * STEPS):
                    r = res[i % RES]
                    hold(pool, res_in[i % RES], m * (2 * STEPS // RES * 16) + (i // RES + 1) * 16, pool_passed)
                    pool.tensor_tensor(r[:, :, :], r[:, :, :], bcast_rows(b["bout"][:, :], QW), ALU.add).then_inc(biased, 1)

        @block.tensor
        def _(pe):
            with pe.Fori(0, STRIPS // 2) as m:
                base = m * (2 * STEPS)

                def project(i):
                    pe.wait_ge(ht_ready, base + (i + 1))
                    if i >= 2:
                        pe.wait_ge(o_ready, base + (i - 1))
                    for j in range(QW):
                        last = nc.tensor.matmul(op[i % 2][:, (QW - 1 - j) * C:(QW - j) * C],
                                                ht[i % 2][:, j * P:(j + 1) * P], b["w2"][:, :], start=True, stop=True)
                    last.then_inc(o_done, 1)

                for i in range(2 * STEPS):
                    if i % STEPS == 0:
                        pe.wait_ge(h_in[i // STEPS], m * (NCC * 16) + NCC * 16)
                    if i >= 2:
                        pe.wait_ge(ht_ready, base + (i - 1))
                    for j in range(QW):
                        last = nc.tensor.transpose(tp[i % 2][:, j * P:(j + 1) * P],
                                                   h[i // STEPS][:, :, i % STEPS * QW + j], b["ident"][:, :])
                    last.then_inc(t_done, 1)
                    if i >= 1:
                        project(i - 1)
                project(2 * STEPS - 1)
                pe.wait_ge(o_ready, base + 2 * STEPS)

        @block.scalar
        def _(act):
            def load(n, s):
                for q in range(NCC):
                    act.dma_start(h[s][:, q * CCH:(q + 1) * CCH, :], d["h"][ds(n + q * STRIPS, 1)].squeeze(0))\
                        .then_inc(h_in[s], 16)

            def steps(m, more):
                for i in range(2 * STEPS):
                    act.wait_ge(t_done, m * (2 * STEPS) + (i + 1))
                    if i >= 2:
                        act.wait_ge(o_done, m * (2 * STEPS) + (i - 1))
                    act.activation(ht[i % 2][:, :], tp[i % 2][:, :], ACT.Identity, scale=scan, bias=eps[:, :])\
                        .then_inc(ht_ready, 1)
                    if more and i % STEPS == STEPS - 1:
                        load(m * 2 + (2 + i // STEPS), i // STEPS)

            for s in range(2):
                load(s, s)
            act.wait_ge(eps_ready, 1)
            with act.Fori(0, STRIPS // 2 - 1) as m:
                steps(m, True)
            steps(STRIPS // 2 - 1, False)

        @block.vector
        def _(dve):
            with dve.Fori(0, STRIPS // 2) as m:
                for i in range(2 * STEPS):
                    r = res[i % RES][:, :, :].rearrange("p w c -> p (w c)")
                    dve.wait_ge(biased, m * (2 * STEPS) + (i + 1))
                    dve.wait_ge(o_done, m * (2 * STEPS) + (i + 1))
                    dve.tensor_tensor(r, r, op[i % 2][:, :], ALU.add).then_inc(o_ready, 1)


def block_attention_then_gated_convolution(nc, x, mask, gamma, beta, wq, wk, wv, wb, wg, wo,
                                           kA, kB, gB, w2, bout, taps, out):
    d = {
        "x": x, "mask": mask, "gamma": gamma.rearrange("(c o) -> c o", o=1), "beta": beta.rearrange("(c o) -> c o", o=1),
        "wq": wq, "wk": wk, "wv": wv, "wb": wb, "wg": wg, "wo": wo, "w2": w2, "kA": kA, "bout": bout,
        "kB": kB, "gB": gB, "taps": taps, "out": out,
        "flat": nc.dram_tensor("flat_kernels", (C, 2, FLAT), F16).ap(),
        "split": nc.dram_tensor("split_queries_keys", (3, DH, 2, 2, HEADS, 2 * N), F16).ap(),
        "peaks": nc.dram_tensor("peaks", (C, 4), F32).ap(),
        "h": nc.dram_tensor("hidden", (NCC * STRIPS, P, CCH, P), F32).ap(),
        "znt": nc.dram_tensor("zn_transposed", (C, N * N), F32).ap(),
        "x1": nc.dram_tensor("x1_rows", (N, N, C), F32).ap(),
        "square": nc.dram_tensor("corner_square", (2 * TAPS - 1, 2 * TAPS - 1, C), F32).ap(),
        "x1h": nc.dram_tensor("x1_halo", (NCC, HPAD, BW, WB, CCH), F32).ap(),
    }
    with ExitStack() as ctx:
        def sb(name, shape, dt=F32):
            return ctx.enter_context(nc.sbuf_tensor(name, shape, dt))

        b = {"w2": sb("w2", [C, C]), "bout": sb("bout", [P, C]), "ident": sb("ident", [P, P])}
        b["gn_a"], b["gn_b"], b["mean0"] = sb("gn_a", [P, C]), sb("gn_b", [P, C]), sb("mean0", [P, C])
        b["xscale"], b["kscale"] = sb("xscale", [P, C]), sb("kscale", [P, 2])
        b["corner"] = sb("corner", [TAPS * TAPS, C])
        middle = ctx.enter_context(ExitStack())
        with ExitStack() as inner:
            def sbi(name, shape, dt=F32, to=inner):
                return to.enter_context(nc.sbuf_tensor(name, shape, dt))

            b["mean_w"] = sbi("mean_w", [P, P], to=middle)
            b["acc"] = sbi("acc", [P, 2, WT * C], to=middle)
            for name in ("wq", "wk", "wv", "wg", "wo"):
                b[name] = sbi(name, [C, C])
            b["wb"] = sbi("wb", [C, HEADS])
            b["fs"], b["fs_inv"] = sbi("fs", [P, 1]), sbi("fs_inv", [P, 1])
            b["gamma"], b["beta"] = sbi("gamma", [C, 1]), sbi("beta", [C, 1])
            b["mask8"] = sbi("mask8", [P, N], U8)
            b["half"] = sbi("half", [P, N])
            b["pow"] = sbi("pow", [P, 8])
            b["nbias"] = sbi("nbias", [P, WT, HEADS, N])
            setup_stage(nc, d, b)
            stats_stage(nc, d, b)
            norm_stage(nc, d, b)
            attention_stage(nc, d, b)
        corner_stage(nc, d, b)
        middle.close()
        conv_stage(nc, d, b)
        output_stage(nc, d, b)


def kernel(**inputs):
    import numpy as _np
    import concourse.bacc as _bacc
    from concourse import mybir as _mybir
    from concourse.bass_utils import run_bass_kernel_spmd as _run

    def rotated(k):
        return k[:, ::-1, ::-1].reshape(C, TAPS * TAPS)

    first, second = "L0_conv_", "L1_conv_"
    gate_a, gate_b, b_kernel = (rotated(_np.asarray(inputs[second + n])) for n in ("gate_A_kernel", "gate_B_kernel", "B_kernel"))
    given = [
        ("x", inputs["x"]),
        ("mask", _np.asarray(inputs[first + "single_mask"]).reshape(-1)),
        ("gamma", inputs[first + "ln_gamma"]),
        ("beta", inputs[first + "ln_beta"]),
        ("wq", inputs[first + "Wq"]),
        ("wk", inputs[first + "Wk"]),
        ("wv", inputs[first + "Wv"]),
        ("wb", inputs[first + "Wb"]),
        ("wg", inputs[first + "Wg"]),
        ("wo", inputs[first + "Wout"]),
        ("kA", _np.asarray(inputs[second + "A_kernel"]).reshape(C, TAPS * TAPS).T),
        ("kB", b_kernel),
        ("gB", gate_b),
        ("w2", inputs[second + "W_out"]),
        ("bout", inputs[second + "b_out"]),
        ("taps", _np.stack([gate_a.T, gate_b.T, b_kernel.T])),
    ]
    nc = _bacc.Bacc("TRN2", target_bir_lowering=False, num_devices=1)
    arrays, args = {}, []
    for name, a in given:
        a = _np.ascontiguousarray(a)
        arrays[f"in_{name}_dram"] = a
        args.append(nc.dram_tensor(f"in_{name}_dram", a.shape, _mybir.dt.from_np(a.dtype), kind="ExternalInput").ap())
    args.append(nc.dram_tensor("out_dram", (1, N, N, C), F32, kind="ExternalOutput").ap())
    block_attention_then_gated_convolution(nc, *args)
    r = _run(nc, [arrays], core_ids=[0])
    return r.results[0]["out_dram"]
```
